# Optimizing a Trainium2 kernel written in Bass

```python
import numpy as np
import jax
import jax.numpy as jnp

def _softmax(x, axis=-1):
    return jax.nn.softmax(x, axis=axis)

def _gelu(x):
    return jax.nn.gelu(x, approximate=True)

def _silu(x):
    return jax.nn.silu(x)

def _sigmoid(x):
    return jax.nn.sigmoid(x)

def _layernorm(x, axis=-1, eps=1e-05):
    m = jnp.mean(x, axis=axis, keepdims=True)
    v = jnp.var(x, axis=axis, keepdims=True)
    return (x - m) / jnp.sqrt(v + eps)

def _scatter_add(tgt, idx, src, axis=0):
    return tgt.at[idx].add(src)

def _segment_sum(src, seg, n):
    return jax.ops.segment_sum(src, seg, n)
kernel_name = 'mk_flamingo_gated_d2_seqx_r8_0499d4'

def setup_inputs(seed: int=0):
    np.random.seed(seed)
    _w = jnp.asarray

    def _rec_inputs():
        import jax
        import jax.numpy as jnp
        _rk = jax.random.key(seed)
        x = -0.0002928 + 1 * jax.random.normal(jax.random.fold_in(_rk, 1), (16, 64, 128), jnp.float32)
        _lenS = 64 - jax.random.randint(jax.random.fold_in(_rk, 7), (16,), 0, max(1, 64 // 4) + 1, jnp.int32)
        _lenS2 = 64 - jax.random.randint(jax.random.fold_in(_rk, 8), (16,), 0, max(1, 64 // 4) + 1, jnp.int32)
        _ctx_1024P = jax.random.normal(jax.random.fold_in(_rk, 11), (16, 16, 128), jnp.float32)
        _ctx_1024c = jax.random.dirichlet(jax.random.fold_in(_rk, 511), 0.3 * jnp.ones((16,), jnp.float32), (16, 64))
        _ctx_1024t = jnp.einsum('bsk,bkd->bsd', _ctx_1024c, _ctx_1024P)
        _ctx_1024t = _ctx_1024t * jax.lax.rsqrt(jnp.mean(jnp.square(_ctx_1024t)) + 1e-12) * 0.953939
        ctx_1024 = -1.39393e-06 + 0.999914 * (_ctx_1024t + 0.3 * jax.random.normal(jax.random.fold_in(_rk, 611), (16, 64, 128), jnp.float32))
        _g = jax.random.normal(jax.random.fold_in(_rk, 9001), (2, 2), jnp.float32)
        _g = jnp.sign(_g) * jnp.maximum(jnp.abs(_g), 1.0) + (_g == 0) * 1.0
        g_xattn = _g[0]
        g_ffn = _g[1]
        return (x, ctx_1024, g_xattn, g_ffn)
    x, ctx_1024, g_xattn, g_ffn = _rec_inputs()

    def _L0_xattn_setup():
        import jax, jax.numpy as jnp
        import numpy as np
        B, S, D = (2, 256, 128)
        H, HD = (16, 64)
        key = jax.random.key(seed)
        ks = jax.random.split(key, 8)
        scale = 1.0 / np.sqrt(D)
        return {'q': jax.random.normal(ks[0], (B, S, D), jnp.float32), 'k': jax.random.normal(ks[1], (B, S, D), jnp.float32), 'v': jax.random.normal(ks[2], (B, S, D), jnp.float32), 'Wq': jax.random.normal(ks[3], (H * HD, D), jnp.float32) * scale, 'bq': jnp.zeros((H * HD,), jnp.float32), 'Wk': jax.random.normal(ks[4], (H * HD, D), jnp.float32) * scale, 'bk': jnp.zeros((H * HD,), jnp.float32), 'Wv': jax.random.normal(ks[5], (H * HD, D), jnp.float32) * scale, 'bv': jnp.zeros((H * HD,), jnp.float32), 'Wo': jax.random.normal(ks[6], (D, H * HD), jnp.float32) * scale, 'bo': jnp.zeros((D,), jnp.float32)}
    _L0_xattn_all = _L0_xattn_setup()
    _L0_xattn_in = {k: v for k, v in _L0_xattn_all.items() if k in ('Wq', 'bq', 'Wk', 'bk', 'Wv', 'bv', 'Wo', 'bo')}
    del _L0_xattn_all

    def _L0_ffn_setup():
        import jax, jax.numpy as jnp
        import numpy as np
        B, S, D, M, E, K = (2, 256, 128, 176, 8, 2)
        key = jax.random.key(seed)
        k0, k1, k2, k3, k4 = jax.random.split(key, 5)
        scale = 0.02
        return {'x': jax.random.normal(k0, (B, S, D), dtype=jnp.float32), 'w_gate': jax.random.normal(k1, (D, E), dtype=jnp.float32) * scale, 'w_g': jax.random.normal(k2, (E, D, M), dtype=jnp.float32) * scale, 'w_u': jax.random.normal(k3, (E, D, M), dtype=jnp.float32) * scale, 'w_d': jax.random.normal(k4, (E, M, D), dtype=jnp.float32) * scale}
    _L0_ffn_all = _L0_ffn_setup()
    _L0_ffn_in = {k: v for k, v in _L0_ffn_all.items() if k in ('w_gate', 'w_g', 'w_u', 'w_d')}
    del _L0_ffn_all

    def _L1_xattn_setup():
        import jax, jax.numpy as jnp
        import numpy as np
        B, SQ, SK, D = (4, 256, 256, 128)
        key = jax.random.key(seed)
        ks = jax.random.split(key, 8)
        s = 1.0 / np.sqrt(D)
        return {'input_seq': jax.random.normal(ks[0], (B, SQ, D), jnp.float32), 'condition_seq': jax.random.normal(ks[1], (B, SK, D), jnp.float32), 'Wq': jax.random.normal(ks[2], (D, D), jnp.float32) * s, 'bq': jnp.zeros((D,), jnp.float32), 'Wk': jax.random.normal(ks[3], (D, D), jnp.float32) * s, 'bk': jnp.zeros((D,), jnp.float32), 'Wv': jax.random.normal(ks[4], (D, D), jnp.float32) * s, 'bv': jnp.zeros((D,), jnp.float32)}
    _L1_xattn_all = _L1_xattn_setup()
    _L1_xattn_in = {k: v for k, v in _L1_xattn_all.items() if k in ('Wq', 'bq', 'Wk', 'bk', 'Wv', 'bv')}
    del _L1_xattn_all

    def _L1_ffn_setup():
        import jax, jax.numpy as jnp
        import numpy as np
        H, KVH, HD, D = (8, 2, 128, 128)
        E, TOPK, FFN = (8, 2, 448)
        THETA, EPS = (1000000.0, 1e-05)
        NBITS, GS = (4, 128)
        QMAX = float(2 ** NBITS - 1)
        NEG = -1e+30

        def qgroup(w):
            shp = w.shape
            w2 = w.reshape(-1, GS)
            wmax = jnp.max(w2, -1, keepdims=True)
            wmin = jnp.min(w2, -1, keepdims=True)
            scales = jnp.clip(wmax - wmin, 1e-05, None) / QMAX
            base = jnp.clip(jnp.round(-wmin / scales), 0.0, QMAX)
            wq = (jnp.clip(jnp.round(w2 / scales) + base, 0.0, QMAX) - base) * scales
            return wq.reshape(shp)

        def rms(x, g):
            return x * jax.lax.rsqrt(jnp.mean(x * x, -1, keepdims=True) + EPS) * g

        def rot_half(x):
            h = x.shape[-1] // 2
            return jnp.concatenate([-x[..., h:], x[..., :h]], axis=-1)
        key = jax.random.key(seed)
        ks = jax.random.split(key, 12)
        B, S = (2, 128)
        n = lambda k, s: 0.02 * jax.random.normal(k, s, dtype=jnp.float32)
        return {'hidden_states': jax.random.normal(ks[0], (B, S, D), dtype=jnp.float32), 'w_q': n(ks[1], (H * HD, D)), 'w_k': n(ks[2], (KVH * HD, D)), 'w_v': n(ks[3], (KVH * HD, D)), 'w_o': n(ks[4], (D, H * HD)), 'g1': jnp.ones((D,), jnp.float32), 'g2': jnp.ones((D,), jnp.float32), 'w_gate': n(ks[5], (E, D)), 'w1': n(ks[6], (E, FFN, D)), 'w3': n(ks[7], (E, FFN, D)), 'w2': n(ks[8], (E, D, FFN))}
    _L1_ffn_all = _L1_ffn_setup()
    _L1_ffn_in = {k: v for k, v in _L1_ffn_all.items() if k in ('w_q', 'w_k', 'w_v', 'w_o', 'g1', 'g2', 'w_gate', 'w1', 'w3', 'w2')}
    del _L1_ffn_all
    return {'x': x, 'ctx_1024': ctx_1024, 'g_xattn': g_xattn, 'g_ffn': g_ffn, 'L0_xattn_Wq': _L0_xattn_in['Wq'], 'L0_xattn_bq': _L0_xattn_in['bq'], 'L0_xattn_Wk': _L0_xattn_in['Wk'], 'L0_xattn_bk': _L0_xattn_in['bk'], 'L0_xattn_Wv': _L0_xattn_in['Wv'], 'L0_xattn_bv': _L0_xattn_in['bv'], 'L0_xattn_Wo': _L0_xattn_in['Wo'], 'L0_xattn_bo': _L0_xattn_in['bo'], 'L0_ffn_w_gate': _L0_ffn_in['w_gate'], 'L0_ffn_w_g': _L0_ffn_in['w_g'], 'L0_ffn_w_u': _L0_ffn_in['w_u'], 'L0_ffn_w_d': _L0_ffn_in['w_d'], 'L1_xattn_Wq': _L1_xattn_in['Wq'], 'L1_xattn_bq': _L1_xattn_in['bq'], 'L1_xattn_Wk': _L1_xattn_in['Wk'], 'L1_xattn_bk': _L1_xattn_in['bk'], 'L1_xattn_Wv': _L1_xattn_in['Wv'], 'L1_xattn_bv': _L1_xattn_in['bv'], 'L1_ffn_w_q': _L1_ffn_in['w_q'], 'L1_ffn_w_k': _L1_ffn_in['w_k'], 'L1_ffn_w_v': _L1_ffn_in['w_v'], 'L1_ffn_w_o': _L1_ffn_in['w_o'], 'L1_ffn_g1': _L1_ffn_in['g1'], 'L1_ffn_g2': _L1_ffn_in['g2'], 'L1_ffn_w_gate': _L1_ffn_in['w_gate'], 'L1_ffn_w1': _L1_ffn_in['w1'], 'L1_ffn_w3': _L1_ffn_in['w3'], 'L1_ffn_w2': _L1_ffn_in['w2']}

def reference(x, ctx_1024, g_xattn, g_ffn, L0_xattn_Wq, L0_xattn_bq, L0_xattn_Wk, L0_xattn_bk, L0_xattn_Wv, L0_xattn_bv, L0_xattn_Wo, L0_xattn_bo, L0_ffn_w_gate, L0_ffn_w_g, L0_ffn_w_u, L0_ffn_w_d, L1_xattn_Wq, L1_xattn_bq, L1_xattn_Wk, L1_xattn_bk, L1_xattn_Wv, L1_xattn_bv, L1_ffn_w_q, L1_ffn_w_k, L1_ffn_w_v, L1_ffn_w_o, L1_ffn_g1, L1_ffn_g2, L1_ffn_w_gate, L1_ffn_w1, L1_ffn_w3, L1_ffn_w2):
    import jax
    import jax.numpy as jnp

    def _L0_xattn_ref(q, k, v, Wq, bq, Wk, bk, Wv, bv, Wo, bo):
        import jax, jax.numpy as jnp
        import numpy as np
        B, S, D = (2, 256, 128)
        H, HD = (16, 64)
        b, s, _ = q.shape
        qh = (q @ Wq.T + bq).reshape(b, s, H, HD).transpose(0, 2, 1, 3)
        kh = (k @ Wk.T + bk).reshape(b, s, H, HD).transpose(0, 2, 1, 3)
        vh = (v @ Wv.T + bv).reshape(b, s, H, HD).transpose(0, 2, 1, 3)
        scores = jnp.einsum('bhqd,bhkd->bhqk', qh, kh) / np.sqrt(HD).astype(np.float32)
        causal = jnp.tril(jnp.ones((s, s), bool))
        scores = jnp.where(causal, scores, -jnp.inf)
        attn = jax.nn.softmax(scores, axis=-1)
        out = jnp.einsum('bhqk,bhkd->bhqd', attn, vh)
        out = out.transpose(0, 2, 1, 3).reshape(b, s, H * HD)
        return out @ Wo.T + bo

    def _L0_ffn_ref(x, w_gate, w_g, w_u, w_d):
        import jax, jax.numpy as jnp
        import numpy as np
        B, S, D, M, E, K = (2, 256, 128, 176, 8, 2)
        scores = x @ w_gate
        topk_scores, topk_idx = jax.lax.top_k(scores, K)
        topk_probs = jax.nn.softmax(topk_scores, axis=-1)
        gating = jnp.sum(jax.nn.one_hot(topk_idx, E, dtype=topk_probs.dtype) * topk_probs[..., None], axis=-2)
        hidden = jax.nn.silu(jnp.einsum('bsd,edm->ebsm', x, w_g)) * jnp.einsum('bsd,edm->ebsm', x, w_u)
        expert_out = jnp.einsum('ebsm,emd->ebsd', hidden, w_d)
        y = jnp.einsum('bse,ebsd->bsd', gating, expert_out)
        return y

    def _L1_xattn_ref(input_seq, condition_seq, Wq, bq, Wk, bk, Wv, bv):
        import jax, jax.numpy as jnp
        import numpy as np
        B, SQ, SK, D = (4, 256, 256, 128)
        q = jnp.einsum('bsd,ed->bse', input_seq, Wq) + bq
        k = jnp.einsum('btd,ed->bte', condition_seq, Wk) + bk
        v = jnp.einsum('btd,ed->bte', condition_seq, Wv) + bv
        scores = jnp.einsum('bse,bte->bst', q, k)
        attn = jax.nn.softmax(scores, axis=-1)
        attended = jnp.einsum('bst,bte->bse', attn, v)
        return attended

    def _L1_ffn_ref(hidden_states, w_q, w_k, w_v, w_o, g1, g2, w_gate, w1, w3, w2):
        import jax, jax.numpy as jnp
        import numpy as np
        H, KVH, HD, D = (8, 2, 128, 128)
        E, TOPK, FFN = (8, 2, 448)
        THETA, EPS = (1000000.0, 1e-05)
        NBITS, GS = (4, 128)
        QMAX = float(2 ** NBITS - 1)
        NEG = -1e+30

        def qgroup(w):
            shp = w.shape
            w2 = w.reshape(-1, GS)
            wmax = jnp.max(w2, -1, keepdims=True)
            wmin = jnp.min(w2, -1, keepdims=True)
            scales = jnp.clip(wmax - wmin, 1e-05, None) / QMAX
            base = jnp.clip(jnp.round(-wmin / scales), 0.0, QMAX)
            wq = (jnp.clip(jnp.round(w2 / scales) + base, 0.0, QMAX) - base) * scales
            return wq.reshape(shp)

        def rms(x, g):
            return x * jax.lax.rsqrt(jnp.mean(x * x, -1, keepdims=True) + EPS) * g

        def rot_half(x):
            h = x.shape[-1] // 2
            return jnp.concatenate([-x[..., h:], x[..., :h]], axis=-1)
        B, S, _ = hidden_states.shape
        T = B * S
        xn = rms(hidden_states, g1)
        q = (xn @ qgroup(w_q).T).reshape(B, S, H, HD).transpose(0, 2, 1, 3)
        k = (xn @ qgroup(w_k).T).reshape(B, S, KVH, HD).transpose(0, 2, 1, 3)
        v = (xn @ qgroup(w_v).T).reshape(B, S, KVH, HD).transpose(0, 2, 1, 3)
        k = qgroup(k)
        pos = jnp.arange(S, dtype=jnp.float32)
        inv = 1.0 / THETA ** (jnp.arange(0, HD, 2, dtype=jnp.float32) / HD)
        freqs = pos[:, None] * inv[None, :]
        emb = jnp.concatenate([freqs, freqs], axis=-1)
        cos = jnp.cos(emb)[None, None]
        sin = jnp.sin(emb)[None, None]
        q = q * cos + rot_half(q) * sin
        k = k * cos + rot_half(k) * sin
        rep = H // KVH
        k = jnp.repeat(k, rep, axis=1)
        v = jnp.repeat(v, rep, axis=1)
        v = qgroup(v)
        scores = jnp.einsum('bhqd,bhkd->bhqk', q, k) / np.float32(np.sqrt(HD))
        causal = jnp.tril(jnp.ones((S, S), dtype=bool))
        scores = jnp.where(causal[None, None], scores, NEG)
        attn = jax.nn.softmax(scores, axis=-1)
        o = jnp.einsum('bhqk,bhkd->bhqd', attn, v).transpose(0, 2, 1, 3).reshape(B, S, H * HD)
        h = hidden_states + o @ qgroup(w_o).T
        hn = rms(h, g2).reshape(T, D)
        logits = hn @ w_gate.T
        probs = jax.nn.softmax(logits, axis=-1)
        tv, ti = jax.lax.top_k(probs, TOPK)
        tv = tv / jnp.sum(tv, axis=-1, keepdims=True)
        rw = jnp.zeros((T, E), hn.dtype).at[jnp.arange(T)[:, None], ti].set(tv)
        moe = jnp.zeros((T, D), hn.dtype)
        for e in range(E):
            up = jax.nn.silu(hn @ qgroup(w1[e]).T) * (hn @ qgroup(w3[e]).T)
            moe = moe + rw[:, e:e + 1] * (up @ qgroup(w2[e]).T)
        return h + moe.reshape(B, S, D)
    x = x + jnp.tanh(g_xattn[0]) * _L0_xattn_ref(_layernorm(x, axis=-1), ctx_1024, ctx_1024, L0_xattn_Wq, L0_xattn_bq, L0_xattn_Wk, L0_xattn_bk, L0_xattn_Wv, L0_xattn_bv, L0_xattn_Wo, L0_xattn_bo)
    x = x + jnp.tanh(g_ffn[0]) * _L0_ffn_ref(_layernorm(x, axis=-1), L0_ffn_w_gate, L0_ffn_w_g, L0_ffn_w_u, L0_ffn_w_d)
    x = x + jnp.tanh(g_xattn[1]) * _L1_xattn_ref(_layernorm(x, axis=-1), ctx_1024, L1_xattn_Wq, L1_xattn_bq, L1_xattn_Wk, L1_xattn_bk, L1_xattn_Wv, L1_xattn_bv)
    x = x + jnp.tanh(g_ffn[1]) * _L1_ffn_ref(_layernorm(x, axis=-1), L1_ffn_w_q, L1_ffn_w_k, L1_ffn_w_v, L1_ffn_w_o, L1_ffn_g1, L1_ffn_g2, L1_ffn_w_gate, L1_ffn_w1, L1_ffn_w3, L1_ffn_w2)
    return x

_drawn_inputs = setup_inputs


def setup_inputs(seed=0):
    import zlib

    import numpy as np

    out = dict(_drawn_inputs(seed))
    spreads = {'g_ffn': (-1.0, 0.2),
     'L0_xattn_bq': (0.0, 0.1),
     'L0_xattn_bk': (0.0, 0.8),
     'L0_xattn_bv': (0.0, 0.1),
     'L0_xattn_bo': (0.0, 0.1),
     'L1_xattn_bq': (0.0, 0.1),
     'L1_xattn_bk': (0.0, 0.8),
     'L1_xattn_bv': (0.0, 0.1),
     'L1_ffn_g1': (1.0, 0.6),
     'L1_ffn_g2': (1.0, 0.6)}
    factors = {'L0_ffn_w_gate': 8.0,
     'L0_ffn_w_g': 8.0,
     'L0_ffn_w_u': 8.0,
     'L0_ffn_w_d': 8.0,
     'L1_ffn_w_q': 8.0,
     'L1_ffn_w_k': 8.0,
     'L1_ffn_w_gate': 8.0,
     'L1_ffn_w1': 8.0,
     'L1_ffn_w3': 8.0,
     'L1_ffn_w2': 8.0}
    for name, (base, spread) in spreads.items():
        noise = np.random.default_rng([zlib.crc32(name.encode()), seed]).standard_normal(out[name].shape)
        drawn = base * np.exp(spread * noise) if base else spread * noise
        out[name] = jnp.asarray(drawn.astype(out[name].dtype))
    for name, factor in factors.items():
        out[name] = (out[name] * factor).astype(out[name].dtype)
    return out
```

```python
from contextlib import ExitStack

import numpy as np

import concourse.bass as bass
from concourse import mybir

F32 = mybir.dt.float32
F32R = mybir.dt.float32r
BF16 = mybir.dt.bfloat16
ALU = mybir.AluOpType
ACT = mybir.ActivationFunctionType
AX = mybir.AxisListType.X

P = 128
B, S, D = 16, 64, 128
TOK = B * S
NT = TOK // P
HALF = TOK // 2
E = 8
HP0 = 8
HP1 = 4
M0 = 11
PAIRS = 4
MT = 7
QMAX = 15.0
MAGIC = 1.5 * 2.0 ** 23
LN_EPS = 1e-5

C_ID, C_CAU, C_BLK, C_COS, C_SIN, C_COSK, C_SINK, C_REV, C_END = (
    0, 128, 192, 320, 384, 448, 576, 704, 712)
V_BO, V_BQ, V_BK, V_BV, V_G1, V_G2, V_BV0, V_WG0, V_WG1, V_GX, V_GF, V_END = (
    0, 1, 2, 3, 4, 5, 6, 14, 22, 30, 32, 34)
WST = 3 * P + 2


def build(nc, cst_d, vec_d, x_d, ctx_d, w0_d, wo0_d, sel0_d, sel1_d, gu0_d, d0_d, wx_d, wl_d, wm_d, out_d):
    with ExitStack() as ctx:
        def sb(name, shape, dt=F32):
            return ctx.enter_context(nc.sbuf_tensor(name, shape, dt))

        def sem(name):
            return ctx.enter_context(nc.semaphore(name))

        ps = ctx.enter_context(nc.psum_tensor("ps", [P, 8, 512], F32))

        cst = sb("cst", [P, C_END])
        vec = sb("vec", [P, V_END])
        idb = sb("idb", [P, P], BF16)
        caub = sb("caub", [P, S], BF16)
        blkb = sb("blkb", [P, P], BF16)
        tg = sb("tg", [P, 4])
        wg_h = sb("wg_h", [P, 2 * E], F32R)
        wg_l = sb("wg_l", [P, 2 * E], F32R)
        half = sb("half", [P, NT])
        magic = sb("magic", [P, 1])
        sel0 = sb("sel0", [E, M0 * P])
        sel1 = sb("sel1", [E, E * P])
        selr0 = sb("selr0", [E, P], F32R)
        selr1 = sb("selr1", [E, E * P], F32R)
        x_tok = sb("x_tok", [P, NT, D])
        nrm = sb("nrm", [P, NT, D])
        hs = sb("hs", [P, NT, D])
        xh = sb("xh", [P, TOK], F32R)
        xl = sb("xl", [P, TOK], F32R)
        cT = sb("cT", [P, TOK])
        ch = sb("ch", [P, TOK], F32R)
        cl = sb("cl", [P, TOK], F32R)
        bst = sb("bst", [P, NT, 6])
        bmv = sb("bmv", [P, NT, 2])
        ve = sb("ve", [P, NT])
        rs = sb("rs", [P, NT])
        wst = sb("wst", [P, WST])
        w_h = sb("w_h", [P, 3 * P], F32R)
        w_l = sb("w_l", [P, 3 * P], F32R)
        qbd = sb("qbd", [P, B, 2, S])
        kT = sb("kT", [P, 2, TOK])
        v_sb = sb("v_sb", [P, NT, P])
        prob = sb("prob", [P, 2, 512])
        attT = sb("attT", [P, NT, P])
        mx = sb("mx", [P, B])
        den = sb("den", [P, B])
        rden = sb("rden", [P, B])
        big = sb("big", [P, 8, TOK])
        wo0 = sb("wo0", [P, HP0, D])
        yT = sb("yT", [P, TOK])
        yc = sb("yc", [P, 1])
        lg = sb("lg", [P, NT, E])
        gp = sb("gp", [P, NT, E])
        gk = sb("gk", [P, NT, E])
        f1 = sb("f1", [P, NT, E])
        f2 = sb("f2", [P, NT, E])
        gm = sb("gm", [P, NT])
        g_h = sb("g_h", [E, TOK], F32R)
        g_l = sb("g_l", [E, TOK], F32R)
        gu_st = sb("gu_st", [P, 2 * P])
        gu_h = sb("gu_h", [P, 2 * P], F32R)
        gu_l = sb("gu_l", [P, 2 * P], F32R)
        d_st = sb("d_st", [P, D])
        act = sb("act", [P, 2, 512])
        hid1 = sb("hid1", [P, 2, 512])
        hid = sb("hid", [P, 2, 512])
        wx_st = sb("wx_st", [P, 3 * P])
        wx_h = sb("wx_h", [P, 3 * P], F32R)
        wx_l = sb("wx_l", [P, 3 * P], F32R)
        st = sb("st", [P, 32, P])
        wqT = sb("wqT", [P, 8, P], F32R)
        wqR = sb("wqR", [P, 8, P], F32R)
        wkv_h = sb("wkv_h", [P, 4 * P], F32R)
        wkv_l = sb("wkv_l", [P, 4 * P], F32R)
        woT = wo0
        q1s = sb("q1s", [P, 2, 512])
        q2s = sb("q2s", [P, 2, 512])
        qmx = sb("qmx", [P, 32])
        qmn = sb("qmn", [P, 32])
        qsc = sb("qsc", [P, 32])
        qrs = sb("qrs", [P, 32])
        qb = sb("qb", [P, 32])
        qlo = sb("qlo", [P, 32])
        qhi = sb("qhi", [P, 32])
        wsc = sb("wsc", [P, 8])
        wscR = sb("wscR", [P, 8])
        w13T = sb("w13T", [P, 2 * MT, P], F32R)
        w2T = sb("w2T", [P, MT, D])
        msc = sb("msc", [P, 2 * MT])
        macc = sb("macc", [P, TOK])

        ident = cst[:, C_ID:C_ID + P]

        def bank(n):
            return ps[:, n, :]

        s = {n: sem(n) for n in (
            "cst_in", "vec_in", "x_in", "ctx_in", "wo0_in", "sel_in", "w0_in", "gu_in", "d_in", "wx_in", "wl_in",
            "wm_in", "scr_in", "stored",
            "pool_set", "tanh_done", "dve_set", "hi_set", "lo_set",
            "dve_step", "ve_ready", "rstd_ready", "nrm_ready", "turned", "xh_ready", "xl_ready",
            "yT_act", "yT_dve", "back", "x_new",
            "a_w_h", "a_w_l", "a_proj", "a_act", "a_dve", "a_scores", "a_max", "a_sub", "a_exp", "a_sum", "a_den",
            "a_norm", "a_attT", "a_attT_act", "a_attT_dve", "a_out", "a_out_act", "a_out_dve",
            "y_ready", "yc_ps", "yc_ready",
            "logits", "g_sub", "g_exp", "gates", "gT", "g_h_ready", "g_l_ready",
            "f_w_h", "f_w_l", "f_sel", "f_gu", "f_act", "f_h1", "f_gate", "f_hid", "f_down",
            "x_proj", "x_act", "x_dve", "q_stats", "q_round", "q_clip", "q_deq", "w_turn", "w_act", "w_dve",
            "w_rot", "kv_ps", "kv_act", "kv_dve", "k_rope", "k_turn", "k_act", "k_dve",
            "r_ps", "r_q1", "r_q2", "r_q", "r_wait",
            "m_stats", "m_round", "m_clip", "m_deq", "m_turn", "m_wact", "m_wdve", "gb_ps", "gb_act", "gb_dve",
            "m_gu", "m_act", "m_up", "m_down", "m_gy", "m_acc", "selr",
        )}

        def mm3(out, a_h, a_l, b_h, b_l, start=True, stop=True):
            nc.tensor.matmul(out, a_h, b_h, start=start, stop=False, skip_group_check=True)
            nc.tensor.matmul(out, a_h, b_l, start=False, stop=False, skip_group_check=True)
            return nc.tensor.matmul(out, a_l, b_h, start=False, stop=stop, skip_group_check=True)

        def mm2(out, a, b_h, b_l):
            nc.tensor.matmul(out, a, b_h, start=True, stop=False, skip_group_check=True)
            return nc.tensor.matmul(out, a, b_l, start=False, stop=True, skip_group_check=True)

        def per_group(t, n, w, sl=slice(None)):
            return t.unsqueeze(2).to_broadcast([P, n, w])

        def of_batches(t, b):
            return t.rearrange("p a (t b q) -> p a t b q", b=2, q=S)[:, :, :, b, :]

        block = ctx.enter_context(nc.Block())

        @block.sync
        def _(sp):
            sp.dma_start(x_tok[:], x_d).then_inc(s["x_in"], 16)
            sp.dma_start(cst[:], cst_d).then_inc(s["cst_in"], 16)
            sp.dma_start(cT[:], ctx_d).then_inc(s["ctx_in"], 16)
            sp.dma_start(vec[:], vec_d).then_inc(s["vec_in"], 16)
            sp.dma_start(wst[:], w0_d[0]).then_inc(s["w0_in"], 16)
            sp.wait_ge(s["a_w_l"], 1)
            sp.wait_ge(s["a_act"], 2)
            sp.wait_ge(s["a_dve"], 2)
            sp.dma_start(wst[:], w0_d[1]).then_inc(s["w0_in"], 16)
            sp.dma_start(wo0[:], wo0_d).then_inc(s["wo0_in"], 16)
            sp.dma_start(sel0[:], sel0_d).then_inc(s["sel_in"], 16)
            sp.dma_start(sel1[:], sel1_d).then_inc(s["sel_in"], 16)
            sp.dma_start(wx_st[:], wx_d).then_inc(s["wx_in"], 16)
            sp.dma_start(gu_st[:], gu0_d[0]).then_inc(s["gu_in"], 16)
            sp.dma_start(d_st[:], d0_d[0]).then_inc(s["d_in"], 16)
            sp.dma_start(st[:, 0:20, :], wl_d).then_inc(s["wl_in"], 16)
            with sp.Fori(0, HP0 - 1) as j:
                sp.wait_ge(s["a_w_l"], j + 2)
                sp.wait_ge(s["a_act"], 3 * j + 5)
                sp.wait_ge(s["a_dve"], 3 * j + 5)
                sp.dma_start(wst[:], w0_d[bass.ds(j + 2, 1)].rearrange("n p c -> (n p) c")).then_inc(s["w0_in"], 16)
            with sp.Fori(0, M0 - 1) as m:
                sp.wait_ge(s["f_w_l"], m + 1)
                sp.dma_start(gu_st[:], gu0_d[bass.ds(m + 1, 1)].rearrange("n p c -> (n p) c")).then_inc(s["gu_in"], 16)
                sp.wait_ge(s["f_down"], 2 * m + 2)
                sp.dma_start(d_st[:], d0_d[bass.ds(m + 1, 1)].rearrange("n p c -> (n p) c")).then_inc(s["d_in"], 16)
            sp.wait_ge(s["q_stats"], 1)
            sp.dma_start(wscR[0:64, :], wsc[64:128, :]).then_inc(s["scr_in"], 16)
            sp.dma_start(wscR[64:128, :], wsc[0:64, :]).then_inc(s["scr_in"], 16)
            for p in range(PAIRS):
                if p == 0:
                    sp.wait_ge(s["a_out"], O_L1 + 4 * HP1)
                else:
                    sp.wait_ge(s["m_turn"], 5 * p)
                sp.dma_start(st[:, 0:21, :], wm_d[p]).then_inc(s["wm_in"], 16)
            sp.wait_ge(s["x_new"], 5)
            sp.dma_start(out_d, x_tok[:]).then_inc(s["stored"], 16)
            sp.wait_ge(s["stored"], 16)

        @block.gpsimd
        def _(pool):
            nc.gpsimd.memset(qbd[:], 0.0)
            nc.gpsimd.memset(half[:], -0.5)
            nc.gpsimd.memset(magic[:], MAGIC).then_inc(s["pool_set"], 1)
            pool.wait_ge(s["pool_set"], 1)

            def rstd(k):
                pool.wait_ge(s["ve_ready"], k + 1)
                nc.gpsimd.tensor_tensor(rs[:], ve[:], half[:], ALU.pow).then_inc(s["rstd_ready"], 1)

            def normalise(n, c, nb, w):
                pool.wait_ge(s["a_den"], n + c + 1)
                pr = prob[:, c, :].rearrange("p (b k) -> p b k", k=w)
                nc.gpsimd.tensor_tensor(pr, pr, per_group(rden[:, nb * c:nb * (c + 1)], nb, w),
                                        ALU.mult).then_inc(s["a_norm"], 1)

            rstd(0)
            with pool.Fori(0, HP0) as j:
                for c in range(2):
                    normalise(2 * j, c, 8, S)
            rstd(1)
            rstd(2)
            for c in range(2):
                normalise(2 * HP0, c, 4, P)
            for n in range(12):
                g = 8 + n
                pool.wait_ge(s["q_clip"], g + 1)
                nc.gpsimd.tensor_scalar(st[:, g, :], st[:, g, :], -MAGIC, qsc[:, g:g + 1], ALU.add,
                                        ALU.mult).then_inc(s["q_deq"], 1)
            rstd(3)
            rstd(4)
            for g in range(32):
                pool.wait_ge(s["q_clip"], 20 + g + 1)
                nc.gpsimd.tensor_scalar(st[:, g, :], st[:, g, :], -MAGIC, qsc[:, g:g + 1], ALU.add,
                                        ALU.mult).then_inc(s["q_deq"], 1)

            def rotate_add(hp):
                for hh in range(2):
                    for c in range(2):
                        n = 4 * hp + 2 * hh + c
                        pool.wait_ge(s["r_q1"], n + 1)
                        pool.wait_ge(s["r_q2"], n + 1)
                        if hp > 0:
                            pool.wait_ge(s["a_scores"], 2 * HP0 + 2 + 2 * hp)
                        nc.gpsimd.tensor_tensor(qbd[:, 8 * c:8 * c + 8, hh, :],
                                                q1s[:, n % 2, :].rearrange("p (b q) -> p b q", q=S),
                                                q2s[:, n % 2, :].rearrange("p (b q) -> p b q", q=S),
                                                ALU.add).then_inc(s["r_q"], 1)

            rotate_add(0)
            for hp in range(HP1):
                for c in range(2):
                    normalise(2 * HP0 + 2 + 2 * hp, c, 8, S)
                if hp + 1 < HP1:
                    rotate_add(hp + 1)
            rstd(5)
            nc.gpsimd.memset(macc[:], 0.0).then_inc(s["m_acc"], 1)

            def dequant2(p):
                for n in range(MT):
                    g = 2 * MT + n
                    pool.wait_ge(s["m_clip"], 21 * p + g + 1)
                    nc.gpsimd.tensor_scalar(st[:, g, :], st[:, g, :], -MAGIC, qsc[:, g:g + 1], ALU.add,
                                            ALU.mult).then_inc(s["m_deq"], 1)

            dequant2(0)
            for p in range(PAIRS):
                for e in range(2):
                    for c in range(2):
                        n = 4 * p + 2 * e + c
                        pool.wait_ge(s["m_gy"], n + 1)
                        pool.wait_ge(s["m_acc"], n + 1)
                        nc.gpsimd.tensor_tensor(macc[:, 512 * c:512 * c + 512], macc[:, 512 * c:512 * c + 512],
                                                hid1[:, c, :], ALU.add).then_inc(s["m_acc"], 1)
                if p + 1 < PAIRS:
                    dequant2(p + 1)

        @block.scalar
        def _(sc):
            sc.wait_ge(s["ctx_in"], 16)
            nc.scalar.activation(ch[:], cT[:], ACT.Copy).then_inc(s["hi_set"], 1)
            sc.wait_ge(s["vec_in"], 16)
            nc.scalar.activation(wg_h[:], vec[:, V_WG0:V_WG0 + 2 * E], ACT.Copy).then_inc(s["hi_set"], 1)
            nc.scalar.activation(tg[:], vec[:, V_GX:V_GX + 4], ACT.Tanh).then_inc(s["tanh_done"], 1)
            sc.wait_ge(s["w0_in"], 16)
            nc.scalar.activation(w_h[:], wst[:, 0:3 * P], ACT.Copy).then_inc(s["a_w_h"], 1)

            def turn_hi(k, scale=1.0):
                for c in range(2):
                    sc.wait_ge(s["turned"], 2 * k + c + 1)
                    nc.scalar.activation(xh[:, 512 * c:512 * c + 512], bank(4 + c), ACT.Copy,
                                         scale=scale).then_inc(s["xh_ready"], 1)

            def exps(n, scale):
                for c in range(2):
                    sc.wait_ge(s["a_sub"], n + c + 1)
                    nc.scalar.activation(prob[:, c, :], prob[:, c, :], ACT.Exp, scale=scale).then_inc(s["a_exp"], 1)

            def attT_copy(n):
                sc.wait_ge(s["a_attT"], 2 * n + 1)
                nc.scalar.activation(attT[:, 0:4, :], bank(4).rearrange("p (t q) -> p t q", q=P),
                                     ACT.Copy).then_inc(s["a_attT_act"], 1)

            def queries_in(n):
                sc.wait_ge(s["a_proj"], n)
                for h in range(2):
                    r = slice(64 * h, 64 * h + 64)
                    ins = nc.scalar.activation(qbd[r, 0:8, h, :], ps[r, 2, :].rearrange("p (b q) -> p b q", q=S),
                                               ACT.Identity, bias=wst[r, 3 * P:3 * P + 1])
                ins.then_inc(s["a_act"], 1)

            def keys_in(n):
                sc.wait_ge(s["a_proj"], n)
                nc.scalar.activation(kT[:, 0, 0:512], bank(2), ACT.Identity,
                                     bias=wst[:, 3 * P + 1:3 * P + 2]).then_inc(s["a_act"], 1)

            turn_hi(0)
            sc.wait_ge(s["pool_set"], 1)
            queries_in(1)
            keys_in(3)

            def pair_step(j, first, last):
                if not first:
                    attT_copy(j - 1)
                exps(2 * j, 0.125)
                if not first:
                    sc.wait_ge(s["a_out"], 2 * j - 1)
                    nc.scalar.activation(of_batches(big[:, bass.ds(j - 1, 1), :], 0), ps[:, 6:7, :].rearrange(
                        "p a (t q) -> p a t q", q=S), ACT.Copy).then_inc(s["a_out_act"], 1)
                sc.wait_ge(s["w0_in"], 16 * j + 32)
                sc.wait_ge(s["a_proj"], 6 * j + 4)
                nc.scalar.activation(w_h[:], wst[:, 0:3 * P], ACT.Copy).then_inc(s["a_w_h"], 1)
                sc.wait_ge(s["a_proj"], 6 * j + 5)
                nc.scalar.activation(v_sb[:, 0:4, :], bank(2).rearrange("p (t d) -> p t d", d=P),
                                     ACT.Copy).then_inc(s["a_act"], 1)
                if not last:
                    queries_in(6 * j + 7)
                    keys_in(6 * j + 9)

            pair_step(0, True, False)
            with sc.Fori(1, HP0 - 1) as j:
                pair_step(j, False, False)
            pair_step(HP0 - 1, False, True)
            attT_copy(HP0 - 1)
            sc.wait_ge(s["a_out"], 2 * HP0 - 1)
            nc.scalar.activation(of_batches(big[:, HP0 - 1:HP0, :], 0), ps[:, 6:7, :].rearrange(
                "p a (t q) -> p a t q", q=S), ACT.Copy).then_inc(s["a_out_act"], 1)

            def y_first(k, n_ready, src, bias=None):
                sc.wait_ge(s["y_ready"], n_ready)
                if bias is None:
                    nc.scalar.activation(yT[:, 0:512], src, ACT.Copy).then_inc(s["yT_act"], 1)
                else:
                    nc.scalar.activation(yT[:, 0:512], src, ACT.Identity, bias=bias).then_inc(s["yT_act"], 1)

            sc.wait_ge(s["yc_ready"], 1)
            y_first(0, 1, bank(0), yc[:])

            sc.wait_ge(s["gu_in"], 16)
            nc.scalar.activation(gu_h[:], gu_st[:], ACT.Copy).then_inc(s["f_w_h"], 1)
            turn_hi(1)
            sc.wait_ge(s["g_sub"], 1)
            nc.scalar.activation(gp[:], gp[:], ACT.Exp).then_inc(s["g_exp"], 1)

            def gate_rows(k):
                for c in range(2):
                    sc.wait_ge(s["gT"], 2 * k + c + 1)
                    nc.scalar.activation(g_h[:, 512 * c:512 * c + 512], ps[0:E, 4 + c, :],
                                         ACT.Copy).then_inc(s["g_h_ready"], 1)

            def expert_step(m, first, last):
                for c in range(2):
                    sc.wait_ge(s["f_gu"], 2 * m + c + 1)
                    if not first:
                        sc.wait_ge(s["f_h1"], 2 * m + c - 1)
                    nc.scalar.activation(act[:, c, :], bank(c), ACT.Silu).then_inc(s["f_act"], 1)
                    if c == 0 and not last:
                        sc.wait_ge(s["gu_in"], 16 * m + 32)
                        sc.wait_ge(s["f_gu"], 2 * m + 2)
                        nc.scalar.activation(gu_h[:], gu_st[:], ACT.Copy).then_inc(s["f_w_h"], 1)

            gate_rows(0)
            expert_step(0, True, False)
            with sc.Fori(1, M0 - 1) as m:
                expert_step(m, False, False)
            expert_step(M0 - 1, False, True)
            sc.wait_ge(s["f_down"], 2 * M0 - 1)
            nc.scalar.activation(yT[:, 0:512], bank(6), ACT.Copy).then_inc(s["yT_act"], 1)

            sc.wait_ge(s["wx_in"], 16)
            nc.scalar.activation(wx_h[:], wx_st[:], ACT.Copy).then_inc(s["hi_set"], 1)
            turn_hi(2)
            sc.wait_ge(s["x_proj"], 1)
            nc.scalar.activation(kT[:, 1, 0:512], bank(0), ACT.Identity,
                                 bias=vec[:, V_BQ:V_BQ + 1]).then_inc(s["x_act"], 1)
            sc.wait_ge(s["x_proj"], 3)
            nc.scalar.activation(kT[:, 0, 0:512], bank(2), ACT.Identity,
                                 bias=vec[:, V_BK:V_BK + 1]).then_inc(s["x_act"], 1)
            sc.wait_ge(s["x_proj"], 5)
            nc.scalar.activation(v_sb[:, 0:4, :], bank(6).rearrange("p (t d) -> p t d", d=P),
                                 ACT.Copy).then_inc(s["x_act"], 1)
            exps(2 * HP0, 1.0)
            attT_copy(HP0)
            sc.wait_ge(s["a_out"], 2 * HP0 + 1)
            nc.scalar.activation(yT[:, 0:512], bank(6), ACT.Identity,
                                 bias=vec[:, V_BV:V_BV + 1]).then_inc(s["yT_act"], 1)

            def rounds(n, g0, g1, sem_in, sem_out):
                for g in range(g0, g1):
                    nc.scalar.activation(st[:, g, :], st[:, g, :], ACT.Identity, scale=qrs[:, g:g + 1],
                                         bias=magic[:]).then_inc(sem_out, 1)

            sc.wait_ge(s["q_stats"], 1)
            rounds(0, 0, 20, None, s["q_round"])
            for n in range(2):
                sc.wait_ge(s["w_turn"], n + 1)
                nc.scalar.activation(wqT[:, 4 * n:4 * n + 4, :], bank(n).rearrange("p (t d) -> p t d", d=P),
                                     ACT.Copy, bias=-MAGIC).then_inc(s["w_act"], 1)
            sc.wait_ge(s["w_turn"], 3)
            nc.scalar.activation(wkv_h[:], bank(2), ACT.Copy).then_inc(s["w_act"], 1)
            sc.wait_ge(s["w_turn"], 4)
            nc.scalar.activation(woT[:, 0:4, :], bank(6).rearrange("p (t d) -> p t d", d=P),
                                 ACT.Copy).then_inc(s["w_act"], 1)
            turn_hi(3, vec[:, V_G1:V_G1 + 1])
            for t in range(0, NT, 2):
                sc.wait_ge(s["kv_ps"], t + 1)
                nc.scalar.activation(st[:, 4 * t:4 * t + 4, :], bank(0).rearrange("p (g d) -> p g d", d=P),
                                     ACT.Copy).then_inc(s["kv_act"], 1)
            sc.wait_ge(s["q_stats"], 2)
            rounds(20, 0, 32, None, s["q_round"])
            for n in (0, 2):
                sc.wait_ge(s["k_turn"], n + 1)
                nc.scalar.activation(kT[:, n // 2, 0:512], bank(4), ACT.Copy).then_inc(s["k_act"], 1)

            def out_quarters(n, h):
                for q in range(2):
                    sc.wait_ge(s["a_out"], O_L1 + 4 * h + 2 * q + 1)
                    nc.scalar.activation(
                        of_batches(big[:, 2 * h:2 * h + 2, 512 * q:512 * q + 512], 0).rearrange("p a t q -> p t a q"),
                        bank(6).rearrange("p (t a q) -> p t a q", a=2, q=S), ACT.Copy).then_inc(s["a_out_act"], 1)

            for hp in range(HP1):
                if hp > 0:
                    attT_copy(HP0 + hp)
                exps(2 * HP0 + 2 + 2 * hp, float(P) ** -0.5)
                if hp > 0:
                    out_quarters(0, hp - 1)
            attT_copy(HP0 + HP1)
            out_quarters(0, HP1 - 1)
            y_first(3, 3, bank(0))

            turn_hi(4, vec[:, V_G2:V_G2 + 1])

            def m_prep(p):
                sc.wait_ge(s["m_stats"], p + 1)
                for g in range(21):
                    nc.scalar.activation(st[:, g, :], st[:, g, :], ACT.Identity, scale=qrs[:, g:g + 1],
                                         bias=magic[:]).then_inc(s["m_round"], 1)

            def m_weights(p):
                for n in range(2):
                    k = 4 if n == 0 else 3
                    sc.wait_ge(s["m_turn"], 5 * p + 2 * n + 1)
                    nc.scalar.activation(w13T[:, 4 * n:4 * n + k, :],
                                         ps[:, 4, 0:k * P].rearrange("p (t d) -> p t d", d=P),
                                         ACT.Copy, bias=-MAGIC).then_inc(s["m_wact"], 1)

            m_prep(0)
            m_weights(0)
            sc.wait_ge(s["g_sub"], 2)
            nc.scalar.activation(gp[:], gp[:], ACT.Exp).then_inc(s["g_exp"], 1)
            gate_rows(1)
            for n in range(0, 16, 2):
                sc.wait_ge(s["gb_ps"], n + 1)
                nc.scalar.activation(big[:, n // 2, 0:512], bank(4), ACT.Copy).then_inc(s["gb_act"], 1)
            for p in range(PAIRS):
                for m in range(MT):
                    for c in range(2):
                        n = 2 * (MT * p + m) + c
                        sc.wait_ge(s["m_gu"], n + 1)
                        if n >= 2:
                            sc.wait_ge(s["m_up"], n - 1)
                        nc.scalar.activation(act[:, c, :], bank(c), ACT.Silu,
                                             scale=msc[:, m:m + 1]).then_inc(s["m_act"], 1)
                if p + 1 < PAIRS:
                    m_prep(p + 1)
                    m_weights(p + 1)
            sc.wait_ge(s["m_acc"], 1 + 4 * PAIRS)

        @block.tensor
        def _(pe):
            T = nc.tensor

            def turn_norm(k):
                pe.wait_ge(s["nrm_ready"], k + 1)
                for c in range(2):
                    for t in range(4):
                        ins = T.transpose(ps[:, 4 + c, P * t:P * t + P], nrm[:, 4 * c + t, :], ident)
                    ins.then_inc(s["turned"], 1)

            def turn_back(k, src=None):
                src = yT if src is None else src
                for c in range(2):
                    if k < 4:
                        pe.wait_ge(s["yT_act" if c == 0 else "yT_dve"], k + 1)
                    for t in range(4):
                        o = 512 * c + P * t
                        ins = T.transpose(ps[:, 2 + c, P * t:P * t + P], src[:, o:o + P], ident)
                    ins.then_inc(s["back"], 1)

            def ring(n):
                if isinstance(n, int) and n < 2:
                    return
                raise AssertionError

            def project(i, out_bank, w0, src_h, src_l, c):
                return mm3(bank(out_bank), w_h[:, w0:w0 + P], w_l[:, w0:w0 + P],
                           src_h[:, 512 * c:512 * c + 512], src_l[:, 512 * c:512 * c + 512])

            def q_and_k(j, first):
                for n, (w0, a_h, a_l) in enumerate(((0, xh, xl), (P, ch, cl))):
                    for c in range(2):
                        if not (first and n == 0):
                            pe.wait_ge(s["a_act" if c == 0 else "a_dve"], 1 if first else 3 * j + n)
                        project(0, 2 + c, w0, a_h, a_l, c).then_inc(s["a_proj"], 1)

            pe.wait_ge(s["cst_in"], 16)
            turn_norm(0)
            pe.wait_ge(s["lo_set"], 2)
            pe.wait_ge(s["a_w_l"], 1)
            pe.wait_ge(s["xl_ready"], 2)
            q_and_k(0, True)

            def scores(n, lhs, rhs, mask, nb, w):
                for c in range(2):
                    pe.wait_ge(s["a_sub"], n + c - 1) if not (isinstance(n, int) and n == 0) else None
                    T.matmul(bank(c), idb[:], mask.unsqueeze(1).to_broadcast([P, nb, w]), start=True, stop=False,
                             skip_group_check=True)
                    for b in range(nb):
                        ins = T.matmul(ps[:, c, w * b:w * b + w], lhs(nb * c + b), rhs(nb * c + b), start=False,
                                       stop=True, skip_group_check=True)
                    ins.then_inc(s["a_scores"], 1)

            def turn_probs(n, gaps=True):
                for c in range(2):
                    pe.wait_ge(s["a_norm"], 2 * n + c + 1)
                    for t in range(4):
                        ins = T.transpose(ps[:, 4 + c, P * t:P * t + P], prob[:, c, P * t:P * t + P], ident)
                    ins.then_inc(s["a_attT"], 1)

            def values0(j, first):
                for c in range(2):
                    pe.wait_ge(s["a_attT_act" if c == 0 else "a_attT_dve"], j + 1)
                    pe.wait_ge(s["a_act" if c == 0 else "a_dve"], 3 * j + 3)
                    if c == 0 and not first:
                        pe.wait_ge(s["a_out_act"], j)
                        pe.wait_ge(s["a_out_dve"], j)
                    for t in range(4 * c, 4 * c + 4):
                        for b in range(2):
                            r = slice(64 * b, 64 * b + 64)
                            o = slice(S * t, S * t + S)
                            if t == 4 * c and b == 0:
                                T.matmul(ps[:, 6, o], v_sb[r, t, :], attT[r, t, 0:64], start=True, stop=True,
                                         skip_group_check=True)
                            else:
                                T.matmul(ps[0:64, 6 + b, o], v_sb[r, t, 0:64], attT[r, t, 0:64], start=True,
                                         stop=True, skip_group_check=True)
                            ins = T.matmul(ps[64:128, 6 + b, o], v_sb[r, t, 64:128], attT[r, t, 64:128],
                                           start=True, stop=True, skip_group_check=True)
                            if t == NT - 1:
                                ins.then_inc(s["a_out"], 1)

            def pair_step(j, first, last):
                if not first:
                    turn_probs(j - 1)
                pe.wait_ge(s["a_act"], 3 * j + 2)
                pe.wait_ge(s["a_dve"], 3 * j + 2)
                scores(2 * j if not first else 0, lambda b: qbd[:, b, :, :], lambda b: kT[:, 0, S * b:S * b + S],
                       caub[:], 8, S)
                if not first:
                    values0(j - 1, first=False) if not PEEL_SECOND else None
                pe.wait_ge(s["a_w_l"], j + 2)
                for c in range(2):
                    pe.wait_ge(s["a_act" if c == 0 else "a_dve"], 3 * j + 2)
                    for t in range(4):
                        o = 512 * c + P * t
                        ins = mm3(ps[:, 2 + c, P * t:P * t + P], ch[:, o:o + P], cl[:, o:o + P],
                                  w_h[:, 2 * P:3 * P], w_l[:, 2 * P:3 * P])
                    ins.then_inc(s["a_proj"], 1)
                if not last:
                    q_and_k_next(j)

            def q_and_k_next(j):
                for n, (w0, a_h, a_l) in enumerate(((0, xh, xl), (P, ch, cl))):
                    for c in range(2):
                        pe.wait_ge(s["a_act" if c == 0 else "a_dve"], 3 * j + 3 + n)
                        project(0, 2 + c, w0, a_h, a_l, c).then_inc(s["a_proj"], 1)

            PEEL_SECOND = False
            pe.wait_ge(s["dve_set"], 1)
            pair_step(0, True, False)
            with pe.Fori(1, HP0 - 1) as j:
                pair_step(j, False, False)
            pair_step(HP0 - 1, False, True)
            turn_probs(HP0 - 1)
            values0(HP0 - 1, False)

            pe.wait_ge(s["wo0_in"], 16)
            for j in range(HP0):
                ins = T.matmul(ps[:, 2, 0:1], wo0[:, j, :], vec[:, V_BV0 + j:V_BV0 + j + 1], start=(j == 0),
                               stop=(j == HP0 - 1))
            ins.then_inc(s["yc_ps"], 1)
            pe.wait_ge(s["a_out_act"], HP0)
            pe.wait_ge(s["a_out_dve"], HP0)
            for c in range(2):
                for j in range(HP0):
                    ins = T.matmul(bank(c), wo0[:, j, :], big[:, j, 512 * c:512 * c + 512], start=(j == 0),
                                   stop=(j == HP0 - 1))
                ins.then_inc(s["y_ready"], 1)
            turn_back(0)

            def gate_logits(k):
                pe.wait_ge(s["xl_ready"], 2 * (4 if k else 1) + 2)
                for t in range(NT):
                    ins = mm3(ps[:, 6, E * t:E * t + E], xh[:, P * t:P * t + P], xl[:, P * t:P * t + P],
                              wg_h[:, E * k:E * k + E], wg_l[:, E * k:E * k + E])
                ins.then_inc(s["logits"], 1)

            def gates_turned(k):
                pe.wait_ge(s["gates"], k + 1)
                for c in range(2):
                    for t in range(4):
                        ins = T.transpose(ps[0:E, 4 + c, P * t:P * t + P], lg[:, 4 * c + t, :], ident)
                    ins.then_inc(s["gT"], 1)

            def gate_up(m, first):
                pe.wait_ge(s["f_w_l"], m + 1)
                for c in range(2):
                    if not first:
                        pe.wait_ge(s["f_act"], 2 * m + c - 1)
                        pe.wait_ge(s["f_h1"], 2 * m + c - 1)
                    x0, x1 = xh[:, 512 * c:512 * c + 512], xl[:, 512 * c:512 * c + 512]
                    mm3(bank(c), gu_h[:, 0:P], gu_l[:, 0:P], x0, x1)
                    mm3(bank(2 + c), gu_h[:, P:2 * P], gu_l[:, P:2 * P], x0, x1).then_inc(s["f_gu"], 1)

            def expert_step(m, first, last):
                pe.wait_ge(s["f_sel"], m + 1)
                for c in range(2):
                    if not first:
                        pe.wait_ge(s["f_hid"], 2 * m + c - 1)
                    mm2(bank(4 + c), selr0[:], g_h[:, 512 * c:512 * c + 512],
                        g_l[:, 512 * c:512 * c + 512]).then_inc(s["f_gate"], 1)
                if not last:
                    gate_up(m + 1, False)
                pe.wait_ge(s["d_in"], 16 * m + 16)
                for c in range(2):
                    pe.wait_ge(s["f_hid"], 2 * m + c + 1)
                    T.matmul(bank(6 + c), d_st[:], hid[:, c, :], start=first, stop=last,
                             skip_group_check=True).then_inc(s["f_down"], 1)

            turn_norm(1)
            gate_logits(0)
            gate_up(0, True)
            gates_turned(0)
            pe.wait_ge(s["g_h_ready"], 2)
            pe.wait_ge(s["g_l_ready"], 2)
            expert_step(0, True, False)
            with pe.Fori(1, M0 - 1) as m:
                expert_step(m, False, False)
            expert_step(M0 - 1, False, True)
            turn_back(1)

            turn_norm(2)
            pe.wait_ge(s["xl_ready"], 6)
            pe.wait_ge(s["lo_set"], 3)
            for n, (w0, a_h, a_l) in enumerate(((0, xh, xl), (P, ch, cl))):
                for c in range(2):
                    mm3(bank(2 * n + c), wx_h[:, w0:w0 + P], wx_l[:, w0:w0 + P], a_h[:, 512 * c:512 * c + 512],
                        a_l[:, 512 * c:512 * c + 512]).then_inc(s["x_proj"], 1)
            for c in range(2):
                for t in range(4):
                    o = 512 * c + P * t
                    ins = mm3(ps[:, 6 + c, P * t:P * t + P], ch[:, o:o + P], cl[:, o:o + P], wx_h[:, 2 * P:3 * P],
                              wx_l[:, 2 * P:3 * P])
                ins.then_inc(s["x_proj"], 1)
            pe.wait_ge(s["x_act"], 2)
            pe.wait_ge(s["x_dve"], 2)
            scores(2 * HP0, lambda b: kT[:, 1, P * b:P * b + P], lambda b: kT[:, 0, P * b:P * b + P], blkb[:], 4, P)
            turn_probs(HP0)
            for c in range(2):
                pe.wait_ge(s["a_attT_act" if c == 0 else "a_attT_dve"], HP0 + 1)
                pe.wait_ge(s["x_act" if c == 0 else "x_dve"], 3)
                for t in range(4):
                    ins = T.matmul(ps[:, 6 + c, P * t:P * t + P], v_sb[:, 4 * c + t, :], attT[:, 4 * c + t, :],
                                   start=True, stop=True, skip_group_check=True)
                ins.then_inc(s["a_out"], 1)
            turn_back(2)

            for n in range(2):
                for t in range(4):
                    pe.wait_ge(s["q_clip"], 4 * n + t + 1)
                    ins = T.transpose(ps[:, n, P * t:P * t + P], st[:, 4 * n + t, :], ident)
                ins.then_inc(s["w_turn"], 1)
            pe.wait_ge(s["x_new"], 3)
            for n, b in ((2, 2), (3, 6), (4, 7)):
                for t in range(4):
                    pe.wait_ge(s["q_deq"], 4 * (n - 2) + t + 1)
                    ins = T.transpose(ps[:, b, P * t:P * t + P], st[:, 4 * n + t, :], ident)
                ins.then_inc(s["w_turn"], 1)
            turn_norm(3)
            pe.wait_ge(s["xl_ready"], 8)
            pe.wait_ge(s["w_act"], 4)
            pe.wait_ge(s["w_dve"], 2)
            for t in range(NT):
                if t >= 2:
                    pe.wait_ge(s["kv_act" if t % 2 == 0 else "kv_dve"], t // 2)
                mm3(bank(t % 2), xh[:, P * t:P * t + P], xl[:, P * t:P * t + P], wkv_h[:],
                    wkv_l[:]).then_inc(s["kv_ps"], 1)

            def rotate(hp):
                for hh in range(2):
                    for c in range(2):
                        n = 4 * hp + 2 * hh + c
                        x0, x1 = xh[:, 512 * c:512 * c + 512], xl[:, 512 * c:512 * c + 512]
                        if n >= 1:
                            pe.wait_ge(s["r_q1"], n)
                        mm2(bank(2), wqT[:, 2 * hp + hh, :], x0, x1).then_inc(s["r_ps"], 1)
                        if n >= 1:
                            pe.wait_ge(s["r_q2"], n)
                        mm2(bank(3), wqR[:, 2 * hp + hh, :], x0, x1).then_inc(s["r_ps"], 1)

            pe.wait_ge(s["w_rot"], 1)
            rotate(0)
            for n in range(4):
                if n >= 2:
                    pe.wait_ge(s["k_act" if n % 2 == 0 else "k_dve"], 1)
                pe.wait_ge(s["k_rope"], 1)
                for t in range(4):
                    tt = 4 * (n % 2) + t
                    ins = T.transpose(ps[:, 4 + n % 2, P * t:P * t + P], st[:, 4 * tt + n // 2, :], ident)
                ins.then_inc(s["k_turn"], 1)
            pe.wait_ge(s["k_act"], 2)
            pe.wait_ge(s["k_dve"], 2)

            def values1(hp):
                pe.wait_ge(s["a_attT_act"], HP0 + 2 + hp)
                pe.wait_ge(s["a_attT_dve"], HP0 + 2 + hp)
                for q in range(2):
                    n = 2 * hp + q
                    if n >= 1:
                        pe.wait_ge(s["a_out_act"], HP0 + n)
                        pe.wait_ge(s["a_out_dve"], HP0 + n)
                    for t in range(4):
                        for b in range(2):
                            r = slice(64 * b, 64 * b + 64)
                            ins = T.matmul(ps[:, 6 + b, P * t:P * t + P], st[r, 4 * (4 * q + t) + 2 + hp // 2, :],
                                           attT[r, 4 * q + t, :], start=True, stop=True, skip_group_check=True)
                            if t == 3:
                                ins.then_inc(s["a_out"], 1)

            for hp in range(HP1):
                if hp > 0:
                    turn_probs(HP0 + hp)
                pe.wait_ge(s["r_q"], 4 * hp + 4)
                scores(2 * HP0 + 2 + 2 * hp, lambda b: qbd[:, b, :, :],
                       lambda b, hp=hp: kT[:, hp // 2, S * b:S * b + S], caub[:], 8, S)
                if hp > 0:
                    values1(hp - 1)
                if hp + 1 < HP1:
                    rotate(hp + 1)
            turn_probs(HP0 + HP1)
            values1(HP1 - 1)
            pe.wait_ge(s["a_out_act"], HP0 + 2 * HP1)
            pe.wait_ge(s["a_out_dve"], HP0 + 2 * HP1)
            for c in range(2):
                for h in range(2 * HP1):
                    ins = T.matmul(bank(c), woT[:, h, :], big[:, h, 512 * c:512 * c + 512], start=(h == 0),
                                   stop=(h == 2 * HP1 - 1))
                ins.then_inc(s["y_ready"], 1)
            turn_back(3)

            def m_weights(p):
                for n in range(2):
                    k = 4 if n == 0 else 3
                    for w in range(2):
                        if n == 1:
                            pe.wait_ge(s["m_wact" if w == 0 else "m_wdve"], (2 if w == 0 else 3) * p + 1)
                        for t in range(k):
                            g = MT * w + 4 * n + t
                            pe.wait_ge(s["m_clip"], 21 * p + g + 1)
                            ins = T.transpose(ps[:, 4 + w, P * t:P * t + P], st[:, g, :], ident)
                        ins.then_inc(s["m_turn"], 1)
                pe.wait_ge(s["m_deq"], MT * (p + 1))
                pe.wait_ge(s["m_wdve"], 3 * p + 2)
                pe.wait_ge(s["m_wact"], 2 * p + 2)
                w2 = st[:, 2 * MT:3 * MT, :].rearrange("p g d -> p (g d)")
                for m in range(MT):
                    bk, o = (4, P * m) if m < 4 else (5, P * (m - 4))
                    for r in range(2):
                        oo = o + 64 * r
                        if m == 3:
                            T.matmul(ps[0:64, bk, oo:oo + 64], w2[0:64, 448 * r + 384:448 * r + 448],
                                     ident[0:64, 0:64], start=True, stop=True, skip_group_check=True)
                            ins = T.matmul(ps[64:128, bk, oo:oo + 64], w2[64:128, 448 * r:448 * r + 64],
                                           ident[64:128, 64:128], start=True, stop=True, skip_group_check=True)
                        else:
                            e, f = (0, P * m) if m < 3 else (64, P * (m - 4) + 64)
                            ins = T.transpose(ps[:, bk, oo:oo + 64], w2[e:e + 64, 448 * r + f:448 * r + f + P],
                                              ident[e:e + 64, e:e + 64])
                ins.then_inc(s["m_turn"], 1)

            turn_norm(4)
            gate_logits(1)
            m_weights(0)
            gates_turned(1)
            pe.wait_ge(s["g_h_ready"], 4)
            pe.wait_ge(s["g_l_ready"], 4)
            pe.wait_ge(s["selr"], 1)
            for n in range(16):
                e, c = n // 2, n % 2
                if n >= 2:
                    pe.wait_ge(s["gb_act" if c == 0 else "gb_dve"], n // 2)
                mm2(bank(4 + c), selr1[:, P * e:P * e + P], g_h[:, 512 * c:512 * c + 512],
                    g_l[:, 512 * c:512 * c + 512]).then_inc(s["gb_ps"], 1)

            def m_gate_up(p, m):
                for c in range(2):
                    n = 2 * (MT * p + m) + c
                    if n >= 2:
                        pe.wait_ge(s["m_act"], n - 1)
                        pe.wait_ge(s["m_up"], n - 1)
                    x0, x1 = xh[:, 512 * c:512 * c + 512], xl[:, 512 * c:512 * c + 512]
                    mm2(bank(c), w13T[:, m, :], x0, x1)
                    mm2(bank(2 + c), w13T[:, MT + m, :], x0, x1).then_inc(s["m_gu"], 1)

            def m_down(p, m, e):
                r = slice(0, P) if m != 3 else (slice(0, 64) if e == 0 else slice(64, 128))
                lo, hi = (0, 3) if e == 0 else (3, 6)
                for c in range(2):
                    n = 2 * (MT * p + m) + c
                    pe.wait_ge(s["m_up"], n + 1)
                    if m == lo and (p, e) != (0, 0):
                        pe.wait_ge(s["m_gy"], 4 * p + 2 * e + c - 1)
                    T.matmul(bank(6 + c), w2T[r, m, :], hid[r, c, :], start=(m == lo), stop=(m == hi),
                             skip_group_check=True).then_inc(s["m_down"], 1)

            m_gate_up(0, 0)
            for p in range(PAIRS):
                for m in range(MT):
                    if m + 1 < MT:
                        m_gate_up(p, m + 1)
                    if m <= 3:
                        m_down(p, m, 0)
                    if m >= 3:
                        m_down(p, m, 1)
                if p + 1 < PAIRS:
                    m_weights(p + 1)
                    pe.wait_ge(s["m_wact"], 2 * p + 4)
                    pe.wait_ge(s["m_wdve"], 3 * p + 6 + 0)
                    m_gate_up(p + 1, 0)
            pe.wait_ge(s["m_acc"], 1 + 4 * PAIRS)
            turn_back(4, macc)

        @block.vector
        def _(dve):
            V = nc.vector
            steps = [0]

            def step(ins):
                steps[0] += 1
                ins.then_inc(s["dve_step"], 1)
                dve.wait_ge(s["dve_step"], steps[0])

            dve.wait_ge(s["x_in"], 16)

            def norm(k, src, dst, rms, done=None):
                for t in range(NT):
                    ins = V.bn_stats(bst[:, t, :], src[:, t, :])
                step(ins)
                for t in range(NT):
                    ins = V.bn_aggr(bmv[:, t, :], bst[:, t, :])
                step(ins)
                if rms:
                    step(V.tensor_tensor(ve[:], bmv[:, :, 0], bmv[:, :, 0], ALU.mult))
                    V.scalar_tensor_tensor(ve[:], ve[:], LN_EPS, bmv[:, :, 1], ALU.add,
                                           ALU.add).then_inc(s["ve_ready"], 1)
                else:
                    V.tensor_scalar(ve[:], bmv[:, :, 1], LN_EPS, None, ALU.add).then_inc(s["ve_ready"], 1)
                dve.wait_ge(s["rstd_ready"], k + 1)
                for t in range(NT):
                    if rms:
                        ins = V.tensor_scalar(dst[:, t, :], src[:, t, :], rs[:, t:t + 1], None, ALU.mult)
                    else:
                        ins = V.tensor_scalar(dst[:, t, :], src[:, t, :], bmv[:, t, 0:1], rs[:, t:t + 1],
                                              ALU.subtract, ALU.mult)
                if done is None:
                    step(ins)
                else:
                    ins.then_inc(done, 1)

            def turn_lo(k, gain=None):
                for c in range(2):
                    dve.wait_ge(s["xh_ready"], 2 * k + c + 1)
                    o = slice(512 * c, 512 * c + 512)
                    V.scalar_tensor_tensor(xl[:, o], bank(4 + c), 1.0 if gain is None else gain,
                                           xh[:, o].bitcast(F32), ALU.mult, ALU.subtract).then_inc(s["xl_ready"], 1)

            norm(0, x_tok, nrm, False, s["nrm_ready"])
            dve.wait_ge(s["cst_in"], 16)
            V.tensor_copy(idb[:], ident)
            V.tensor_copy(caub[:], cst[:, C_CAU:C_CAU + S])
            V.tensor_copy(blkb[:], cst[:, C_BLK:C_BLK + P]).then_inc(s["dve_set"], 1)
            dve.wait_ge(s["hi_set"], 1)
            V.tensor_tensor(cl[:], cT[:], ch[:].bitcast(F32), ALU.subtract).then_inc(s["lo_set"], 1)
            dve.wait_ge(s["hi_set"], 2)
            V.tensor_tensor(wg_l[:], vec[:, V_WG0:V_WG0 + 2 * E], wg_h[:].bitcast(F32),
                            ALU.subtract).then_inc(s["lo_set"], 1)

            def w_lo(n):
                dve.wait_ge(s["a_w_h"], n)
                V.tensor_tensor(w_l[:], wst[:, 0:3 * P], w_h[:].bitcast(F32), ALU.subtract).then_inc(s["a_w_l"], 1)

            def queries_in(n):
                dve.wait_ge(s["a_proj"], n)
                for h in range(2):
                    r = slice(64 * h, 64 * h + 64)
                    ins = V.tensor_scalar(qbd[r, 8:16, h, :], ps[r, 3, :].rearrange("p (b q) -> p b q", q=S),
                                          wst[r, 3 * P:3 * P + 1], None, ALU.add)
                ins.then_inc(s["a_dve"], 1)

            def keys_in(n):
                dve.wait_ge(s["a_proj"], n)
                V.tensor_scalar(kT[:, 0, 512:1024], bank(3), wst[:, 3 * P + 1:3 * P + 2], None,
                                ALU.add).then_inc(s["a_dve"], 1)

            w_lo(1)
            turn_lo(0)
            dve.wait_ge(s["pool_set"], 1)
            queries_in(2)
            keys_in(4)

            def softmax_in(n, nb, w):
                for c in range(2):
                    dve.wait_ge(s["a_scores"], n + c + 1)
                    sc3 = bank(c).rearrange("p (b k) -> p b k", k=w)
                    m = mx[:, nb * c:nb * c + nb]
                    V.tensor_reduce(m, sc3, AX, ALU.max).then_inc(s["a_max"], 1)
                    dve.wait_ge(s["a_max"], n + c + 1)
                    V.tensor_tensor(prob[:, c, :].rearrange("p (b k) -> p b k", k=w), sc3, per_group(m, nb, w),
                                    ALU.subtract).then_inc(s["a_sub"], 1)

            def softmax_sum(n, c, nb, w):
                dve.wait_ge(s["a_exp"], n + c + 1)
                d = den[:, nb * c:nb * c + nb]
                V.tensor_reduce(d, prob[:, c, :].rearrange("p (b k) -> p b k", k=w), AX, ALU.add).then_inc(s["a_sum"], 1)
                dve.wait_ge(s["a_sum"], n + c + 1)
                V.reciprocal(rden[:, nb * c:nb * c + nb], d).then_inc(s["a_den"], 1)

            def attT_copy(n):
                dve.wait_ge(s["a_attT"], 2 * n + 2)
                V.tensor_copy(attT[:, 4:8, :], bank(5).rearrange("p (t q) -> p t q", q=P)).then_inc(s["a_attT_dve"], 1)

            def pair_step(j, first, last):
                if not first:
                    attT_copy(j - 1)
                softmax_in(2 * j, 8, S)
                if not first:
                    dve.wait_ge(s["a_out"], 2 * j)
                    V.tensor_copy(of_batches(big[:, bass.ds(j - 1, 1), :], 1), ps[:, 7:8, :].rearrange(
                        "p a (t q) -> p a t q", q=S)).then_inc(s["a_out_dve"], 1)
                w_lo(j + 2)
                softmax_sum(2 * j, 0, 8, S)
                dve.wait_ge(s["a_proj"], 6 * j + 6)
                V.tensor_copy(v_sb[:, 4:8, :], bank(3).rearrange("p (t d) -> p t d", d=P)).then_inc(s["a_dve"], 1)
                softmax_sum(2 * j, 1, 8, S)
                if not last:
                    queries_in(6 * j + 8)
                    keys_in(6 * j + 10)

            pair_step(0, True, False)
            with dve.Fori(1, HP0 - 1) as j:
                pair_step(j, False, False)
            pair_step(HP0 - 1, False, True)
            attT_copy(HP0 - 1)
            dve.wait_ge(s["a_out"], 2 * HP0)
            V.tensor_copy(of_batches(big[:, HP0 - 1:HP0, :], 1), ps[:, 7:8, :].rearrange(
                "p a (t q) -> p a t q", q=S)).then_inc(s["a_out_dve"], 1)

            dve.wait_ge(s["yc_ps"], 1)
            V.tensor_tensor(yc[:], ps[:, 2, 0:1], vec[:, V_BO:V_BO + 1], ALU.add).then_inc(s["yc_ready"], 1)
            dve.wait_ge(s["yc_ready"], 1)
            dve.wait_ge(s["y_ready"], 2)
            V.tensor_scalar(yT[:, 512:1024], bank(1), yc[:], None, ALU.add).then_inc(s["yT_dve"], 1)

            def residual(k, gate):
                for c in range(2):
                    dve.wait_ge(s["back"], 2 * k + c + 1)
                    xx = x_tok[:, 4 * c:4 * c + 4, :]
                    ins = V.scalar_tensor_tensor(xx, bank(2 + c).rearrange("p (t d) -> p t d", d=D),
                                                 tg[:, gate:gate + 1], xx, ALU.mult, ALU.add)
                    if c == 0:
                        step(ins)
                ins.then_inc(s["x_new"], 1)
                dve.wait_ge(s["x_new"], k + 1)

            dve.wait_ge(s["tanh_done"], 1)
            residual(0, 0)

            norm(1, x_tok, nrm, False, s["nrm_ready"])
            dve.wait_ge(s["f_w_h"], 1)
            V.tensor_tensor(gu_l[:], gu_st[:], gu_h[:].bitcast(F32), ALU.subtract).then_inc(s["f_w_l"], 1)
            dve.wait_ge(s["sel_in"], 32)
            V.tensor_copy(selr1[:], sel1[:]).then_inc(s["selr"], 1)
            V.tensor_copy(selr0[:], sel0[:, 0:P]).then_inc(s["f_sel"], 1)
            turn_lo(1)
            rev = cst[:, C_REV:C_REV + E].unsqueeze(1).to_broadcast([P, NT, E])

            def first_of(dst, key, top):
                step(V.tensor_tensor(gk[:], key, per_group(top, NT, E), ALU.is_equal))
                step(V.tensor_tensor(gk[:], gk[:], rev, ALU.mult))
                step(V.tensor_reduce(gm[:], gk[:], AX, ALU.max))
                step(V.tensor_tensor(dst, gk[:], per_group(gm[:], NT, E), ALU.is_equal))

            def gating(k):
                dve.wait_ge(s["logits"], k + 1)
                step(V.tensor_copy(lg[:], ps[:, 6, 0:NT * E].rearrange("p (t e) -> p t e", e=E)))
                step(V.tensor_reduce(gm[:], lg[:], AX, ALU.max))
                V.tensor_tensor(gp[:], lg[:], per_group(gm[:], NT, E), ALU.subtract).then_inc(s["g_sub"], 1)
                dve.wait_ge(s["g_exp"], k + 1)
                if k == 1:
                    step(V.tensor_reduce(gm[:], gp[:], AX, ALU.add))
                    step(V.reciprocal(gm[:], gm[:]))
                    step(V.tensor_tensor(gp[:], gp[:], per_group(gm[:], NT, E), ALU.mult))
                    step(V.tensor_copy(lg[:], gp[:]))
                    step(V.tensor_reduce(gm[:], lg[:], AX, ALU.max))
                first_of(f1[:], lg[:], gm[:])
                step(V.scalar_tensor_tensor(lg[:], f1[:], -3e38, lg[:], ALU.mult, ALU.add))
                step(V.tensor_reduce(gm[:], lg[:], AX, ALU.max))
                first_of(f2[:], lg[:], gm[:])
                step(V.tensor_tensor(f1[:], f1[:], f2[:], ALU.add))
                step(V.tensor_tensor(gp[:], gp[:], f1[:], ALU.mult))
                step(V.tensor_reduce(gm[:], gp[:], AX, ALU.add))
                step(V.reciprocal(gm[:], gm[:]))
                V.tensor_tensor(lg[:], gp[:], per_group(gm[:], NT, E), ALU.mult).then_inc(s["gates"], 1)
                for c in range(2):
                    dve.wait_ge(s["g_h_ready"], 2 * k + c + 1)
                    o = slice(512 * c, 512 * c + 512)
                    V.tensor_tensor(g_l[:, o], ps[0:E, 4 + c, :], g_h[:, o].bitcast(F32),
                                    ALU.subtract).then_inc(s["g_l_ready"], 1)

            gating(0)

            def expert_step(m, first, last):
                for c in range(2):
                    dve.wait_ge(s["f_act"], 2 * m + c + 1)
                    if not first:
                        dve.wait_ge(s["f_hid"], 2 * m + c - 1)
                    V.tensor_tensor(hid1[:, c, :], act[:, c, :], bank(2 + c), ALU.mult).then_inc(s["f_h1"], 1)
                    if c == 0 and not last:
                        dve.wait_ge(s["f_w_h"], m + 2)
                        V.tensor_tensor(gu_l[:], gu_st[:], gu_h[:].bitcast(F32),
                                        ALU.subtract).then_inc(s["f_w_l"], 1)
                for c in range(2):
                    dve.wait_ge(s["f_h1"], 2 * m + c + 1)
                    dve.wait_ge(s["f_gate"], 2 * m + c + 1)
                    if not first:
                        dve.wait_ge(s["f_down"], 2 * m + c - 1)
                    V.tensor_tensor(hid[:, c, :], hid1[:, c, :], bank(4 + c), ALU.mult).then_inc(s["f_hid"], 1)
                if not last:
                    V.tensor_copy(selr0[:], sel0[:, bass.ds((m + 1) * P, P)]).then_inc(s["f_sel"], 1)

            expert_step(0, True, False)
            with dve.Fori(1, M0 - 1) as m:
                expert_step(m, False, False)
            expert_step(M0 - 1, False, True)
            dve.wait_ge(s["f_down"], 2 * M0)
            V.tensor_copy(yT[:, 512:1024], bank(7)).then_inc(s["yT_dve"], 1)
            residual(1, 2)

            norm(2, x_tok, nrm, False, s["nrm_ready"])
            dve.wait_ge(s["hi_set"], 3)
            V.tensor_tensor(wx_l[:], wx_st[:], wx_h[:].bitcast(F32), ALU.subtract).then_inc(s["lo_set"], 1)
            turn_lo(2)
            dve.wait_ge(s["x_proj"], 2)
            V.tensor_scalar(kT[:, 1, 512:1024], bank(1), vec[:, V_BQ:V_BQ + 1], None, ALU.add).then_inc(s["x_dve"], 1)
            dve.wait_ge(s["x_proj"], 4)
            V.tensor_scalar(kT[:, 0, 512:1024], bank(3), vec[:, V_BK:V_BK + 1], None, ALU.add).then_inc(s["x_dve"], 1)
            dve.wait_ge(s["x_proj"], 6)
            V.tensor_copy(v_sb[:, 4:8, :], bank(7).rearrange("p (t d) -> p t d", d=P)).then_inc(s["x_dve"], 1)
            softmax_in(2 * HP0, 4, P)
            for c in range(2):
                softmax_sum(2 * HP0, c, 4, P)
            attT_copy(HP0)
            dve.wait_ge(s["a_out"], 2 * HP0 + 2)
            V.tensor_scalar(yT[:, 512:1024], bank(7), vec[:, V_BV:V_BV + 1], None, ALU.add).then_inc(s["yT_dve"], 1)

            def quant_stats(n, extra=None, done=None):
                a = lambda t: t[:, 0:n]
                V.tensor_reduce(a(qmx), st[:, 0:n, :], AX, ALU.max)
                step(V.tensor_reduce(a(qmn), st[:, 0:n, :], AX, ALU.min))
                step(V.tensor_tensor(a(qsc), a(qmx), a(qmn), ALU.subtract))
                step(V.tensor_scalar(a(qsc), a(qsc), 1e-5, 1.0 / QMAX, ALU.max, ALU.mult))
                step(V.reciprocal(a(qrs), a(qsc)))
                step(V.scalar_tensor_tensor(a(qb), a(qmn), -1.0, a(qrs), ALU.mult, ALU.mult))
                step(V.tensor_scalar(a(qb), a(qb), MAGIC, None, ALU.add))
                step(V.tensor_scalar(a(qb), a(qb), MAGIC, 0.0, ALU.subtract, ALU.max))
                step(V.tensor_scalar(a(qb), a(qb), QMAX, -1.0, ALU.min, ALU.mult))
                step(V.tensor_scalar(a(qlo), a(qb), MAGIC, None, ALU.add))
                if extra is not None:
                    extra()
                V.tensor_scalar(a(qhi), a(qlo), QMAX, None, ALU.add).then_inc(done, 1)

            def clip(g, sem_out):
                V.tensor_scalar(st[:, g, :], st[:, g, :], qlo[:, g:g + 1], qhi[:, g:g + 1], ALU.max,
                                ALU.min).then_inc(sem_out, 1)

            dve.wait_ge(s["wl_in"], 16)
            quant_stats(20, lambda: V.tensor_copy(wsc[:], qsc[:, 0:8]), s["q_stats"])
            for g in range(20):
                dve.wait_ge(s["q_round"], g + 1)
                clip(g, s["q_clip"])
            residual(2, 1)
            dve.wait_ge(s["w_act"], 2)
            for a in range(2):
                ins = V.tensor_copy(wqR[:, :, 64 * a:64 * a + 64], wqT[:, :, 64 - 64 * a:128 - 64 * a].bitcast(F32))
            ins.then_inc(s["w_rot"], 1)
            dve.wait_ge(s["w_act"], 3)
            V.tensor_tensor(wkv_l[:], bank(2), wkv_h[:].bitcast(F32), ALU.subtract).then_inc(s["w_dve"], 1)
            dve.wait_ge(s["w_turn"], 5)
            V.tensor_copy(woT[:, 4:8, :], bank(7).rearrange("p (t d) -> p t d", d=P)).then_inc(s["w_dve"], 1)
            norm(3, x_tok, hs, False)
            norm(4, hs, nrm, True, s["nrm_ready"])
            turn_lo(3, vec[:, V_G1:V_G1 + 1])
            for t in range(1, NT, 2):
                dve.wait_ge(s["kv_ps"], t + 1)
                V.tensor_copy(st[:, 4 * t:4 * t + 4, :],
                              bank(1).rearrange("p (g d) -> p g d", d=P)).then_inc(s["kv_dve"], 1)
            dve.wait_ge(s["kv_dve"], 4)
            dve.wait_ge(s["kv_act"], 4)
            dve.wait_ge(s["q_deq"], 12)
            quant_stats(32, None, s["q_stats"])
            for g in range(32):
                dve.wait_ge(s["q_round"], 20 + g + 1)
                clip(g, s["q_clip"])

            cosT = cst[:, C_COS:C_COS + S].unsqueeze(1).to_broadcast([P, 8, S])
            sinT = cst[:, C_SIN:C_SIN + S].unsqueeze(1).to_broadcast([P, 8, S])

            def rotate(hp):
                for hh in range(2):
                    for c in range(2):
                        n = 4 * hp + 2 * hh + c
                        h = 2 * hp + hh
                        for i, (dst, scale, table, done) in enumerate(((q1s, wsc, cosT, "r_q1"),
                                                                       (q2s, wscR, sinT, "r_q2"))):
                            dve.wait_ge(s["r_ps"], 2 * n + i + 1)
                            if n >= 2:
                                dve.wait_ge(s["r_q"], n - 1)
                            V.scalar_tensor_tensor(dst[:, n % 2, :].rearrange("p (b q) -> p b q", q=S),
                                                   bank(2 + i).rearrange("p (b q) -> p b q", q=S),
                                                   scale[:, h:h + 1], table, ALU.mult, ALU.mult).then_inc(s[done], 1)

            dve.wait_ge(s["scr_in"], 32)
            dve.wait_ge(s["x_new"], 3)
            rotate(0)
            dve.wait_ge(s["q_deq"], 44)
            kk = st[:, 0:32, :].rearrange("p (t g) d -> p t g d", g=4)[:, :, 0:2, :]
            kr = big[:, 0:2, :].rearrange("p a (t d) -> p t a d", d=D)
            cosK = cst[:, C_COSK:C_COSK + D].unsqueeze(1).unsqueeze(1).to_broadcast([P, NT, 2, D])
            sinK = lambda a: cst[:, C_SINK + 64 * a:C_SINK + 64 * a + 64].unsqueeze(1).unsqueeze(1).to_broadcast(
                [P, NT, 2, 64])
            for a in range(2):
                ins = V.tensor_tensor(kr[:, :, :, 64 * a:64 * a + 64], kk[:, :, :, 64 - 64 * a:128 - 64 * a], sinK(a),
                                      ALU.mult)
            step(ins)
            step(V.tensor_tensor(kk, kk, cosK, ALU.mult))
            V.tensor_tensor(kk, kk, kr, ALU.add).then_inc(s["k_rope"], 1)
            for n in (1, 3):
                dve.wait_ge(s["k_turn"], n + 1)
                V.tensor_copy(kT[:, n // 2, 512:1024], bank(5)).then_inc(s["k_dve"], 1)

            def out_quarters(h):
                for q in range(2):
                    dve.wait_ge(s["a_out"], O_L1 + 4 * h + 2 * q + 2)
                    V.tensor_copy(
                        of_batches(big[:, 2 * h:2 * h + 2, 512 * q:512 * q + 512], 1).rearrange("p a t q -> p t a q"),
                        bank(7).rearrange("p (t a q) -> p t a q", a=2, q=S)).then_inc(s["a_out_dve"], 1)

            for hp in range(HP1):
                n = 2 * HP0 + 2 + 2 * hp
                if hp > 0:
                    attT_copy(HP0 + hp)
                softmax_in(n, 8, S)
                for c in range(2):
                    softmax_sum(n, c, 8, S)
                if hp > 0:
                    out_quarters(hp - 1)
                if hp + 1 < HP1:
                    rotate(hp + 1)
            attT_copy(HP0 + HP1)
            out_quarters(HP1 - 1)
            dve.wait_ge(s["y_ready"], 4)
            V.tensor_copy(yT[:, 512:1024], bank(1)).then_inc(s["yT_dve"], 1)
            for c in range(2):
                dve.wait_ge(s["back"], 6 + c + 1)
                hh = hs[:, 4 * c:4 * c + 4, :]
                ins = V.tensor_tensor(hh, bank(2 + c).rearrange("p (t d) -> p t d", d=D), hh, ALU.add)
                if c == 0:
                    step(ins)
            ins.then_inc(s["x_new"], 1)
            dve.wait_ge(s["x_new"], 4)
            norm(5, hs, nrm, True, s["nrm_ready"])

            def m_prep(p):
                dve.wait_ge(s["wm_in"], 16 * p + 16)
                if p > 0:
                    dve.wait_ge(s["m_act"], 2 * MT * p)
                quant_stats(21, lambda: V.tensor_copy(msc[:], qsc[:, 0:2 * MT]), s["m_stats"])
                for g in range(21):
                    dve.wait_ge(s["m_round"], 21 * p + g + 1)
                    clip(g, s["m_clip"])

            def m_weights(p):
                for n in range(2):
                    k = 4 if n == 0 else 3
                    dve.wait_ge(s["m_turn"], 5 * p + 2 * n + 2)
                    V.tensor_scalar(w13T[:, MT + 4 * n:MT + 4 * n + k, :],
                                    ps[:, 5, 0:k * P].rearrange("p (t d) -> p t d", d=P), MAGIC, None,
                                    ALU.subtract).then_inc(s["m_wdve"], 1)
                dve.wait_ge(s["m_turn"], 5 * p + 5)
                for bk, t0, k in ((4, 0, 4), (5, 4, 3)):
                    ins = V.tensor_copy(
                        w2T[:, t0:t0 + k, :].rearrange("p t (r c) -> p t c r", c=2),
                        ps[:, bk, 0:k * P].rearrange("p (t c r) -> p t c r", c=2, r=64))
                ins.then_inc(s["m_wdve"], 1)

            turn_lo(4, vec[:, V_G2:V_G2 + 1])
            m_prep(0)
            m_weights(0)
            gating(1)
            for n in range(1, 16, 2):
                dve.wait_ge(s["gb_ps"], n + 1)
                V.tensor_copy(big[:, n // 2, 512:1024], bank(5)).then_inc(s["gb_dve"], 1)
            dve.wait_ge(s["gb_dve"], 8)
            dve.wait_ge(s["gb_act"], 8)

            def gated(p, e):
                for c in range(2):
                    n = 4 * p + 2 * e + c
                    dve.wait_ge(s["m_down"], 16 * p + (7 + c if e == 0 else 15 + c))
                    if n >= 2:
                        dve.wait_ge(s["m_acc"], n)
                    V.tensor_tensor(hid1[:, c, :], bank(6 + c), big[:, 2 * p + e, 512 * c:512 * c + 512],
                                    ALU.mult).then_inc(s["m_gy"], 1)

            for p in range(PAIRS):
                for m in range(MT):
                    for c in range(2):
                        n = 2 * (MT * p + m) + c
                        dve.wait_ge(s["m_act"], n + 1)
                        if n >= 2:
                            prev = MT * p + m - 1
                            q, r = divmod(prev, MT)
                            dve.wait_ge(s["m_down"], 16 * q + 2 * r + c + 1 + (2 if r >= 3 else 0))
                        V.scalar_tensor_tensor(hid[:, c, :], bank(2 + c), msc[:, MT + m:MT + m + 1], act[:, c, :],
                                               ALU.mult, ALU.mult).then_inc(s["m_up"], 1)
                    if m == 3:
                        gated(p, 0)
                gated(p, 1)
                if p + 1 < PAIRS:
                    m_prep(p + 1)
                    m_weights(p + 1)
            for c in range(2):
                dve.wait_ge(s["back"], 8 + c + 1)
                hh = hs[:, 4 * c:4 * c + 4, :]
                step(V.tensor_tensor(hh, bank(2 + c).rearrange("p (t d) -> p t d", d=D), hh, ALU.add))
                xx = x_tok[:, 4 * c:4 * c + 4, :]
                ins = V.scalar_tensor_tensor(xx, hh, tg[:, 3:4], xx, ALU.mult, ALU.add)
            ins.then_inc(s["x_new"], 1)


O_L1 = 2 * HP0 + 2


def constants():
    c = np.zeros((P, C_END), np.float32)
    i = np.arange(P)
    c[:, C_ID:C_ID + P] = np.eye(P)
    c[:, C_CAU:C_CAU + S] = np.where(np.arange(S)[None] <= (i % S)[:, None], 0.0, -1e30)
    c[:, C_BLK:C_BLK + P] = np.where((i // S)[None] == (i // S)[:, None], 0.0, -1e30)
    inv = (np.float32(1.0) / np.float32(1e6) ** (np.arange(0, D, 2, dtype=np.float32) / np.float32(D))).astype(np.float32)
    freqs = np.arange(S, dtype=np.float32)[:, None] * inv[None]
    emb = np.concatenate([freqs, freqs], -1)
    cos, sin = np.cos(emb), np.sin(emb)
    sin = sin * np.where(i < 64, -1.0, 1.0)[None]
    c[:, C_COS:C_COS + S], c[:, C_SIN:C_SIN + S] = cos.T, sin.T
    c[:, C_COSK:C_COSK + D], c[:, C_SINK:C_SINK + D] = np.tile(cos, (2, 1)), np.tile(sin, (2, 1))
    c[:, C_REV:C_REV + E] = np.arange(E, 0, -1)
    sel0 = (np.arange(M0 * P)[None] // 176 == np.arange(E)[:, None]).astype(np.float32)
    sel1 = (np.arange(E * P)[None] // P == np.arange(E)[:, None]).astype(np.float32)
    return c, sel0, sel1


def kernel(**inputs):
    import concourse.bacc as _bacc
    from concourse.bass_utils import run_bass_kernel_spmd as _run

    a = {k: np.asarray(v) for k, v in inputs.items()}
    cst, sel0, sel1 = constants()
    col = lambda v: v.reshape(-1, P).T
    row = lambda v: np.tile(v[None], (P, 1))
    vec = np.concatenate([col(a["L0_xattn_bo"]), col(a["L1_xattn_bq"]), col(a["L1_xattn_bk"]), col(a["L1_xattn_bv"]),
                          col(a["L1_ffn_g1"]), col(a["L1_ffn_g2"]), col(a["L0_xattn_bv"]), a["L0_ffn_w_gate"],
                          a["L1_ffn_w_gate"].T, row(a["g_xattn"]), row(a["g_ffn"])], 1)
    tiles = lambda w: w.reshape(-1, P, D)
    w0 = np.zeros((HP0 + 1, P, WST), np.float32)
    w0[:HP0, :, 0:P] = tiles(a["L0_xattn_Wq"]).transpose(0, 2, 1)
    w0[:HP0, :, P:2 * P] = tiles(a["L0_xattn_Wk"]).transpose(0, 2, 1)
    w0[1:, :, 2 * P:3 * P] = tiles(a["L0_xattn_Wv"]).transpose(0, 2, 1)
    w0[:HP0, :, 3 * P] = a["L0_xattn_bq"].reshape(HP0, P)
    w0[:HP0, :, 3 * P + 1] = a["L0_xattn_bk"].reshape(HP0, P)
    up_cols = lambda w: w.transpose(1, 0, 2).reshape(D, M0, P).transpose(1, 0, 2)
    gu0 = np.concatenate([up_cols(a["L0_ffn_w_g"]), up_cols(a["L0_ffn_w_u"])], 2)
    wx = np.concatenate([a["L1_xattn_Wq"].T, a["L1_xattn_Wk"].T, a["L1_xattn_Wv"].T], 1)
    wl = np.concatenate([tiles(a["L1_ffn_w_q"]).transpose(1, 0, 2), tiles(a["L1_ffn_w_k"]).transpose(1, 0, 2),
                         tiles(a["L1_ffn_w_v"]).transpose(1, 0, 2), a["L1_ffn_w_o"].reshape(D, 8, P)], 1)
    pair = lambda w: w.reshape(PAIRS, MT, P, D).transpose(0, 2, 1, 3)
    wm = np.concatenate([pair(a["L1_ffn_w1"]), pair(a["L1_ffn_w3"]),
                         a["L1_ffn_w2"].reshape(PAIRS, P, MT, P)], 2)
    tok = lambda v: v.reshape(NT, P, D).transpose(1, 0, 2)
    arrays = {
        "cst": cst, "vec": vec, "x": tok(a["x"]), "ctx": a["ctx_1024"].reshape(TOK, D).T, "w0": w0,
        "wo0": a["L0_xattn_Wo"].T.reshape(HP0, P, D).transpose(1, 0, 2), "sel0": sel0, "sel1": sel1, "gu0": gu0,
        "d0": a["L0_ffn_w_d"].reshape(M0, P, D), "wx": wx, "wl": wl, "wm": wm,
    }
    nc = _bacc.Bacc("TRN2", target_bir_lowering=False, num_devices=1)
    args = []
    for k in arrays:
        arrays[k] = np.ascontiguousarray(arrays[k])
        args.append(nc.dram_tensor(k + "_dram", arrays[k].shape, F32, kind="ExternalInput").ap())
    args.append(nc.dram_tensor("out_dram", (P, NT, D), F32, kind="ExternalOutput").ap())
    build(nc, *args)
    r = _run(nc, [{k + "_dram": v for k, v in arrays.items()}], core_ids=[0])
    got = r.results[0]["out_dram"]
    return got.transpose(1, 0, 2).reshape(B, S, D)
```

```python
from contextlib import ExitStack

import numpy as np

import concourse.bass as bass
from concourse import mybir

F32 = mybir.dt.float32
F32R = mybir.dt.float32r
BF16 = mybir.dt.bfloat16
ALU = mybir.AluOpType
ACT = mybir.ActivationFunctionType
AX = mybir.AxisListType.X

P = 128
B, S, D = 16, 64, 128
TOK = B * S
NT = TOK // P
HALF = TOK // 2
E = 8
HP0 = 8
HP1 = 4
M0 = 11
PAIRS = 4
MT = 7
QMAX = 15.0
MAGIC = 1.5 * 2.0 ** 23
LN_EPS = 1e-5

C_ID, C_CAU, C_BLK, C_COS, C_SIN, C_COSK, C_SINK, C_REV, C_END = (
    0, 128, 192, 320, 384, 448, 576, 704, 712)
V_BO, V_BQ, V_BK, V_BV, V_G1, V_G2, V_BV0, V_WG0, V_WG1, V_GX, V_GF, V_END = (
    0, 1, 2, 3, 4, 5, 6, 14, 22, 30, 32, 34)
WST = 3 * P + 2


def build(nc, cst_d, vec_d, x_d, ctx_d, w0_d, wo0_d, sel0_d, sel1_d, gu0_d, d0_d, wx_d, wl_d, wm_d, out_d):
    with ExitStack() as ctx:
        def sb(name, shape, dt=F32):
            return ctx.enter_context(nc.sbuf_tensor(name, shape, dt))

        def sem(name):
            return ctx.enter_context(nc.semaphore(name))

        ps = ctx.enter_context(nc.psum_tensor("ps", [P, 8, 512], F32))

        cst = sb("cst", [P, C_END])
        vec = sb("vec", [P, V_END])
        idb = sb("idb", [P, P], BF16)
        caub = sb("caub", [P, S], BF16)
        blkb = sb("blkb", [P, P], BF16)
        tg = sb("tg", [P, 4])
        wg_h = sb("wg_h", [P, 2 * E], F32R)
        wg_l = sb("wg_l", [P, 2 * E], F32R)
        half = sb("half", [P, NT])
        magic = sb("magic", [P, 1])
        sel0 = sb("sel0", [E, M0 * P])
        selr0 = sb("selr0", [E, P], F32R)
        selr1 = sb("selr1", [E, E * P], F32R)
        x_tok = sb("x_tok", [P, NT, D])
        nrm = sb("nrm", [P, NT, D])
        hs = sb("hs", [P, NT, D])
        xh = sb("xh", [P, TOK], F32R)
        xl = sb("xl", [P, TOK], F32R)
        cT = sb("cT", [P, TOK])
        ch = sb("ch", [P, TOK], F32R)
        cl = sb("cl", [P, TOK], F32R)
        bst = sb("bst", [P, NT, 6])
        bmv = sb("bmv", [P, NT, 2])
        ve = sb("ve", [P, NT])
        rs = sb("rs", [P, NT])
        wst = sb("wst", [P, WST])
        w_h = sb("w_h", [P, 3 * P], F32R)
        w_l = sb("w_l", [P, 3 * P], F32R)
        qbd = sb("qbd", [P, B, 2, S])
        kT = sb("kT", [P, 2, TOK])
        v_sb = sb("v_sb", [P, NT, P])
        prob = sb("prob", [P, 2, 512])
        attT = sb("attT", [P, NT, P])
        mx = sb("mx", [P, B])
        den = sb("den", [P, B])
        rden = sb("rden", [P, B])
        big = sb("big", [P, 8, TOK])
        wo0 = sb("wo0", [P, HP0, D])
        yT = cT
        yc = sb("yc", [P, 1])
        lg = sb("lg", [P, NT, E])
        gp = sb("gp", [P, NT, E])
        gk = sb("gk", [P, NT, E])
        f1 = sb("f1", [P, NT, E])
        f2 = sb("f2", [P, NT, E])
        gm = sb("gm", [P, NT])
        g_h = sb("g_h", [E, TOK], F32R)
        g_l = sb("g_l", [E, TOK], F32R)
        gu_st = sb("gu_st", [P, 2 * P])
        gu_h = sb("gu_h", [P, 2, 2 * P], F32R)
        gu_l = sb("gu_l", [P, 2, 2 * P], F32R)
        d_st = sb("d_st", [P, 2, D])
        act = sb("act", [P, 2, 512])
        hid1 = sb("hid1", [P, 2, 512])
        hid = sb("hid", [P, 2, 512])
        wx_st = sb("wx_st", [P, 3 * P])
        wx_h = sb("wx_h", [P, 3 * P], F32R)
        wx_l = sb("wx_l", [P, 3 * P], F32R)
        st = sb("st", [P, 32, P])
        wqT = sb("wqT", [P, 8, P], F32R)
        wqR = sb("wqR", [P, 8, P], F32R)
        wkv_h = sb("wkv_h", [P, 4 * P], F32R)
        wkv_l = sb("wkv_l", [P, 4 * P], F32R)
        woT = wo0
        stB = sb("stB", [P, 21, P])
        q1s = sb("q1s", [P, 2, 512])
        sel1 = q1s[0:E, :, :].rearrange("e a c -> e (a c)")
        q2s = sb("q2s", [P, 2, 512])
        qs = [{n: sb(f"q_{n}{i}", [P, 32]) for n in ("max", "min", "scale", "recip", "base", "lo", "hi")}
              for i in range(2)]
        rs2 = sb("rs2", [P, NT])
        wsc = sb("wsc", [P, 8])
        wscR = sb("wscR", [P, 8])
        w13T = sb("w13T", [P, 2 * MT, P], F32R)
        w2T = sb("w2T", [P, MT, D])
        macc = kT[:, 0, :]

        ident = cst[:, C_ID:C_ID + P]

        def bank(n):
            return ps[:, n, :]

        s = {n: sem(n) for n in (
            "cst_in", "vec_in", "x_in", "ctx_in", "wo0_in", "sel_in", "w0_in", "gu_in", "d_in0", "d_in1", "wx_in", "wl_in",
            "wm_in0", "wm_in1", "scr_in", "stored",
            "pool_set", "tanh_done", "dve_set", "hi_set", "lo_set",
            "dve_step", "ve_ready", "rstd_ready", "nrm_ready", "turned", "xh_ready", "xl_ready",
            "yT_act", "yT_dve", "back", "x_new",
            "a_w_h", "a_w_l", "a_proj", "a_act", "a_dve", "a_scores", "a_max", "a_sub", "a_exp", "a_sum", "a_den",
            "a_norm", "a_attT", "a_attT_act", "a_attT_dve", "a_out", "a_out_act", "a_out_dve",
            "y_ready", "yc_ps", "yc_ready",
            "logits", "g_sub", "g_exp", "gates", "gT", "g_h_ready", "g_l_ready",
            "f_w_h", "f_w_l", "f_sel", "f_gu", "f_act", "f_h1", "f_gate", "f_hid", "f_down",
            "x_proj", "x_act", "x_dve", "q_stats", "q_round", "q_clip", "q_deq", "w_turn", "w_act", "w_dve",
            "w_rot", "kv_ps", "kv_act", "kv_dve", "k_rope", "k_turn", "k_act", "k_dve",
            "r_ps", "r_q1", "r_q2", "r_q", "r_wait",
            "q_red", "q_done", "m_stats", "m_round", "m_clip", "m_deq", "aux_ps", "aux_act",
            "m_gu", "m_act", "m_up", "m_down", "m_gy", "m_acc", "selr",
        )}

        def mm3(out, a_h, a_l, b_h, b_l, start=True, stop=True):
            nc.tensor.matmul(out, a_h, b_h, start=start, stop=False, skip_group_check=True)
            nc.tensor.matmul(out, a_h, b_l, start=False, stop=False, skip_group_check=True)
            return nc.tensor.matmul(out, a_l, b_h, start=False, stop=stop, skip_group_check=True)

        def mm2(out, a, b_h, b_l):
            nc.tensor.matmul(out, a, b_h, start=True, stop=False, skip_group_check=True)
            return nc.tensor.matmul(out, a, b_l, start=False, stop=True, skip_group_check=True)

        def per_group(t, n, w, sl=slice(None)):
            return t.unsqueeze(2).to_broadcast([P, n, w])

        def of_batches(t, b):
            return t.rearrange("p a (t b q) -> p a t b q", b=2, q=S)[:, :, :, b, :]

        block = ctx.enter_context(nc.Block())

        @block.sync
        def _(sp):
            sp.dma_start(x_tok[:], x_d).then_inc(s["x_in"], 16)
            sp.dma_start(cst[:], cst_d).then_inc(s["cst_in"], 16)
            sp.dma_start(cT[:], ctx_d).then_inc(s["ctx_in"], 16)
            sp.dma_start(vec[:], vec_d).then_inc(s["vec_in"], 16)
            sp.dma_start(wst[:], w0_d[0]).then_inc(s["w0_in"], 16)
            sp.wait_ge(s["a_w_l"], 1)
            sp.wait_ge(s["a_act"], 2)
            sp.wait_ge(s["a_dve"], 2)
            sp.dma_start(wst[:], w0_d[1]).then_inc(s["w0_in"], 16)
            sp.dma_start(wo0[:], wo0_d).then_inc(s["wo0_in"], 16)
            sp.dma_start(sel0[:], sel0_d).then_inc(s["sel_in"], 16)
            sp.dma_start(sel1, sel1_d).then_inc(s["sel_in"], 16)
            sp.dma_start(st[:, 0:20, :], wl_d).then_inc(s["wl_in"], 16)
            sp.dma_start(wx_st[:], wx_d).then_inc(s["wx_in"], 16)
            sp.dma_start(gu_st[:], gu0_d[0]).then_inc(s["gu_in"], 16)
            for m in range(2):
                sp.dma_start(d_st[:, m, :], d0_d[m]).then_inc(s[f"d_in{m}"], 16)
            sp.dma_start(stB[:], wm_d[0]).then_inc(s["wm_in0"], 16)
            with sp.Fori(0, HP0 - 1) as j:
                sp.wait_ge(s["a_w_l"], j + 2)
                sp.wait_ge(s["a_act"], 3 * j + 5)
                sp.wait_ge(s["a_dve"], 3 * j + 5)
                sp.dma_start(wst[:], w0_d[bass.ds(j + 2, 1)].rearrange("n p c -> (n p) c")).then_inc(s["w0_in"], 16)
            sp.wait_ge(s["f_w_l"], 1)
            sp.dma_start(gu_st[:], gu0_d[1]).then_inc(s["gu_in"], 16)
            with sp.Fori(0, M0 - 3, 2) as m:
                for u in range(2):
                    sp.wait_ge(s["f_w_l"], m + u + 2)
                    sp.dma_start(gu_st[:], gu0_d[bass.ds(m + u + 2, 1)].rearrange("n p c -> (n p) c")).then_inc(
                        s["gu_in"], 16)
                    sp.wait_ge(s["f_down"], 2 * (m + u) + 2)
                    sp.dma_start(d_st[:, u, :], d0_d[bass.ds(m + u + 2, 1)].rearrange("n p c -> (n p) c")).then_inc(
                        s[f"d_in{u}"], 16)
            sp.wait_ge(s["f_w_l"], M0 - 1)
            sp.dma_start(gu_st[:], gu0_d[M0 - 1]).then_inc(s["gu_in"], 16)
            sp.wait_ge(s["f_down"], 2 * (M0 - 2))
            sp.dma_start(d_st[:, 0, :], d0_d[M0 - 1]).then_inc(s["d_in0"], 16)
            sp.wait_ge(s["q_stats"], 1)
            sp.dma_start(wscR[0:64, :], wsc[64:128, :]).then_inc(s["scr_in"], 16)
            sp.dma_start(wscR[64:128, :], wsc[0:64, :]).then_inc(s["scr_in"], 16)
            for p in range(1, PAIRS):
                if p == 1:
                    sp.wait_ge(s["a_out"], O_L1 + 4 * HP1)
                else:
                    sp.wait_ge(s["aux_ps"], AUX[("w2", p - 2, 1)] + 1)
                sp.dma_start(st[:, 0:21, :] if p % 2 else stB[:], wm_d[p]).then_inc(s[f"wm_in{p % 2}"], 16)
            sp.wait_ge(s["x_new"], 1)
            sp.dma_start(out_d, x_tok[:]).then_inc(s["stored"], 16)
            sp.wait_ge(s["stored"], 16)

        @block.gpsimd
        def _(pool):
            nc.gpsimd.memset(qbd[:], 0.0)
            nc.gpsimd.memset(half[:], -0.5)
            nc.gpsimd.memset(magic[:], MAGIC).then_inc(s["pool_set"], 1)
            pool.wait_ge(s["pool_set"], 1)

            def rstd(k, dst=rs):
                for c in range(2):
                    pool.wait_ge(s["ve_ready"], 2 * k + c + 1)
                    h = slice(4 * c, 4 * c + 4)
                    nc.gpsimd.tensor_tensor(dst[:, h], ve[:, h], half[:, h], ALU.pow).then_inc(s["rstd_ready"], 1)

            def normalise(n, c, nb, w):
                pool.wait_ge(s["a_den"], n + c + 1)
                pr = prob[:, c, :].rearrange("p (b k) -> p b k", k=w)
                nc.gpsimd.tensor_tensor(pr, pr, per_group(rden[:, nb * c:nb * (c + 1)], nb, w),
                                        ALU.mult).then_inc(s["a_norm"], 1)

            rstd(0)
            with pool.Fori(0, HP0) as j:
                for c in range(2):
                    normalise(2 * j, c, 8, S)

            def dequant(t, q, g, n_clip, done):
                pool.wait_ge(n_clip[0], n_clip[1])
                nc.gpsimd.tensor_scalar(t[:, g, :], t[:, g, :], -MAGIC, q["scale"][:, g:g + 1], ALU.add,
                                        ALU.mult).then_inc(done, 1)

            for g in range(8, 20):
                dequant(st, qs[0], g, (s["q_clip"], g + 1), s["q_deq"])
            rstd(1)
            pool.wait_ge(s["w_act"], 2)
            for a in range(2):
                ins = nc.gpsimd.tensor_copy(wqR[:, :, 64 * a:64 * a + 64],
                                            wqT[:, :, 64 - 64 * a:128 - 64 * a].bitcast(F32))
            ins.then_inc(s["w_rot"], 1)
            rstd(2)
            for c in range(2):
                normalise(2 * HP0, c, 4, P)
            rstd(3)
            rstd(4, rs2)
            for n in range(32):
                g = KV_ORDER[n]
                dequant(st, qs[0], g, (s["q_clip"], 20 + n + 1), s["q_deq"])

            def rotate_add(hp):
                for hh in range(2):
                    for c in range(2):
                        n = 4 * hp + 2 * hh + c
                        pool.wait_ge(s["r_q1"], n + 1)
                        pool.wait_ge(s["r_q2"], n + 1)
                        if hp > 0:
                            pool.wait_ge(s["a_scores"], 2 * HP0 + 2 + 2 * hp)
                        nc.gpsimd.tensor_tensor(qbd[:, 8 * c:8 * c + 8, hh, :],
                                                q1s[:, n % 2, :].rearrange("p (b q) -> p b q", q=S),
                                                q2s[:, n % 2, :].rearrange("p (b q) -> p b q", q=S),
                                                ALU.add).then_inc(s["r_q"], 1)

            rotate_add(0)
            for hp in range(HP1):
                for c in range(2):
                    normalise(2 * HP0 + 2 + 2 * hp, c, 8, S)
                if hp + 1 < HP1:
                    rotate_add(hp + 1)

            def clip_pair(p, a, b):
                q, w = qs[1 - p % 2], stB if p % 2 == 0 else st
                for g in range(a, b):
                    pool.wait_ge(s["m_round"], 21 * p + g + 1)
                    nc.gpsimd.tensor_scalar(w[:, g, :], w[:, g, :], q["hi"][:, g:g + 1], q["lo"][:, g:g + 1],
                                            ALU.min, ALU.max).then_inc(s["m_clip"], 1)
                    if g < MT:
                        dequant(w, q, g, (s["m_clip"], 21 * p + g + 1), s["m_deq"])

            def add_up(p, e):
                for c in range(2):
                    n = 4 * p + 2 * e + c
                    pool.wait_ge(s["m_gy"], n + 1)
                    pool.wait_ge(s["m_acc"], n + 1)
                    nc.gpsimd.tensor_tensor(macc[:, 512 * c:512 * c + 512], macc[:, 512 * c:512 * c + 512],
                                            hid1[:, c, :], ALU.add).then_inc(s["m_acc"], 1)

            clip_pair(0, 0, 21)
            rstd(5)
            nc.gpsimd.memset(macc, 0.0).then_inc(s["m_acc"], 1)
            for p in range(PAIRS):
                add_up(p, 0)
                if p + 1 < PAIRS:
                    clip_pair(p + 1, 0, 21)
                add_up(p, 1)

        @block.scalar
        def _(sc):
            sc.wait_ge(s["ctx_in"], 16)
            nc.scalar.activation(ch[:], cT[:], ACT.Copy).then_inc(s["hi_set"], 1)
            sc.wait_ge(s["vec_in"], 16)
            nc.scalar.activation(wg_h[:], vec[:, V_WG0:V_WG0 + 2 * E], ACT.Copy).then_inc(s["hi_set"], 1)
            nc.scalar.activation(tg[:], vec[:, V_GX:V_GX + 4], ACT.Tanh).then_inc(s["tanh_done"], 1)
            sc.wait_ge(s["w0_in"], 16)
            nc.scalar.activation(w_h[:], wst[:, 0:3 * P], ACT.Copy).then_inc(s["a_w_h"], 1)

            def turn_hi(k, scale=1.0):
                for c in range(2):
                    sc.wait_ge(s["turned"], 2 * k + c + 1)
                    nc.scalar.activation(xh[:, 512 * c:512 * c + 512], bank(4 + c), ACT.Copy,
                                         scale=scale).then_inc(s["xh_ready"], 1)

            def exps(n, scale):
                for c in range(2):
                    sc.wait_ge(s["a_sub"], n + c + 1)
                    nc.scalar.activation(prob[:, c, :], prob[:, c, :], ACT.Exp, scale=scale).then_inc(s["a_exp"], 1)

            def attT_copy(n):
                sc.wait_ge(s["a_attT"], 2 * n + 1)
                nc.scalar.activation(attT[:, 0:4, :], bank(4).rearrange("p (t q) -> p t q", q=P),
                                     ACT.Copy).then_inc(s["a_attT_act"], 1)

            def queries_in(n):
                sc.wait_ge(s["a_proj"], n)
                for h in range(2):
                    r = slice(64 * h, 64 * h + 64)
                    ins = nc.scalar.activation(qbd[r, 0:8, h, :], ps[r, 2, :].rearrange("p (b q) -> p b q", q=S),
                                               ACT.Identity, bias=wst[r, 3 * P:3 * P + 1])
                ins.then_inc(s["a_act"], 1)

            def keys_in(n):
                sc.wait_ge(s["a_proj"], n)
                nc.scalar.activation(kT[:, 0, 0:512], bank(2), ACT.Identity,
                                     bias=wst[:, 3 * P + 1:3 * P + 2]).then_inc(s["a_act"], 1)

            turn_hi(0)
            sc.wait_ge(s["pool_set"], 1)
            queries_in(1)
            keys_in(3)

            def pair_step(j, first, last):
                sc.wait_ge(s["w0_in"], 16 * j + 32)
                sc.wait_ge(s["a_proj"], 6 * j + 4)
                nc.scalar.activation(w_h[:], wst[:, 0:3 * P], ACT.Copy).then_inc(s["a_w_h"], 1)
                if not first:
                    attT_copy(j - 1)
                exps(2 * j, 0.125)
                if not first:
                    sc.wait_ge(s["a_out"], 2 * j - 1)
                    nc.scalar.activation(of_batches(big[:, bass.ds(j - 1, 1), :], 0), ps[:, 6:7, :].rearrange(
                        "p a (t q) -> p a t q", q=S), ACT.Copy).then_inc(s["a_out_act"], 1)
                sc.wait_ge(s["a_proj"], 6 * j + 5)
                nc.scalar.activation(v_sb[:, 0:4, :], bank(2).rearrange("p (t d) -> p t d", d=P),
                                     ACT.Copy).then_inc(s["a_act"], 1)
                if not last:
                    queries_in(6 * j + 7)
                    keys_in(6 * j + 9)

            pair_step(0, True, False)
            with sc.Fori(1, HP0 - 1) as j:
                pair_step(j, False, False)
            pair_step(HP0 - 1, False, True)
            attT_copy(HP0 - 1)
            sc.wait_ge(s["a_out"], 2 * HP0 - 1)
            nc.scalar.activation(of_batches(big[:, HP0 - 1:HP0, :], 0), ps[:, 6:7, :].rearrange(
                "p a (t q) -> p a t q", q=S), ACT.Copy).then_inc(s["a_out_act"], 1)

            def y_first(k, n_ready, src, bias=None):
                sc.wait_ge(s["y_ready"], n_ready)
                if bias is None:
                    nc.scalar.activation(yT[:, 0:512], src, ACT.Copy).then_inc(s["yT_act"], 1)
                else:
                    nc.scalar.activation(yT[:, 0:512], src, ACT.Identity, bias=bias).then_inc(s["yT_act"], 1)

            def rounds(w, q, a, b, done):
                for g in range(a, b):
                    nc.scalar.activation(w[:, g, :], w[:, g, :], ACT.Identity, scale=q["recip"][:, g:g + 1],
                                         bias=magic[:]).then_inc(done, 1)

            sc.wait_ge(s["q_stats"], 1)
            rounds(st, qs[0], 0, 20, s["q_round"])
            sc.wait_ge(s["yc_ready"], 1)
            y_first(0, 1, bank(0), yc[:])
            for n in range(2):
                sc.wait_ge(s["w_turn"], n + 1)
                nc.scalar.activation(wqT[:, 4 * n:4 * n + 4, :], bank(6 + n).rearrange("p (t d) -> p t d", d=P),
                                     ACT.Copy, bias=-MAGIC).then_inc(s["w_act"], 1)
            sc.wait_ge(s["w_turn"], 3)
            nc.scalar.activation(wkv_h[:], bank(0), ACT.Copy).then_inc(s["w_act"], 1)
            for n in range(2):
                sc.wait_ge(s["w_turn"], 4 + n)
                nc.scalar.activation(woT[:, 4 * n:4 * n + 4, :],
                                     bank(1 + 5 * n).rearrange("p (t d) -> p t d", d=P),
                                     ACT.Copy).then_inc(s["w_act"], 1)

            sc.wait_ge(s["gu_in"], 16)
            nc.scalar.activation(gu_h[:, 0, :], gu_st[:], ACT.Copy).then_inc(s["f_w_h"], 1)
            turn_hi(1)
            sc.wait_ge(s["g_sub"], 1)
            nc.scalar.activation(gp[:], gp[:], ACT.Exp).then_inc(s["g_exp"], 1)

            def gate_rows(k):
                for c in range(2):
                    sc.wait_ge(s["gT"], 2 * k + c + 1)
                    nc.scalar.activation(g_h[:, 512 * c:512 * c + 512], ps[0:E, 4 + c, :],
                                         ACT.Copy).then_inc(s["g_h_ready"], 1)

            def expert_step(m, par, first, last):
                if not last:
                    sc.wait_ge(s["gu_in"], 16 * m + 32)
                    if not first:
                        sc.wait_ge(s["f_gu"], 2 * m)
                    nc.scalar.activation(gu_h[:, 1 - par, :], gu_st[:], ACT.Copy).then_inc(s["f_w_h"], 1)
                for c in range(2):
                    sc.wait_ge(s["f_gu"], 2 * m + c + 1)
                    if not first:
                        sc.wait_ge(s["f_h1"], 2 * m + c - 1)
                    nc.scalar.activation(act[:, c, :], bank(c), ACT.Silu).then_inc(s["f_act"], 1)

            expert_step(0, 0, True, False)
            gate_rows(0)
            with sc.Fori(1, M0 - 2, 2) as m:
                expert_step(m, 1, False, False)
                expert_step(m + 1, 0, False, False)
            expert_step(M0 - 2, 1, False, False)
            expert_step(M0 - 1, 0, False, True)
            sc.wait_ge(s["f_down"], 2 * M0 - 1)
            nc.scalar.activation(yT[:, 0:512], bank(6), ACT.Copy).then_inc(s["yT_act"], 1)

            sc.wait_ge(s["wx_in"], 16)
            nc.scalar.activation(wx_h[:], wx_st[:], ACT.Copy).then_inc(s["hi_set"], 1)
            turn_hi(2)
            sc.wait_ge(s["x_proj"], 1)
            nc.scalar.activation(kT[:, 1, 0:512], bank(0), ACT.Identity,
                                 bias=vec[:, V_BQ:V_BQ + 1]).then_inc(s["x_act"], 1)
            sc.wait_ge(s["x_proj"], 3)
            nc.scalar.activation(kT[:, 0, 0:512], bank(2), ACT.Identity,
                                 bias=vec[:, V_BK:V_BK + 1]).then_inc(s["x_act"], 1)
            sc.wait_ge(s["x_proj"], 5)
            nc.scalar.activation(v_sb[:, 0:4, :], bank(6).rearrange("p (t d) -> p t d", d=P),
                                 ACT.Copy).then_inc(s["x_act"], 1)
            exps(2 * HP0, 1.0)
            attT_copy(HP0)
            sc.wait_ge(s["a_out"], 2 * HP0 + 1)
            nc.scalar.activation(yT[:, 0:512], bank(6), ACT.Identity,
                                 bias=vec[:, V_BV:V_BV + 1]).then_inc(s["yT_act"], 1)

            turn_hi(3, vec[:, V_G1:V_G1 + 1])
            for n in range(32):
                g = KV_ORDER[n]
                if n % 16 == 0:
                    sc.wait_ge(s["q_stats"], 2 + n // 16)
                nc.scalar.activation(st[:, g, :], ps[:, g // 4, P * (g % 4):P * (g % 4) + P], ACT.Identity,
                                     scale=qs[0]["recip"][:, g:g + 1], bias=magic[:]).then_inc(s["q_round"], 1)
            for n in (0, 2):
                sc.wait_ge(s["k_turn"], n + 1)
                nc.scalar.activation(kT[:, n // 2, 0:512], bank(4), ACT.Copy).then_inc(s["k_act"], 1)

            def attT_both(h):
                for c in range(2):
                    sc.wait_ge(s["a_attT"], 2 * (HP0 + 1 + h) + c + 1)
                    nc.scalar.activation(attT[:, 4 * c:4 * c + 4, :], bank(4 + c).rearrange("p (t q) -> p t q", q=P),
                                         ACT.Copy).then_inc(s["a_attT_act"], 1)

            def outputs(h):
                for q in range(2):
                    for b in range(2):
                        sc.wait_ge(s["a_out"], O_L1 + 4 * h + 2 * q + b + 1)
                        nc.scalar.activation(
                            of_batches(big[:, 2 * h:2 * h + 2, 512 * q:512 * q + 512], b).rearrange(
                                "p a t q -> p t a q"),
                            bank(6 + b).rearrange("p (t a q) -> p t a q", a=2, q=S),
                            ACT.Copy).then_inc(s["a_out_act"], 1)

            for hp in range(HP1):
                if hp > 0:
                    attT_both(hp - 1)
                exps(2 * HP0 + 2 + 2 * hp, float(P) ** -0.5)
                if hp > 0:
                    outputs(hp - 1)
                if hp == HP1 - 1:
                    sc.wait_ge(s["m_stats"], 2)
                    rounds(stB, qs[1], 0, 11, s["m_round"])
            attT_both(HP1 - 1)
            outputs(HP1 - 1)
            rounds(stB, qs[1], 11, 21, s["m_round"])
            y_first(3, 3, bank(0))

            def aux_out(*key):
                n = AUX[key]
                src = bank(AUX_BANK[n])
                sc.wait_ge(s["aux_ps"], n + 1)
                if key[0] == "w13":
                    t0, k = 4 * key[2], min(4, 2 * MT - 4 * key[2])
                    nc.scalar.activation(w13T[:, t0:t0 + k, :], src[:, 0:k * P].rearrange("p (t d) -> p t d", d=P),
                                         ACT.Copy, bias=-MAGIC).then_inc(s["aux_act"], 1)
                elif key[0] == "w2":
                    t0, k = 4 * key[2], min(4, MT - 4 * key[2])
                    nc.scalar.activation(w2T[:, t0:t0 + k, :].rearrange("p t (r c) -> p t c r", c=2),
                                         src[:, 0:k * P].rearrange("p (t c r) -> p t c r", c=2, r=64),
                                         ACT.Copy).then_inc(s["aux_act"], 1)
                else:
                    e, c = key[2], key[3]
                    nc.scalar.activation(big[:, 2 * key[1] + e, 512 * c:512 * c + 512], src, ACT.Copy).then_inc(s["aux_act"], 1)

            for key in AUX_FIRST:
                aux_out(*key)
            turn_hi(4, vec[:, V_G2:V_G2 + 1])
            sc.wait_ge(s["g_sub"], 2)
            nc.scalar.activation(gp[:], gp[:], ACT.Exp).then_inc(s["g_exp"], 1)
            gate_rows(1)
            for p in range(PAIRS):
                q = qs[1 - p % 2]
                for m in range(MT):
                    for c in range(2):
                        n = 2 * (MT * p + m) + c
                        sc.wait_ge(s["m_gu"], n + 1)
                        if n >= 2:
                            sc.wait_ge(s["m_up"], n - 1)
                        g = MT + 2 * m
                        nc.scalar.activation(act[:, c, :], bank(c), ACT.Silu,
                                             scale=q["scale"][:, g:g + 1]).then_inc(s["m_act"], 1)
                        a, b = ROUND_SLOTS[2 * m + c]
                        if b > a and p + 1 < PAIRS:
                            sc.wait_ge(s["m_stats"], 2 * (p + 1) + (1 if a < 11 else 2))
                            rounds(stB if p % 2 else st, qs[p % 2], a, b, s["m_round"])
                    for key in AUX_AT.get((p, m), ()):
                        aux_out(*key)

        @block.tensor
        def _(pe):
            T = nc.tensor

            def turn_norm(k):
                for c in range(2):
                    pe.wait_ge(s["nrm_ready"], 2 * (k if k < 3 else k + 1) + c + 1)
                    for t in range(4):
                        ins = T.transpose(ps[:, 4 + c, P * t:P * t + P], nrm[:, 4 * c + t, :], ident)
                    ins.then_inc(s["turned"], 1)

            def turn_back(k, src=None):
                src = yT if src is None else src
                for c in range(2):
                    if k < 4:
                        pe.wait_ge(s["yT_act" if c == 0 else "yT_dve"], k + 1)
                    for t in range(4):
                        o = 512 * c + P * t
                        ins = T.transpose(ps[:, 2 + c, P * t:P * t + P], src[:, o:o + P], ident)
                    ins.then_inc(s["back"], 1)

            def project(i, out_bank, w0, src_h, src_l, c):
                return mm3(bank(out_bank), w_h[:, w0:w0 + P], w_l[:, w0:w0 + P],
                           src_h[:, 512 * c:512 * c + 512], src_l[:, 512 * c:512 * c + 512])

            def q_and_k(j, first):
                for n, (w0, a_h, a_l) in enumerate(((0, xh, xl), (P, ch, cl))):
                    for c in range(2):
                        if not (first and n == 0):
                            pe.wait_ge(s["a_act" if c == 0 else "a_dve"], 1 if first else 3 * j + n)
                        project(0, 2 + c, w0, a_h, a_l, c).then_inc(s["a_proj"], 1)

            pe.wait_ge(s["cst_in"], 16)
            turn_norm(0)
            pe.wait_ge(s["lo_set"], 2)
            pe.wait_ge(s["a_w_l"], 1)
            pe.wait_ge(s["xl_ready"], 2)
            q_and_k(0, True)

            def scores(n, lhs, rhs, mask, nb, w):
                for c in range(2):
                    pe.wait_ge(s["a_sub"], n + c - 1) if not (isinstance(n, int) and n == 0) else None
                    T.matmul(bank(c), idb[:], mask.unsqueeze(1).to_broadcast([P, nb, w]), start=True, stop=False,
                             skip_group_check=True)
                    for b in range(nb):
                        ins = T.matmul(ps[:, c, w * b:w * b + w], lhs(nb * c + b), rhs(nb * c + b), start=False,
                                       stop=True, skip_group_check=True)
                    ins.then_inc(s["a_scores"], 1)

            def turn_probs(n, gaps=True):
                for c in range(2):
                    pe.wait_ge(s["a_norm"], 2 * n + c + 1)
                    for t in range(4):
                        ins = T.transpose(ps[:, 4 + c, P * t:P * t + P], prob[:, c, P * t:P * t + P], ident)
                    ins.then_inc(s["a_attT"], 1)

            def values0(j, first):
                for c in range(2):
                    pe.wait_ge(s["a_attT_act" if c == 0 else "a_attT_dve"], j + 1)
                    pe.wait_ge(s["a_act" if c == 0 else "a_dve"], 3 * j + 3)
                    if c == 0 and not first:
                        pe.wait_ge(s["a_out_act"], j)
                        pe.wait_ge(s["a_out_dve"], j)
                    for t in range(4 * c, 4 * c + 4):
                        for b in range(2):
                            r = slice(64 * b, 64 * b + 64)
                            o = slice(S * t, S * t + S)
                            if t == 4 * c and b == 0:
                                T.matmul(ps[:, 6, o], v_sb[r, t, :], attT[r, t, 0:64], start=True, stop=True,
                                         skip_group_check=True)
                            else:
                                T.matmul(ps[0:64, 6 + b, o], v_sb[r, t, 0:64], attT[r, t, 0:64], start=True,
                                         stop=True, skip_group_check=True)
                            ins = T.matmul(ps[64:128, 6 + b, o], v_sb[r, t, 64:128], attT[r, t, 64:128],
                                           start=True, stop=True, skip_group_check=True)
                            if t == NT - 1:
                                ins.then_inc(s["a_out"], 1)

            def pair_step(j, first, last):
                if not first:
                    turn_probs(j - 1)
                pe.wait_ge(s["a_act"], 3 * j + 2)
                pe.wait_ge(s["a_dve"], 3 * j + 2)
                scores(2 * j if not first else 0, lambda b: qbd[:, b, :, :], lambda b: kT[:, 0, S * b:S * b + S],
                       caub[:], 8, S)
                if not first:
                    values0(j - 1, first=False)
                pe.wait_ge(s["a_w_l"], j + 2)
                for c in range(2):
                    pe.wait_ge(s["a_act" if c == 0 else "a_dve"], 3 * j + 2)
                    for t in range(4):
                        o = 512 * c + P * t
                        ins = mm3(ps[:, 2 + c, P * t:P * t + P], ch[:, o:o + P], cl[:, o:o + P],
                                  w_h[:, 2 * P:3 * P], w_l[:, 2 * P:3 * P])
                    ins.then_inc(s["a_proj"], 1)
                if not last:
                    q_and_k_next(j)

            def q_and_k_next(j):
                for n, (w0, a_h, a_l) in enumerate(((0, xh, xl), (P, ch, cl))):
                    for c in range(2):
                        pe.wait_ge(s["a_act" if c == 0 else "a_dve"], 3 * j + 3 + n)
                        project(0, 2 + c, w0, a_h, a_l, c).then_inc(s["a_proj"], 1)

            pe.wait_ge(s["dve_set"], 1)
            pair_step(0, True, False)
            with pe.Fori(1, HP0 - 1) as j:
                pair_step(j, False, False)
            pair_step(HP0 - 1, False, True)
            turn_probs(HP0 - 1)
            values0(HP0 - 1, False)

            pe.wait_ge(s["wo0_in"], 16)
            for j in range(HP0):
                ins = T.matmul(ps[:, 2, 0:1], wo0[:, j, :], vec[:, V_BV0 + j:V_BV0 + j + 1], start=(j == 0),
                               stop=(j == HP0 - 1))
            ins.then_inc(s["yc_ps"], 1)
            pe.wait_ge(s["a_out_act"], HP0)
            pe.wait_ge(s["a_out_dve"], HP0)
            for c in range(2):
                for j in range(HP0):
                    ins = T.matmul(bank(c), wo0[:, j, :], big[:, j, 512 * c:512 * c + 512], start=(j == 0),
                                   stop=(j == HP0 - 1))
                ins.then_inc(s["y_ready"], 1)

            def turn_own(n, b):
                for t in range(4):
                    g = 4 * n + t
                    pe.wait_ge(s["q_clip" if g < 8 else "q_deq"], g + 1 if g < 8 else g - 7)
                    ins = T.transpose(ps[:, b, P * t:P * t + P], st[:, g, :], ident)
                ins.then_inc(s["w_turn"], 1)

            turn_own(0, 6)
            turn_own(1, 7)
            turn_back(0)
            turn_own(2, 0)
            turn_own(3, 1)
            pe.wait_ge(s["w_act"], 1)
            turn_own(4, 6)

            def gate_logits(k):
                pe.wait_ge(s["xl_ready"], 2 * (4 if k else 1) + 2)
                for t in range(NT):
                    ins = mm3(ps[:, 6, E * t:E * t + E], xh[:, P * t:P * t + P], xl[:, P * t:P * t + P],
                              wg_h[:, E * k:E * k + E], wg_l[:, E * k:E * k + E])
                ins.then_inc(s["logits"], 1)

            def gates_turned(k):
                pe.wait_ge(s["gates"], k + 1)
                for c in range(2):
                    for t in range(4):
                        ins = T.transpose(ps[0:E, 4 + c, P * t:P * t + P], lg[:, 4 * c + t, :], ident)
                    ins.then_inc(s["gT"], 1)

            def gate_up(m, par, c, first):
                pe.wait_ge(s["f_w_l"], m + 1)
                if not first:
                    pe.wait_ge(s["f_act"], 2 * m + c - 1)
                    pe.wait_ge(s["f_h1"], 2 * m + c - 1)
                x0, x1 = xh[:, 512 * c:512 * c + 512], xl[:, 512 * c:512 * c + 512]
                mm3(bank(c), gu_h[:, par, 0:P], gu_l[:, par, 0:P], x0, x1)
                mm3(bank(2 + c), gu_h[:, par, P:2 * P], gu_l[:, par, P:2 * P], x0, x1).then_inc(s["f_gu"], 1)

            def expert_step(m, par, first, last):
                pe.wait_ge(s["f_sel"], m + 1)
                for c in range(2):
                    if not first:
                        pe.wait_ge(s["f_hid"], 2 * m + c - 1)
                    mm2(bank(4 + c), selr0[:], g_h[:, 512 * c:512 * c + 512],
                        g_l[:, 512 * c:512 * c + 512]).then_inc(s["f_gate"], 1)
                pe.wait_ge(s[f"d_in{par}"], 8 * m + 16 - 8 * par)
                for c in range(2):
                    if not last:
                        gate_up(m + 1, 1 - par, c, False)
                    pe.wait_ge(s["f_hid"], 2 * m + c + 1)
                    T.matmul(bank(6 + c), d_st[:, par, :], hid[:, c, :], start=first, stop=last,
                             skip_group_check=True).then_inc(s["f_down"], 1)

            turn_norm(1)
            pe.wait_ge(s["w_act"], 5)
            pe.wait_ge(s["w_dve"], 1)
            gate_logits(0)
            gate_up(0, 0, 0, True)
            gate_up(0, 0, 1, True)
            gates_turned(0)
            pe.wait_ge(s["g_h_ready"], 2)
            pe.wait_ge(s["g_l_ready"], 2)
            expert_step(0, 0, True, False)
            with pe.Fori(1, M0 - 2, 2) as m:
                expert_step(m, 1, False, False)
                expert_step(m + 1, 0, False, False)
            expert_step(M0 - 2, 1, False, False)
            expert_step(M0 - 1, 0, False, True)
            turn_back(1)

            turn_norm(2)
            pe.wait_ge(s["xl_ready"], 6)
            pe.wait_ge(s["lo_set"], 3)
            for n, (w0, a_h, a_l) in enumerate(((0, xh, xl), (P, ch, cl))):
                for c in range(2):
                    mm3(bank(2 * n + c), wx_h[:, w0:w0 + P], wx_l[:, w0:w0 + P], a_h[:, 512 * c:512 * c + 512],
                        a_l[:, 512 * c:512 * c + 512]).then_inc(s["x_proj"], 1)
            for c in range(2):
                for t in range(4):
                    o = 512 * c + P * t
                    ins = mm3(ps[:, 6 + c, P * t:P * t + P], ch[:, o:o + P], cl[:, o:o + P], wx_h[:, 2 * P:3 * P],
                              wx_l[:, 2 * P:3 * P])
                ins.then_inc(s["x_proj"], 1)
            pe.wait_ge(s["x_act"], 2)
            pe.wait_ge(s["x_dve"], 2)
            scores(2 * HP0, lambda b: kT[:, 1, P * b:P * b + P], lambda b: kT[:, 0, P * b:P * b + P], blkb[:], 4, P)
            turn_probs(HP0)
            for c in range(2):
                pe.wait_ge(s["a_attT_act" if c == 0 else "a_attT_dve"], HP0 + 1)
                pe.wait_ge(s["x_act" if c == 0 else "x_dve"], 3)
                for t in range(4):
                    ins = T.matmul(ps[:, 6 + c, P * t:P * t + P], v_sb[:, 4 * c + t, :], attT[:, 4 * c + t, :],
                                   start=True, stop=True, skip_group_check=True)
                ins.then_inc(s["a_out"], 1)
            turn_back(2)

            turn_norm(3)
            pe.wait_ge(s["xl_ready"], 8)
            for t in range(NT):
                mm3(bank(t), xh[:, P * t:P * t + P], xl[:, P * t:P * t + P], wkv_h[:],
                    wkv_l[:]).then_inc(s["kv_ps"], 1)

            def rotate(hp, i):
                n = 4 * hp + i
                hh, c = i // 2, i % 2
                x0, x1 = xh[:, 512 * c:512 * c + 512], xl[:, 512 * c:512 * c + 512]
                if n >= 1:
                    pe.wait_ge(s["r_q1"], n)
                mm2(bank(2), wqT[:, 2 * hp + hh, :], x0, x1).then_inc(s["r_ps"], 1)
                if n >= 1:
                    pe.wait_ge(s["r_q2"], n)
                mm2(bank(3), wqR[:, 2 * hp + hh, :], x0, x1).then_inc(s["r_ps"], 1)

            pe.wait_ge(s["w_rot"], 1)
            pe.wait_ge(s["q_round"], 20 + 16)
            for i in range(4):
                rotate(0, i)
            pe.wait_ge(s["q_round"], 20 + 32)
            for n in range(4):
                if n >= 2:
                    pe.wait_ge(s["k_act" if n % 2 == 0 else "k_dve"], 1)
                pe.wait_ge(s["k_rope"], 2)
                for t in range(4):
                    tt = 4 * (n % 2) + t
                    o = P * t
                    T.matmul(ps[:, 4 + n % 2, o:o + P], st[:, 4 * tt + n // 2, :], ident, start=True, stop=False,
                             skip_group_check=True)
                    ins = T.matmul(ps[:, 4 + n % 2, o:o + P], big[:, n // 2, P * tt:P * tt + P], ident, start=False,
                                   stop=True, skip_group_check=True)
                ins.then_inc(s["k_turn"], 1)
            pe.wait_ge(s["k_act"], 2)
            pe.wait_ge(s["k_dve"], 2)

            def values1(hp, i):
                q = i // 2
                if i == 0:
                    pe.wait_ge(s["a_attT_act"], HP0 + 1 + 2 * hp + 2)
                    pe.wait_ge(s["q_deq"], 12 + 32)
                if i % 2 == 0 and (hp > 0 or q > 0):
                    pe.wait_ge(s["a_out_act"], HP0 + 2 * (2 * hp + q))
                for t in range(2 * (i % 2), 2 * (i % 2) + 2):
                    for b in range(2):
                        r = slice(64 * b, 64 * b + 64)
                        ins = T.matmul(ps[:, 6 + b, P * t:P * t + P], st[r, 4 * (4 * q + t) + 2 + hp // 2, :],
                                       attT[r, 4 * q + t, :], start=True, stop=True, skip_group_check=True)
                        if t == 3:
                            ins.then_inc(s["a_out"], 1)

            for hp in range(HP1):
                if hp > 0:
                    turn_probs(HP0 + hp)
                pe.wait_ge(s["r_q"], 4 * hp + 4)
                scores(2 * HP0 + 2 + 2 * hp, lambda b: qbd[:, b, :, :],
                       lambda b, hp=hp: kT[:, hp // 2, S * b:S * b + S], caub[:], 8, S)
                for i in range(4):
                    if hp + 1 < HP1:
                        rotate(hp + 1, i)
                    if hp > 0:
                        values1(hp - 1, i)
            turn_probs(HP0 + HP1)
            for i in range(4):
                values1(HP1 - 1, i)
            pe.wait_ge(s["a_out_act"], HP0 + 4 * HP1)
            for c in range(2):
                for h in range(2 * HP1):
                    ins = T.matmul(bank(c), woT[:, h, :], big[:, h, 512 * c:512 * c + 512], start=(h == 0),
                                   stop=(h == 2 * HP1 - 1))
                ins.then_inc(s["y_ready"], 1)

            def aux(*key):
                n = AUX[key]
                b, before = AUX_BANK[n], [k for k in range(n) if AUX_BANK[k] == AUX_BANK[n]]
                if before:
                    pe.wait_ge(s["aux_act"], before[-1] + 1)
                p = key[1]
                w = stB if p % 2 == 0 else st
                if key[0] == "w13":
                    for g in range(MT + 4 * key[2], min(MT + 4 * key[2] + 4, 21)):
                        pe.wait_ge(s["m_clip"], 21 * p + g + 1)
                        o = P * (g - MT - 4 * key[2])
                        ins = T.transpose(ps[:, b, o:o + P], w[:, g, :], ident)
                elif key[0] == "w2":
                    pe.wait_ge(s["m_deq"], MT * (p + 1))
                    w2 = w[:, 0:MT, :].rearrange("p g d -> p (g d)")
                    for m in range(4 * key[2], min(4 * key[2] + 4, MT)):
                        for r in range(2):
                            o = P * (m - 4 * key[2]) + 64 * r
                            if m == 3:
                                T.matmul(ps[0:64, b, o:o + 64], w2[0:64, 448 * r + 384:448 * r + 448],
                                         ident[0:64, 0:64], start=True, stop=True, skip_group_check=True)
                                ins = T.matmul(ps[64:128, b, o:o + 64], w2[64:128, 448 * r:448 * r + 64],
                                               ident[64:128, 64:128], start=True, stop=True, skip_group_check=True)
                            else:
                                e, f = (0, P * m) if m < 3 else (64, P * (m - 4) + 64)
                                ins = T.transpose(ps[:, b, o:o + 64], w2[e:e + 64, 448 * r + f:448 * r + f + P],
                                                  ident[e:e + 64, e:e + 64])
                else:
                    e, c = key[2], key[3]
                    if key == ("gate", 0, 0, 0):
                        pe.wait_ge(s["g_h_ready"], 4)
                        pe.wait_ge(s["g_l_ready"], 4)
                        pe.wait_ge(s["selr"], 1)
                    k = P * (2 * p + e)
                    ins = mm2(bank(b), selr1[:, k:k + P], g_h[:, 512 * c:512 * c + 512],
                              g_l[:, 512 * c:512 * c + 512])
                ins.then_inc(s["aux_ps"], 1)

            for key in AUX_FIRST[:2]:
                aux(*key)
            turn_back(3)
            for key in AUX_FIRST[2:]:
                aux(*key)
            turn_norm(4)
            pe.wait_ge(s["aux_act"], len(AUX_FIRST))
            gate_logits(1)

            def m_gate_up(p, m, c):
                n = 2 * (MT * p + m) + c
                if n >= 2:
                    pe.wait_ge(s["m_act"], n - 1)
                    pe.wait_ge(s["m_up"], n - 1)
                if c == 0 and m % 2 == 0:
                    pe.wait_ge(s["aux_act"], AUX[("w13", p, m // 2)] + 1)
                x0, x1 = xh[:, 512 * c:512 * c + 512], xl[:, 512 * c:512 * c + 512]
                mm2(bank(c), w13T[:, 2 * m, :], x0, x1)
                mm2(bank(2 + c), w13T[:, 2 * m + 1, :], x0, x1).then_inc(s["m_gu"], 1)

            def m_down(p, m, e, c):
                r = slice(0, P) if m != 3 else (slice(0, 64) if e == 0 else slice(64, 128))
                lo, hi = (0, 3) if e == 0 else (3, 6)
                n = 2 * (MT * p + m) + c
                pe.wait_ge(s["m_up"], n + 1)
                if m % 4 == 0:
                    pe.wait_ge(s["aux_act"], AUX[("w2", p, m // 4)] + 1)
                if m == lo and (p, e) != (0, 0):
                    pe.wait_ge(s["m_gy"], 4 * p + 2 * e + c - 1)
                T.matmul(bank(6 + c), w2T[r, m, :], hid[r, c, :], start=(m == lo), stop=(m == hi),
                         skip_group_check=True).then_inc(s["m_down"], 1)

            m_gate_up(0, 0, 0)
            m_gate_up(0, 0, 1)
            gates_turned(1)
            for p in range(PAIRS):
                for m in range(MT):
                    for c in range(2):
                        if m + 1 < MT:
                            m_gate_up(p, m + 1, c)
                        elif p + 1 < PAIRS:
                            m_gate_up(p + 1, 0, c)
                        if m <= 3:
                            m_down(p, m, 0, c)
                        if m > 3:
                            m_down(p, m, 1, c)
                    if m == 3:
                        m_down(p, m, 1, 0)
                        m_down(p, m, 1, 1)
                    for key in AUX_AT.get((p, m), ()):
                        aux(*key)
            pe.wait_ge(s["m_acc"], 1 + 4 * PAIRS)
            turn_back(4, macc)

        @block.vector
        def _(dve):
            V = nc.vector
            steps = [0]

            def step(ins):
                steps[0] += 1
                ins.then_inc(s["dve_step"], 1)
                dve.wait_ge(s["dve_step"], steps[0])

            dve.wait_ge(s["x_in"], 16)

            def norm(k, src, dst, rms, pre=None):
                for c in range(2):
                    if pre is not None:
                        step(pre(c))
                    h = slice(4 * c, 4 * c + 4)
                    for t in range(4 * c, 4 * c + 4):
                        ins = V.bn_stats(bst[:, t, :], src[:, t, :])
                    step(ins)
                    for t in range(4 * c, 4 * c + 4):
                        ins = V.bn_aggr(bmv[:, t, :], bst[:, t, :])
                    step(ins)
                    if rms:
                        step(V.tensor_tensor(ve[:, h], bmv[:, h, 0], bmv[:, h, 0], ALU.mult))
                        V.scalar_tensor_tensor(ve[:, h], ve[:, h], LN_EPS, bmv[:, h, 1], ALU.add,
                                               ALU.add).then_inc(s["ve_ready"], 1)
                    else:
                        V.tensor_scalar(ve[:, h], bmv[:, h, 1], LN_EPS, None, ALU.add).then_inc(s["ve_ready"], 1)
                for c in range(2):
                    dve.wait_ge(s["rstd_ready"], 2 * k + c + 1)
                    for t in range(4 * c, 4 * c + 4):
                        if rms:
                            ins = V.tensor_scalar(dst[:, t, :], src[:, t, :], rs[:, t:t + 1], None, ALU.mult)
                        else:
                            ins = V.tensor_scalar(dst[:, t, :], src[:, t, :], bmv[:, t, 0:1], rs[:, t:t + 1],
                                                  ALU.subtract, ALU.mult)
                    ins.then_inc(s["nrm_ready"], 1)

            def turn_lo(k, gain=None):
                for c in range(2):
                    dve.wait_ge(s["xh_ready"], 2 * k + c + 1)
                    o = slice(512 * c, 512 * c + 512)
                    V.scalar_tensor_tensor(xl[:, o], bank(4 + c), 1.0 if gain is None else gain,
                                           xh[:, o].bitcast(F32), ALU.mult, ALU.subtract).then_inc(s["xl_ready"], 1)

            norm(0, x_tok, nrm, False)
            dve.wait_ge(s["cst_in"], 16)
            V.tensor_copy(idb[:], ident)
            V.tensor_copy(caub[:], cst[:, C_CAU:C_CAU + S])
            V.tensor_copy(blkb[:], cst[:, C_BLK:C_BLK + P]).then_inc(s["dve_set"], 1)
            dve.wait_ge(s["hi_set"], 1)
            V.tensor_tensor(cl[:], cT[:], ch[:].bitcast(F32), ALU.subtract).then_inc(s["lo_set"], 1)
            dve.wait_ge(s["hi_set"], 2)
            V.tensor_tensor(wg_l[:], vec[:, V_WG0:V_WG0 + 2 * E], wg_h[:].bitcast(F32),
                            ALU.subtract).then_inc(s["lo_set"], 1)

            def w_lo(n):
                dve.wait_ge(s["a_w_h"], n)
                V.tensor_tensor(w_l[:], wst[:, 0:3 * P], w_h[:].bitcast(F32), ALU.subtract).then_inc(s["a_w_l"], 1)

            def queries_in(n):
                dve.wait_ge(s["a_proj"], n)
                for h in range(2):
                    r = slice(64 * h, 64 * h + 64)
                    ins = V.tensor_scalar(qbd[r, 8:16, h, :], ps[r, 3, :].rearrange("p (b q) -> p b q", q=S),
                                          wst[r, 3 * P:3 * P + 1], None, ALU.add)
                ins.then_inc(s["a_dve"], 1)

            def keys_in(n):
                dve.wait_ge(s["a_proj"], n)
                V.tensor_scalar(kT[:, 0, 512:1024], bank(3), wst[:, 3 * P + 1:3 * P + 2], None,
                                ALU.add).then_inc(s["a_dve"], 1)

            w_lo(1)
            turn_lo(0)
            dve.wait_ge(s["pool_set"], 1)
            queries_in(2)
            keys_in(4)

            def softmax_in(n, nb, w):
                for c in range(2):
                    dve.wait_ge(s["a_scores"], n + c + 1)
                    sc3 = bank(c).rearrange("p (b k) -> p b k", k=w)
                    m = mx[:, nb * c:nb * c + nb]
                    V.tensor_reduce(m, sc3, AX, ALU.max).then_inc(s["a_max"], 1)
                    dve.wait_ge(s["a_max"], n + c + 1)
                    V.tensor_tensor(prob[:, c, :].rearrange("p (b k) -> p b k", k=w), sc3, per_group(m, nb, w),
                                    ALU.subtract).then_inc(s["a_sub"], 1)

            def softmax_sum(n, c, nb, w):
                dve.wait_ge(s["a_exp"], n + c + 1)
                d = den[:, nb * c:nb * c + nb]
                V.tensor_reduce(d, prob[:, c, :].rearrange("p (b k) -> p b k", k=w), AX, ALU.add).then_inc(s["a_sum"], 1)
                dve.wait_ge(s["a_sum"], n + c + 1)
                V.reciprocal(rden[:, nb * c:nb * c + nb], d).then_inc(s["a_den"], 1)

            def group_range(w, q, a, b):
                V.tensor_reduce(q["max"][:, a:b], w[:, a:b, :], AX, ALU.max).then_inc(s["q_red"], 1)
                V.tensor_reduce(q["min"][:, a:b], w[:, a:b, :], AX, ALU.min).then_inc(s["q_red"], 1)

            def quant_scales(q, lo, hi, done, reduced, extra=None):
                v = {n: t[:, lo:hi] for n, t in q.items()}
                dve.wait_ge(s["q_red"], reduced)
                step(V.tensor_tensor(v["scale"], v["max"], v["min"], ALU.subtract))
                step(V.tensor_scalar(v["scale"], v["scale"], 1e-5, 1.0 / QMAX, ALU.max, ALU.mult))
                step(V.reciprocal(v["recip"], v["scale"]))
                step(V.scalar_tensor_tensor(v["base"], v["min"], -1.0, v["recip"], ALU.mult, ALU.mult))
                step(V.tensor_scalar(v["base"], v["base"], MAGIC, None, ALU.add))
                step(V.tensor_scalar(v["base"], v["base"], MAGIC, 0.0, ALU.subtract, ALU.max))
                step(V.tensor_scalar(v["base"], v["base"], QMAX, -1.0, ALU.min, ALU.mult))
                step(V.tensor_scalar(v["lo"], v["base"], MAGIC, None, ALU.add))
                if extra is not None:
                    extra()
                V.tensor_scalar(v["hi"], v["lo"], QMAX, None, ALU.add).then_inc(done, 1)

            def clip(g, sem_out):
                V.tensor_scalar(st[:, g, :], st[:, g, :], qs[0]["lo"][:, g:g + 1], qs[0]["hi"][:, g:g + 1], ALU.max,
                                ALU.min).then_inc(sem_out, 1)

            def attT_copy(n):
                dve.wait_ge(s["a_attT"], 2 * n + 2)
                V.tensor_copy(attT[:, 4:8, :], bank(5).rearrange("p (t q) -> p t q", q=P)).then_inc(s["a_attT_dve"], 1)

            def pair_step(j, first, last):
                w_lo(j + 2)
                if not first:
                    attT_copy(j - 1)
                softmax_in(2 * j, 8, S)
                softmax_sum(2 * j, 0, 8, S)
                softmax_sum(2 * j, 1, 8, S)
                if not first:
                    dve.wait_ge(s["a_out"], 2 * j)
                    V.tensor_copy(of_batches(big[:, bass.ds(j - 1, 1), :], 1), ps[:, 7:8, :].rearrange(
                        "p a (t q) -> p a t q", q=S)).then_inc(s["a_out_dve"], 1)
                dve.wait_ge(s["a_proj"], 6 * j + 6)
                V.tensor_copy(v_sb[:, 4:8, :], bank(3).rearrange("p (t d) -> p t d", d=P)).then_inc(s["a_dve"], 1)
                if not last:
                    queries_in(6 * j + 8)
                    keys_in(6 * j + 10)
                if first:
                    dve.wait_ge(s["wl_in"], 16)
                elif last:
                    group_range(st, qs[0], 18, 20)
                else:
                    g = bass.ds(3 * (j - 1), 3)
                    V.tensor_reduce(qs[0]["max"][:, g], st[:, g, :], AX, ALU.max).then_inc(s["q_red"], 1)
                    V.tensor_reduce(qs[0]["min"][:, g], st[:, g, :], AX, ALU.min).then_inc(s["q_red"], 1)

            pair_step(0, True, False)
            with dve.Fori(1, HP0 - 1) as j:
                pair_step(j, False, False)
            pair_step(HP0 - 1, False, True)
            attT_copy(HP0 - 1)
            dve.wait_ge(s["a_out"], 2 * HP0)
            V.tensor_copy(of_batches(big[:, HP0 - 1:HP0, :], 1), ps[:, 7:8, :].rearrange(
                "p a (t q) -> p a t q", q=S)).then_inc(s["a_out_dve"], 1)
            quant_scales(qs[0], 0, 20, s["q_stats"], 14, lambda: V.tensor_copy(wsc[:], qs[0]["scale"][:, 0:8]))
            for g in range(20):
                dve.wait_ge(s["q_round"], g + 1)
                clip(g, s["q_clip"])

            dve.wait_ge(s["yc_ps"], 1)
            V.tensor_tensor(yc[:], ps[:, 2, 0:1], vec[:, V_BO:V_BO + 1], ALU.add).then_inc(s["yc_ready"], 1)
            dve.wait_ge(s["yc_ready"], 1)
            dve.wait_ge(s["y_ready"], 2)
            V.tensor_scalar(yT[:, 512:1024], bank(1), yc[:], None, ALU.add).then_inc(s["yT_dve"], 1)

            def residual(k, gate):
                def half_of(c):
                    dve.wait_ge(s["back"], 2 * k + c + 1)
                    xx = x_tok[:, 4 * c:4 * c + 4, :]
                    return V.scalar_tensor_tensor(xx, bank(2 + c).rearrange("p (t d) -> p t d", d=D),
                                                  tg[:, gate:gate + 1], xx, ALU.mult, ALU.add)
                return half_of

            dve.wait_ge(s["tanh_done"], 1)

            norm(1, x_tok, nrm, False, residual(0, 0))
            dve.wait_ge(s["w_act"], 3)
            V.tensor_tensor(wkv_l[:], bank(0), wkv_h[:].bitcast(F32), ALU.subtract).then_inc(s["w_dve"], 1)
            dve.wait_ge(s["f_w_h"], 1)
            V.tensor_tensor(gu_l[:, 0, :], gu_st[:], gu_h[:, 0, :].bitcast(F32), ALU.subtract).then_inc(s["f_w_l"], 1)
            dve.wait_ge(s["sel_in"], 32)
            V.tensor_copy(selr1[:], sel1[:]).then_inc(s["selr"], 1)
            V.tensor_copy(selr0[:], sel0[:, 0:P]).then_inc(s["f_sel"], 1)
            turn_lo(1)
            rev = cst[:, C_REV:C_REV + E].unsqueeze(1).to_broadcast([P, NT, E])

            def first_of(dst, key, top):
                step(V.tensor_tensor(gk[:], key, per_group(top, NT, E), ALU.is_equal))
                step(V.tensor_tensor(gk[:], gk[:], rev, ALU.mult))
                step(V.tensor_reduce(gm[:], gk[:], AX, ALU.max))
                step(V.tensor_tensor(dst, gk[:], per_group(gm[:], NT, E), ALU.is_equal))

            def gating(k):
                dve.wait_ge(s["logits"], k + 1)
                step(V.tensor_copy(lg[:], ps[:, 6, 0:NT * E].rearrange("p (t e) -> p t e", e=E)))
                step(V.tensor_reduce(gm[:], lg[:], AX, ALU.max))
                V.tensor_tensor(gp[:], lg[:], per_group(gm[:], NT, E), ALU.subtract).then_inc(s["g_sub"], 1)
                dve.wait_ge(s["g_exp"], k + 1)
                if k == 1:
                    step(V.tensor_reduce(gm[:], gp[:], AX, ALU.add))
                    step(V.reciprocal(gm[:], gm[:]))
                    step(V.tensor_tensor(gp[:], gp[:], per_group(gm[:], NT, E), ALU.mult))
                    step(V.tensor_copy(lg[:], gp[:]))
                    step(V.tensor_reduce(gm[:], lg[:], AX, ALU.max))
                first_of(f1[:], lg[:], gm[:])
                step(V.scalar_tensor_tensor(lg[:], f1[:], -3e38, lg[:], ALU.mult, ALU.add))
                step(V.tensor_reduce(gm[:], lg[:], AX, ALU.max))
                first_of(f2[:], lg[:], gm[:])
                step(V.tensor_tensor(f1[:], f1[:], f2[:], ALU.add))
                step(V.tensor_tensor(gp[:], gp[:], f1[:], ALU.mult))
                step(V.tensor_reduce(gm[:], gp[:], AX, ALU.add))
                step(V.reciprocal(gm[:], gm[:]))
                V.tensor_tensor(lg[:], gp[:], per_group(gm[:], NT, E), ALU.mult).then_inc(s["gates"], 1)
                for c in range(2):
                    dve.wait_ge(s["g_h_ready"], 2 * k + c + 1)
                    o = slice(512 * c, 512 * c + 512)
                    V.tensor_tensor(g_l[:, o], ps[0:E, 4 + c, :], g_h[:, o].bitcast(F32),
                                    ALU.subtract).then_inc(s["g_l_ready"], 1)

            gating(0)

            def expert_step(m, par, first, last):
                for c in range(2):
                    if c == 1 and not last:
                        dve.wait_ge(s["f_w_h"], m + 2)
                        V.tensor_tensor(gu_l[:, 1 - par, :], gu_st[:], gu_h[:, 1 - par, :].bitcast(F32),
                                        ALU.subtract).then_inc(s["f_w_l"], 1)
                    dve.wait_ge(s["f_act"], 2 * m + c + 1)
                    if not first:
                        dve.wait_ge(s["f_hid"], 2 * m + c - 1)
                    V.tensor_tensor(hid1[:, c, :], act[:, c, :], bank(2 + c), ALU.mult).then_inc(s["f_h1"], 1)
                    dve.wait_ge(s["f_h1"], 2 * m + c + 1)
                    dve.wait_ge(s["f_gate"], 2 * m + c + 1)
                    if not first:
                        dve.wait_ge(s["f_down"], 2 * m + c - 1)
                    V.tensor_tensor(hid[:, c, :], hid1[:, c, :], bank(4 + c), ALU.mult).then_inc(s["f_hid"], 1)
                if not last:
                    V.tensor_copy(selr0[:], sel0[:, bass.ds((m + 1) * P, P)]).then_inc(s["f_sel"], 1)

            expert_step(0, 0, True, False)
            with dve.Fori(1, M0 - 2, 2) as m:
                expert_step(m, 1, False, False)
                expert_step(m + 1, 0, False, False)
            expert_step(M0 - 2, 1, False, False)
            expert_step(M0 - 1, 0, False, True)
            dve.wait_ge(s["f_down"], 2 * M0)
            V.tensor_copy(yT[:, 512:1024], bank(7)).then_inc(s["yT_dve"], 1)

            norm(2, x_tok, nrm, False, residual(1, 2))
            dve.wait_ge(s["hi_set"], 3)
            V.tensor_tensor(wx_l[:], wx_st[:], wx_h[:].bitcast(F32), ALU.subtract).then_inc(s["lo_set"], 1)
            turn_lo(2)
            dve.wait_ge(s["x_proj"], 2)
            V.tensor_scalar(kT[:, 1, 512:1024], bank(1), vec[:, V_BQ:V_BQ + 1], None, ALU.add).then_inc(s["x_dve"], 1)
            dve.wait_ge(s["x_proj"], 4)
            V.tensor_scalar(kT[:, 0, 512:1024], bank(3), vec[:, V_BK:V_BK + 1], None, ALU.add).then_inc(s["x_dve"], 1)
            dve.wait_ge(s["x_proj"], 6)
            V.tensor_copy(v_sb[:, 4:8, :], bank(7).rearrange("p (t d) -> p t d", d=P)).then_inc(s["x_dve"], 1)
            softmax_in(2 * HP0, 4, P)
            for c in range(2):
                softmax_sum(2 * HP0, c, 4, P)
            attT_copy(HP0)
            dve.wait_ge(s["a_out"], 2 * HP0 + 2)
            V.tensor_scalar(yT[:, 512:1024], bank(7), vec[:, V_BV:V_BV + 1], None, ALU.add).then_inc(s["yT_dve"], 1)

            pre = residual(2, 1)
            for c in range(2):
                step(pre(c))
                h = slice(4 * c, 4 * c + 4)
                for t in range(4 * c, 4 * c + 4):
                    ins = V.bn_stats(bst[:, t, :], x_tok[:, t, :])
                step(ins)
                for t in range(4 * c, 4 * c + 4):
                    ins = V.bn_aggr(bmv[:, t, :], bst[:, t, :])
                step(ins)
                V.tensor_scalar(ve[:, h], bmv[:, h, 1], LN_EPS, None, ALU.add).then_inc(s["ve_ready"], 1)
            for c in range(2):
                h = slice(4 * c, 4 * c + 4)
                dve.wait_ge(s["rstd_ready"], 6 + c + 1)
                step(V.tensor_tensor(gm[:, h], rs[:, h], rs[:, h], ALU.mult))
                step(V.tensor_tensor(gm[:, h], gm[:, h], bmv[:, h, 1], ALU.mult))
                V.tensor_scalar(ve[:, h], gm[:, h], LN_EPS, None, ALU.add).then_inc(s["ve_ready"], 1)
                for t in range(4 * c, 4 * c + 4):
                    ins = V.tensor_scalar(hs[:, t, :], x_tok[:, t, :], bmv[:, t, 0:1], rs[:, t:t + 1],
                                          ALU.subtract, ALU.mult)
                ins.then_inc(s["nrm_ready"], 1)
            for c in range(2):
                dve.wait_ge(s["rstd_ready"], 8 + c + 1)
                dve.wait_ge(s["nrm_ready"], 6 + c + 1)
                for t in range(4 * c, 4 * c + 4):
                    ins = V.tensor_scalar(nrm[:, t, :], hs[:, t, :], rs2[:, t:t + 1], None, ALU.mult)
                ins.then_inc(s["nrm_ready"], 1)
            turn_lo(3, vec[:, V_G1:V_G1 + 1])
            for b in range(2):
                for t in range(4 * b, 4 * b + 4):
                    dve.wait_ge(s["kv_ps"], t + 1)
                    src = bank(t).rearrange("p (g d) -> p g d", d=P)
                    V.tensor_reduce(qs[0]["max"][:, 4 * t:4 * t + 4], src, AX, ALU.max).then_inc(s["q_red"], 1)
                    V.tensor_reduce(qs[0]["min"][:, 4 * t:4 * t + 4], src, AX, ALU.min).then_inc(s["q_red"], 1)
                quant_scales(qs[0], 16 * b, 16 * b + 16, s["q_stats"], 14 + 8 * b + 8)
            for n in range(32):
                dve.wait_ge(s["q_round"], 20 + n + 1)
                clip(KV_ORDER[n], s["q_clip"])

            cosT = cst[:, C_COS:C_COS + S].unsqueeze(1).to_broadcast([P, 8, S])
            sinT = cst[:, C_SIN:C_SIN + S].unsqueeze(1).to_broadcast([P, 8, S])

            def rotate(hp, i):
                hh, c = i // 2, i % 2
                n = 4 * hp + i
                h = 2 * hp + hh
                for k, (dst, scale, table, done) in enumerate(((q1s, wsc, cosT, "r_q1"),
                                                               (q2s, wscR, sinT, "r_q2"))):
                    dve.wait_ge(s["r_ps"], 2 * n + k + 1)
                    if n >= 2:
                        dve.wait_ge(s["r_q"], n - 1)
                    V.scalar_tensor_tensor(dst[:, n % 2, :].rearrange("p (b q) -> p b q", q=S),
                                           bank(2 + k).rearrange("p (b q) -> p b q", q=S),
                                           scale[:, h:h + 1], table, ALU.mult, ALU.mult).then_inc(s[done], 1)

            for b in range(2):
                dve.wait_ge(s["q_deq"], 12 + (8 if b == 0 else 24))
                kk = st[:, 16 * b:16 * b + 16, :].rearrange("p (t g) d -> p t g d", g=4)[:, :, 0:2, :]
                kr = big[:, 0:2, 512 * b:512 * b + 512].rearrange("p a (t d) -> p t a d", d=D)
                cosK = cst[:, C_COSK:C_COSK + D].unsqueeze(1).unsqueeze(1).to_broadcast([P, 4, 2, D])
                for a in range(2):
                    sinK = cst[:, C_SINK + 64 * a:C_SINK + 64 * a + 64].unsqueeze(1).unsqueeze(1).to_broadcast(
                        [P, 4, 2, 64])
                    ins = V.tensor_tensor(kr[:, :, :, 64 * a:64 * a + 64], kk[:, :, :, 64 - 64 * a:128 - 64 * a],
                                          sinK, ALU.mult)
                step(ins)
                V.tensor_tensor(kk, kk, cosK, ALU.mult).then_inc(s["k_rope"], 1)
            dve.wait_ge(s["scr_in"], 32)
            for i in range(4):
                rotate(0, i)
            for n in (1, 3):
                dve.wait_ge(s["k_turn"], n + 1)
                V.tensor_copy(kT[:, n // 2, 512:1024], bank(5)).then_inc(s["k_dve"], 1)

            for hp in range(HP1):
                n = 2 * HP0 + 2 + 2 * hp
                softmax_in(n, 8, S)
                for i in range(4):
                    if hp + 1 < HP1:
                        rotate(hp + 1, i)
                    if i < 2:
                        softmax_sum(n, i, 8, S)
                if hp == 0:
                    dve.wait_ge(s["wm_in0"], 16)
                    group_range(stB, qs[1], 0, 11)
                elif hp == 1:
                    group_range(stB, qs[1], 11, 21)
                elif hp == 2:
                    quant_scales(qs[1], 0, 11, s["m_stats"], 14 + 16 + 4)
                    quant_scales(qs[1], 11, 21, s["m_stats"], 14 + 16 + 4)
            dve.wait_ge(s["y_ready"], 4)
            V.tensor_copy(yT[:, 512:1024], bank(1)).then_inc(s["yT_dve"], 1)

            def attended(c):
                dve.wait_ge(s["back"], 6 + c + 1)
                hh = hs[:, 4 * c:4 * c + 4, :]
                return V.tensor_tensor(hh, bank(2 + c).rearrange("p (t d) -> p t d", d=D), hh, ALU.add)

            norm(5, hs, nrm, True, attended)

            turn_lo(4, vec[:, V_G2:V_G2 + 1])
            gating(1)

            def gated(p, e, c):
                n = 4 * p + 2 * e + c
                dve.wait_ge(s["aux_act"], AUX[("gate", p, 1, 1)] + 1)
                dve.wait_ge(s["m_down"], DOWN[(p, 3 if e == 0 else 6, e, c)] + 1)
                if n >= 2:
                    dve.wait_ge(s["m_acc"], n)
                V.tensor_tensor(hid1[:, c, :], bank(6 + c), big[:, 2 * p + e, 512 * c:512 * c + 512],
                                ALU.mult).then_inc(s["m_gy"], 1)

            def next_ranges(p, n):
                w, q = (stB, qs[1]) if (p + 1) % 2 == 0 else (st, qs[0])
                parts = {0: ("max", 0, 5), 1: ("max", 5, 11), 2: ("min", 0, 5), 3: ("min", 5, 11),
                         5: ("max", 11, 16), 6: ("max", 16, 21), 7: ("min", 11, 16), 8: ("min", 16, 21)}
                reduced = 34 + 8 * p
                if n == 0:
                    dve.wait_ge(s[f"wm_in{(p + 1) % 2}"], 16 * ((p + 1) // 2 + 1))
                if n in parts:
                    what, a, b = parts[n]
                    V.tensor_reduce(q[what][:, a:b], w[:, a:b, :], AX,
                                    ALU.max if what == "max" else ALU.min).then_inc(s["q_red"], 1)
                elif n == 4:
                    quant_scales(q, 0, 11, s["m_stats"], reduced + 4)
                elif n == 9:
                    quant_scales(q, 11, 21, s["m_stats"], reduced + 8)

            for p in range(PAIRS):
                q = qs[1 - p % 2]
                for m in range(MT):
                    for c in range(2):
                        n = 2 * (MT * p + m) + c
                        dve.wait_ge(s["m_act"], n + 1)
                        if n >= 2:
                            pp, mm = divmod(MT * p + m - 1, MT)
                            dve.wait_ge(s["m_down"], DOWN[(pp, mm, 1 if mm >= 3 else 0, c)] + 1)
                        g = MT + 2 * m + 1
                        V.scalar_tensor_tensor(hid[:, c, :], bank(2 + c), q["scale"][:, g:g + 1], act[:, c, :],
                                               ALU.mult, ALU.mult).then_inc(s["m_up"], 1)
                        if m == 0 and p > 0:
                            gated(p - 1, 1, c)
                        if p + 1 < PAIRS:
                            next_ranges(p, 2 * m + c)
                    if m == 3:
                        gated(p, 0, 0)
                        gated(p, 0, 1)
            for c in range(2):
                gated(PAIRS - 1, 1, c)
            for c in range(2):
                dve.wait_ge(s["back"], 8 + c + 1)
                hh = hs[:, 4 * c:4 * c + 4, :]
                step(V.tensor_tensor(hh, bank(2 + c).rearrange("p (t d) -> p t d", d=D), hh, ALU.add))
                xx = x_tok[:, 4 * c:4 * c + 4, :]
                ins = V.scalar_tensor_tensor(xx, hh, tg[:, 3:4], xx, ALU.mult, ALU.add)
            ins.then_inc(s["x_new"], 1)


O_L1 = 2 * HP0 + 2

KV_ORDER = [4 * t + i for b in range(2) for kv in range(2) for t in range(4 * b, 4 * b + 4)
            for i in (2 * kv, 2 * kv + 1)]


def aux_plan():
    first = [("w13", 0, u) for u in range(4)] + [("w2", 0, 0), ("w2", 0, 1)]
    banks = [6, 7, 0, 1, 6, 7]
    order, after = list(first), {}
    for p in range(PAIRS):
        gates = [("gate", p, e, c) for e in range(2) for c in range(2)]
        own, nxt = p > 0, p + 1 < PAIRS
        after[(p, 0)] = [("w13", p, 2)] if own else []
        after[(p, 1)] = ([("w13", p, 3)] if own else []) + gates + ([("w2", p, 1)] if own else [])
        after[(p, 5)] = [("w13", p + 1, 0)] if nxt else []
        after[(p, 6)] = [("w2", p + 1, 0), ("w13", p + 1, 1)] if nxt else []
        for m in (0, 1, 5, 6):
            order += after[(p, m)]
    banks += [4 + n % 2 for n in range(len(order) - len(banks))]
    return first, after, {key: n for n, key in enumerate(order)}, banks


AUX_FIRST, AUX_AT, AUX, AUX_BANK = aux_plan()

DOWN = {key: n for n, key in enumerate(
    (p, m, e, c) for p in range(PAIRS) for m in range(MT)
    for e in ((0,) if m < 3 else (0, 1) if m == 3 else (1,)) for c in range(2))}

ROUND_SLOTS = [(0, 0)] * 5 + [(0, 3), (3, 6), (6, 9), (9, 11), (0, 0), (11, 14), (14, 17), (17, 19), (19, 21)]


def constants():
    c = np.zeros((P, C_END), np.float32)
    i = np.arange(P)
    c[:, C_ID:C_ID + P] = np.eye(P)
    c[:, C_CAU:C_CAU + S] = np.where(np.arange(S)[None] <= (i % S)[:, None], 0.0, -1e30)
    c[:, C_BLK:C_BLK + P] = np.where((i // S)[None] == (i // S)[:, None], 0.0, -1e30)
    inv = (np.float32(1.0) / np.float32(1e6) ** (np.arange(0, D, 2, dtype=np.float32) / np.float32(D))).astype(np.float32)
    freqs = np.arange(S, dtype=np.float32)[:, None] * inv[None]
    emb = np.concatenate([freqs, freqs], -1)
    cos, sin = np.cos(emb), np.sin(emb)
    sin = sin * np.where(i < 64, -1.0, 1.0)[None]
    c[:, C_COS:C_COS + S], c[:, C_SIN:C_SIN + S] = cos.T, sin.T
    c[:, C_COSK:C_COSK + D], c[:, C_SINK:C_SINK + D] = np.tile(cos, (2, 1)), np.tile(sin, (2, 1))
    c[:, C_REV:C_REV + E] = np.arange(E, 0, -1)
    sel0 = (np.arange(M0 * P)[None] // 176 == np.arange(E)[:, None]).astype(np.float32)
    sel1 = (np.arange(E * P)[None] // P == np.arange(E)[:, None]).astype(np.float32)
    return c, sel0, sel1


def kernel(**inputs):
    import concourse.bacc as _bacc
    from concourse.bass_utils import run_bass_kernel_spmd as _run

    a = {k: np.asarray(v) for k, v in inputs.items()}
    cst, sel0, sel1 = constants()
    col = lambda v: v.reshape(-1, P).T
    row = lambda v: np.tile(v[None], (P, 1))
    vec = np.concatenate([col(a["L0_xattn_bo"]), col(a["L1_xattn_bq"]), col(a["L1_xattn_bk"]), col(a["L1_xattn_bv"]),
                          col(a["L1_ffn_g1"]), col(a["L1_ffn_g2"]), col(a["L0_xattn_bv"]), a["L0_ffn_w_gate"],
                          a["L1_ffn_w_gate"].T, row(a["g_xattn"]), row(a["g_ffn"])], 1)
    tiles = lambda w: w.reshape(-1, P, D)
    w0 = np.zeros((HP0 + 1, P, WST), np.float32)
    w0[:HP0, :, 0:P] = tiles(a["L0_xattn_Wq"]).transpose(0, 2, 1)
    w0[:HP0, :, P:2 * P] = tiles(a["L0_xattn_Wk"]).transpose(0, 2, 1)
    w0[1:, :, 2 * P:3 * P] = tiles(a["L0_xattn_Wv"]).transpose(0, 2, 1)
    w0[:HP0, :, 3 * P] = a["L0_xattn_bq"].reshape(HP0, P)
    w0[:HP0, :, 3 * P + 1] = a["L0_xattn_bk"].reshape(HP0, P)
    up_cols = lambda w: w.transpose(1, 0, 2).reshape(D, M0, P).transpose(1, 0, 2)
    gu0 = np.concatenate([up_cols(a["L0_ffn_w_g"]), up_cols(a["L0_ffn_w_u"])], 2)
    wx = np.concatenate([a["L1_xattn_Wq"].T, a["L1_xattn_Wk"].T, a["L1_xattn_Wv"].T], 1)
    wl = np.concatenate([tiles(a["L1_ffn_w_q"]).transpose(1, 0, 2), tiles(a["L1_ffn_w_k"]).transpose(1, 0, 2),
                         tiles(a["L1_ffn_w_v"]).transpose(1, 0, 2), a["L1_ffn_w_o"].reshape(D, 8, P)], 1)
    pair = lambda w: w.reshape(PAIRS, MT, P, D).transpose(0, 2, 1, 3)
    w13 = np.stack([pair(a["L1_ffn_w1"]), pair(a["L1_ffn_w3"])], 3).reshape(PAIRS, P, 2 * MT, D)
    wm = np.concatenate([a["L1_ffn_w2"].reshape(PAIRS, P, MT, P), w13], 2)
    tok = lambda v: v.reshape(NT, P, D).transpose(1, 0, 2)
    arrays = {
        "cst": cst, "vec": vec, "x": tok(a["x"]), "ctx": a["ctx_1024"].reshape(TOK, D).T, "w0": w0,
        "wo0": a["L0_xattn_Wo"].T.reshape(HP0, P, D).transpose(1, 0, 2), "sel0": sel0, "sel1": sel1, "gu0": gu0,
        "d0": a["L0_ffn_w_d"].reshape(M0, P, D), "wx": wx, "wl": wl, "wm": wm,
    }
    nc = _bacc.Bacc("TRN2", target_bir_lowering=False, num_devices=1)
    args = []
    for k in arrays:
        arrays[k] = np.ascontiguousarray(arrays[k])
        args.append(nc.dram_tensor(k + "_dram", arrays[k].shape, F32, kind="ExternalInput").ap())
    args.append(nc.dram_tensor("out_dram", (P, NT, D), F32, kind="ExternalOutput").ap())
    build(nc, *args)
    r = _run(nc, [{k + "_dram": v for k, v in arrays.items()}], core_ids=[0])
    got = r.results[0]["out_dram"]
    return got.transpose(1, 0, 2).reshape(B, S, D)
```

```python
from contextlib import ExitStack

import numpy as np

import concourse.bass as bass
from concourse import mybir

F32 = mybir.dt.float32
F32R = mybir.dt.float32r
BF16 = mybir.dt.bfloat16
ALU = mybir.AluOpType
ACT = mybir.ActivationFunctionType
AX = mybir.AxisListType.X

P = 128
B, S, D = 16, 64, 128
TOK = B * S
NT = TOK // P
E = 8
M_HID = 176
HP0 = 8
HP1 = 4
M0 = 11
PAIRS = 4
MT = 7
PG = 3 * MT
MG = PAIRS * PG
QMAX = 15.0
MAGIC = 1.5 * 2.0 ** 23
LN_EPS = 1e-5

C_ID, C_CAU, C_BLK, C_COS, C_SIN, C_COSK, C_SINK, C_REV, C_END = (
    0, 128, 192, 320, 384, 448, 576, 704, 712)
V_BQ, V_BK, V_G1, V_G2, V_BV0, V_WG0, V_GX, V_END = (0, 1, 2, 3, 4, 12, 28, 32)
WST = 4 * P + 2


def build(nc, cst_d, vec_d, x_d, ctx_d, w0_d, wo0_d, bias_d, gu0_d, d0_d, wx_d, wl_d, wm_d, out_d):
    with ExitStack() as ctx:
        def sb(name, shape, dt=F32):
            return ctx.enter_context(nc.sbuf_tensor(name, shape, dt))

        def sem(name):
            return ctx.enter_context(nc.semaphore(name))

        ps = ctx.enter_context(nc.psum_tensor("ps", [P, 8, 512], F32))

        cst = sb("cst", [P, C_END])
        vec = sb("vec", [P, V_END])
        idb = sb("idb", [P, P], BF16)
        caub = sb("caub", [P, S], BF16)
        blkb = sb("blkb", [P, P], BF16)
        tg = sb("tg", [P, 4])
        wg_h = sb("wg_h", [P, 2 * E], F32R)
        wg_l = sb("wg_l", [P, 2 * E], F32R)
        half = sb("half", [P, NT])
        magic = sb("magic", [P, 1])
        x_tok = sb("x_tok", [P, NT, D])
        nrm = sb("nrm", [P, NT, D])
        hs = sb("hs", [P, NT, D])
        xh = sb("xh", [P, TOK], F32R)
        xl = sb("xl", [P, TOK], F32R)
        cT = sb("cT", [P, TOK])
        ch = sb("ch", [P, TOK], F32R)
        cl = sb("cl", [P, TOK], F32R)
        bst = sb("bst", [P, NT, 6])
        bmv = sb("bmv", [P, NT, 2])
        ve = sb("ve", [P, NT])
        rs = sb("rs", [P, NT])
        wst = sb("wst", [P, 2, WST])
        w_h = sb("w_h", [P, 4 * P], F32R)
        w_l = sb("w_l", [P, 4 * P], F32R)
        qbd = sb("qbd", [P, B, 2, S])
        v_sb = sb("v_sb", [P, NT, 2, P])
        prob = sb("prob", [P, 2, 512])
        attT = sb("attT", [P, NT, P])
        mx = sb("mx", [P, B])
        den = sb("den", [P, B])
        rden = sb("rden", [P, B])
        room = sb("room", [P, 10, TOK])
        big = room[:, 0:8, :]
        kT = room[:, 8:10, :]
        k_sin, k_cos = big[:, 4:6, :], big[:, 6:8, :]
        wo0 = sb("wo0", [P, HP0, D])
        biases = sb("biases", [P, 2, D])
        y_bias = sb("y_bias", [P, D])
        lg = sb("lg", [P, NT, E])
        gp = sb("gp", [P, NT, E])
        gk = sb("gk", [P, NT, E])
        f1 = sb("f1", [P, NT, E])
        f2 = sb("f2", [P, NT, E])
        gm = sb("gm", [P, NT])
        rows = room[:, 0:4, :]
        gu_all = room[:, 4:7, :].rearrange("p a c -> p (a c)")[:, 0:M0 * 2 * P].rearrange("p (m c) -> p m c", c=2 * P)
        d_all = room[:, 7:9, :].rearrange("p a c -> p (a c)")[:, 0:M0 * D].rearrange("p (m d) -> p m d", d=D)
        gu_h = sb("gu_h", [P, 2, 2 * P], F32R)
        gu_l = sb("gu_l", [P, 2, 2 * P], F32R)
        act = sb("act", [P, 2, 512])
        hid1 = sb("hid1", [P, 2, 512])
        hid = sb("hid", [P, 2, 512])
        wx_st = sb("wx_st", [P, 3 * P])
        wx_h, wx_l = w_h[:, 0:3 * P], w_l[:, 0:3 * P]
        st = sb("st", [P, 32, P])
        wqT = sb("wqT", [P, 8, P], F32R)
        wqR = sb("wqR", [P, 8, P], F32R)
        wkv_h = sb("wkv_h", [P, 4 * P], F32R)
        wkv_l = sb("wkv_l", [P, 4 * P], F32R)
        woT = wo0
        stg = sb("stg", [P, 2, MT, P])
        qB = sb("qB", [P, MG, P], BF16)
        q1s = sb("q1s", [P, 2, 512])
        q2s = sb("q2s", [P, 2, 512])
        qs = {n: sb(f"q_{n}", [P, 32]) for n in ("max", "min", "scale", "recip", "base", "lo", "hi")}
        qm = {n: sb(f"m_{n}", [P, 2, MT]) for n in ("max", "min", "scale", "recip", "base", "lo")}
        msc = sb("msc", [P, MG])
        rs2 = sb("rs2", [P, NT])
        wsc = sb("wsc", [P, 8])
        wscR = sb("wscR", [P, 8])
        w13T = sb("w13T", [P, 2 * MT, P], F32R)
        w2T = q1s.rearrange("p a c -> p (a c)")[:, 0:MT * D].rearrange("p (m d) -> p m d", d=D)
        gT = q2s[0:E, :, :].rearrange("e a c -> e (a c)")
        macc = kT[:, 0, :].rearrange("p (t d) -> p t d", d=D)

        gates_d = nc.dram_tensor("gates_dram", (E, TOK), F32, kind="Internal").ap()
        ident = cst[:, C_ID:C_ID + P]

        def bank(n):
            return ps[:, n, :]

        s = {n: sem(n) for n in (
            "cst_in", "vec_in", "x_in", "ctx_in", "wo0_in", "w0_in0", "w0_in1", "gu_first", "gu_in", "d_in",
            "wx_in", "wl_in", "m_in0", "m_in1", "scr_in", "stored", "pool_set", "tanh_done", "dve_set",
            "hi_set", "lo_set", "dve_step", "ve_ready", "rstd_ready", "nrm_ready", "turned", "xh_ready",
            "xl_ready", "x_new", "a_w_h", "a_w_l", "a_proj", "a_act", "a_dve", "a_scores", "a_max", "a_sub",
            "a_exp", "a_sum", "a_den", "a_norm", "a_attT", "a_attT_act", "a_attT_dve", "a_out", "a_out_act",
            "a_out_dve", "y_ready", "y_bias_ps", "y_bias_ready", "biases_in", "logits", "g_sub", "g_exp",
            "gates", "gT", "gT_copied", "row0_ps", "row0", "gates_out", "rows_in0", "rows_in1", "rows_in2", "rows_in3",
            "f_w_h", "f_w_l", "f_gu", "f_act", "f_h1", "f_hid", "f_down", "x_proj", "x_act", "x_dve",
            "q_stats", "q_round", "q_clip", "q_deq", "w_turn", "w_act", "w_dve", "w_rot", "kv_ps", "v_whole",
            "v_deq", "k_cos", "k_sin", "k_turn", "k_act", "k_dve", "r_ps", "r_q1", "r_q2", "r_q", "q_red",
            "m_red", "m_step", "m_stats", "m_scaled", "m_round", "m_based", "m_floor", "m_clip", "m_deq",
            "aux_ps", "aux_act", "m_gu", "m_act", "m_up", "m_down", "m_gy", "m_acc",
        )}

        def mm3(out, a_h, a_l, b_h, b_l, start=True, stop=True):
            nc.tensor.matmul(out, a_h, b_h, start=start, stop=False, skip_group_check=True)
            nc.tensor.matmul(out, a_h, b_l, start=False, stop=False, skip_group_check=True)
            return nc.tensor.matmul(out, a_l, b_h, start=False, stop=stop, skip_group_check=True)

        def mm2(out, a, b_h, b_l):
            nc.tensor.matmul(out, a, b_h, start=True, stop=False, skip_group_check=True)
            return nc.tensor.matmul(out, a, b_l, start=False, stop=True, skip_group_check=True)

        def per_group(t, n, w, sl=slice(None)):
            return t.unsqueeze(2).to_broadcast([P, n, w])

        def of_batches(t, b):
            return t.rearrange("p a (t b q) -> p a t b q", b=2, q=S)[:, :, :, b, :]

        def proj_base(j, odd):
            return 6 * j + (6 if odd else 4)

        def act_base(j, odd):
            return 4 * j + (4 if odd else 3)

        def dve_base(j, odd):
            return 2 * j + (2 if odd else 1)

        FIRST, ODD, EVEN, LAST = range(4)
        SPLIT = {FIRST: slice(0, 4 * P), EVEN: slice(0, 4 * P), ODD: slice(0, 2 * P)}

        block = ctx.enter_context(nc.Block())

        @block.sync
        def _(sp):
            sp.dma_start(x_tok[:], x_d).then_inc(s["x_in"], 16)
            sp.dma_start(cst[:], cst_d).then_inc(s["cst_in"], 16)
            sp.dma_start(cT[:], ctx_d).then_inc(s["ctx_in"], 16)
            sp.dma_start(vec[:], vec_d).then_inc(s["vec_in"], 16)
            sp.dma_start(wst[:, 0], w0_d[0]).then_inc(s["w0_in0"], 16)
            sp.dma_start(wst[:, 1], w0_d[1]).then_inc(s["w0_in1"], 16)
            sp.dma_start(stg[:, 0], wm_d[0]).then_inc(s["m_in0"], 16)
            sp.dma_start(stg[:, 1], wm_d[1]).then_inc(s["m_in1"], 16)
            sp.dma_start(st[:, 0:20, :], wl_d).then_inc(s["wl_in"], 16)
            sp.dma_start(wo0[:], wo0_d).then_inc(s["wo0_in"], 16)
            sp.dma_start(biases[:], bias_d).then_inc(s["biases_in"], 16)
            sp.dma_start(wx_st[:], wx_d).then_inc(s["wx_in"], 16)

            def columns(j, slot):
                sp.wait_ge(s["a_w_l"], j + 1)
                sp.wait_ge(s["a_act"], act_base(j, slot == 1))
                sp.wait_ge(s["a_dve"], dve_base(j, slot == 1))
                sp.dma_start(wst[:, slot], w0_d[bass.ds(j + 2, 1)].rearrange("n p c -> (n p) c")).then_inc(
                    s[f"w0_in{slot}"], 16)

            def weights_chunk(n, slot):
                sp.dma_start(stg[:, slot], wm_d[bass.ds(n, 1)].rearrange("n p g d -> (n p) g d")).then_inc(
                    s[f"m_in{slot}"], 16)

            columns(0, 0)
            with sp.Fori(0, HP0 // 2 - 2) as i:
                j = 2 * i + 1
                for u in range(2):
                    columns(j + u, 1 - u)
                    sp.wait_ge(s["m_clip"], j + u)
                    weights_chunk(j + u + 1, u)
            columns(HP0 - 3, 1)
            for u in range(2):
                sp.wait_ge(s["m_clip"], HP0 - 3 + u)
                weights_chunk(HP0 - 2 + u, u)

            sp.wait_ge(s["y_ready"], 2)
            sp.dma_start(gu_all[:, 0:2], gu0_d[:, 0:2]).then_inc(s["gu_first"], 16)
            sp.dma_start(gu_all[:, 2:M0], gu0_d[:, 2:M0]).then_inc(s["gu_in"], 16)
            sp.dma_start(d_all, d0_d).then_inc(s["d_in"], 16)
            sp.wait_ge(s["m_clip"], HP0 - 1)
            weights_chunk(HP0, 0)
            sp.wait_ge(s["m_clip"], HP0)
            weights_chunk(HP0 + 1, 1)

            def gate_rows(m):
                e, k = (m, 1) if m < E else (4 * (m - E), 4) if m < M0 - 1 else (0, E)
                sp.dma_start(rows[:, m % 4, :], gates_d[e:e + k, :].unsqueeze(1).to_broadcast([k, P // k, TOK])).then_inc(
                    s[f"rows_in{m % 4}"], 16)

            sp.wait_ge(s["gT_copied"], 2)
            sp.dma_start(gates_d, gT).then_inc(s["gates_out"], 16)
            sp.wait_ge(s["gates_out"], 16)
            for m in range(1, 4):
                gate_rows(m)
            for m in range(M0 - 4):
                sp.wait_ge(s["f_hid"], 2 * m + 2)
                gate_rows(m + 4)
                if m in (2, 4):
                    n = m // 2
                    sp.wait_ge(s["m_clip"], HP0 + n)
                    weights_chunk(HP0 + n + 1, (n + 1) % 2)
            sp.wait_ge(s["q_stats"], 1)
            sp.dma_start(wscR[0:64, :], wsc[64:128, :]).then_inc(s["scr_in"], 16)
            sp.dma_start(wscR[64:128, :], wsc[0:64, :]).then_inc(s["scr_in"], 16)
            sp.wait_ge(s["x_new"], 1)
            sp.dma_start(out_d, x_tok[:]).then_inc(s["stored"], 16)
            sp.wait_ge(s["stored"], 16)

        @block.gpsimd
        def _(pool):
            nc.gpsimd.memset(qbd[:], 0.0)
            nc.gpsimd.memset(half[:], -0.5)
            nc.gpsimd.memset(magic[:], MAGIC).then_inc(s["pool_set"], 1)
            pool.wait_ge(s["pool_set"], 1)

            def rstd(k, dst=rs):
                for c in range(2):
                    pool.wait_ge(s["ve_ready"], 2 * k + c + 1)
                    h = slice(4 * c, 4 * c + 4)
                    nc.gpsimd.tensor_tensor(dst[:, h], ve[:, h], half[:, h], ALU.pow).then_inc(s["rstd_ready"], 1)

            def normalise(n, c, nb, w):
                pool.wait_ge(s["a_den"], n + c + 1)
                pr = prob[:, c, :].rearrange("p (b k) -> p b k", k=w)
                nc.gpsimd.tensor_tensor(pr, pr, per_group(rden[:, nb * c:nb * (c + 1)], nb, w),
                                        ALU.mult).then_inc(s["a_norm"], 1)

            def m_scale(n, slot):
                pool.wait_ge(s["m_stats"], n + 1)
                nc.gpsimd.tensor_tensor(stg[:, slot], stg[:, slot], per_group(qm["recip"][:, slot, :], MT, P),
                                        ALU.mult).then_inc(s["m_scaled"], 1)

            def m_base(n, slot):
                pool.wait_ge(s["m_round"], n + 1)
                nc.gpsimd.tensor_tensor(stg[:, slot], stg[:, slot], per_group(qm["lo"][:, slot, :], MT, P),
                                        ALU.subtract).then_inc(s["m_based"], 1)

            rstd(0)
            for c in range(2):
                normalise(0, c, 8, S)
            with pool.Fori(0, HP0 // 2 - 1) as i:
                j = 2 * i + 1
                for u in range(2):
                    m_scale(j + u - 1, u)
                    m_base(j + u - 1, u)
                    for c in range(2):
                        normalise(2 * (j + u), c, 8, S)
            m_scale(HP0 - 2, 0)
            m_base(HP0 - 2, 0)
            for c in range(2):
                normalise(2 * HP0 - 2, c, 8, S)
            m_scale(HP0 - 1, 1)
            m_base(HP0 - 1, 1)

            def dequant(t, q, g, n_clip, done):
                pool.wait_ge(n_clip[0], n_clip[1])
                nc.gpsimd.tensor_scalar(t[:, g, :], t[:, g, :], -MAGIC, q["scale"][:, g:g + 1], ALU.add,
                                        ALU.mult).then_inc(done, 1)

            for g in range(8, 20):
                dequant(st, qs, g, (s["q_clip"], g + 1), s["q_deq"])
            rstd(1)
            pool.wait_ge(s["w_act"], 2)
            for a in range(2):
                ins = nc.gpsimd.tensor_copy(wqR[:, :, 64 * a:64 * a + 64],
                                            wqT[:, :, 64 - 64 * a:128 - 64 * a].bitcast(F32))
            ins.then_inc(s["w_rot"], 1)
            def expert_step(m, slot, count, first, chunk=None, part=None):
                for c in range(2):
                    if (part, c) == (1, 1):
                        m_base(*chunk)
                    pool.wait_ge(s["f_h1"], 2 * m + c + 1)
                    if first:
                        pool.wait_ge(s["row0"], c + 1)
                    elif c == 0:
                        pool.wait_ge(s[f"rows_in{slot}"], count)
                    if not first:
                        pool.wait_ge(s["f_down"], 2 * m + c - 1)
                    nc.gpsimd.tensor_tensor(hid[:, c, :], hid1[:, c, :], rows[:, slot, 512 * c:512 * c + 512],
                                            ALU.mult).then_inc(s["f_hid"], 1)
                if part == 0:
                    m_scale(*chunk)

            expert_step(0, 0, None, True)
            with pool.Fori(0, 2) as i:
                for k in range(4):
                    expert_step(4 * i + 1 + k, (1 + k) % 4, 16 * i + 16, False, (2 * i + HP0 + k // 2, k // 2), k % 2)
            expert_step(M0 - 2, 1, 48, False)
            expert_step(M0 - 1, 2, 48, False)
            rstd(2)
            for c in range(2):
                normalise(2 * HP0, c, 4, P)

            def real_w2(p):
                if p >= 2:
                    pool.wait_ge(s["aux_ps"], AUX[("w2", p - 2, 1)] + 1)
                for g in range(MT):
                    k = PG * p + g
                    nc.gpsimd.tensor_scalar(stg[:, p % 2, g, :], qB[:, k, :], msc[:, k:k + 1], None,
                                            ALU.mult).then_inc(s["m_deq"], 1)

            rstd(3)
            rstd(4, rs2)
            for n in range(16):
                dequant(st, qs, CLIP_ORDER[n], (s["q_clip"], 20 + n + 1), s["q_deq"])

            for b in range(2):
                pool.wait_ge(s["q_deq"], 12 + 8 * b + 8)
                kk = st[:, 16 * b:16 * b + 16, :].rearrange("p (t g) d -> p t g d", g=4)[:, :, 0:2, :]
                kc = k_cos[:, :, 512 * b:512 * b + 512].rearrange("p a (t d) -> p t a d", d=D)
                cosK = cst[:, C_COSK:C_COSK + D].unsqueeze(1).unsqueeze(1).to_broadcast([P, 4, 2, D])
                nc.gpsimd.tensor_tensor(kc, kk, cosK, ALU.mult).then_inc(s["k_cos"], 1)

            def rotate_add(hp, i):
                c, hh = i // 2, i % 2
                n = 4 * hp + i
                pool.wait_ge(s["r_q1"], n + 1)
                pool.wait_ge(s["r_q2"], n + 1)
                if hp > 0:
                    pool.wait_ge(s["a_scores"], 2 * HP0 + 2 + 2 * hp)
                nc.gpsimd.tensor_tensor(qbd[:, 8 * c:8 * c + 8, hh, :],
                                        q1s[:, n % 2, :].rearrange("p (b q) -> p b q", q=S),
                                        q2s[:, n % 2, :].rearrange("p (b q) -> p b q", q=S),
                                        ALU.add).then_inc(s["r_q"], 1)

            for i in range(4):
                rotate_add(0, i)
            for hp in range(HP1):
                for i in range(4):
                    if hp + 1 < HP1:
                        rotate_add(hp + 1, i)
                    if i < 2:
                        normalise(2 * HP0 + 2 + 2 * hp, i, 8, S)
            pool.wait_ge(s["m_clip"], 3 * PAIRS)
            real_w2(0)
            real_w2(1)

            def add_up(p, e):
                for c in range(2):
                    n = 4 * p + 2 * e + c
                    pool.wait_ge(s["m_gy"], n + 1)
                    pool.wait_ge(s["m_acc"], n + 1)
                    t = slice(4 * c, 4 * c + 4)
                    nc.gpsimd.tensor_tensor(macc[:, t, :], macc[:, t, :],
                                            hid1[:, c, :].rearrange("p (t d) -> p t d", d=D),
                                            ALU.add).then_inc(s["m_acc"], 1)

            rstd(5)
            nc.gpsimd.memset(macc, 0.0).then_inc(s["m_acc"], 1)
            for p in range(PAIRS):
                add_up(p, 0)
                if p + 2 < PAIRS:
                    real_w2(p + 2)
                add_up(p, 1)

        @block.scalar
        def _(sc):
            sc.wait_ge(s["ctx_in"], 16)
            nc.scalar.activation(ch[:], cT[:], ACT.Copy).then_inc(s["hi_set"], 1)
            sc.wait_ge(s["vec_in"], 16)
            nc.scalar.activation(wg_h[:], vec[:, V_WG0:V_WG0 + 2 * E], ACT.Copy).then_inc(s["hi_set"], 1)
            nc.scalar.activation(tg[:], vec[:, V_GX:V_GX + 4], ACT.Tanh).then_inc(s["tanh_done"], 1)
            sc.wait_ge(s["w0_in0"], 16)
            nc.scalar.activation(w_h[:, 0:2 * P], wst[:, 0, 0:2 * P], ACT.Copy).then_inc(s["a_w_h"], 1)

            def turn_hi(k, scale=1.0):
                for c in range(2):
                    sc.wait_ge(s["turned"], 2 * k + c + 1)
                    nc.scalar.activation(xh[:, 512 * c:512 * c + 512], bank(4 + c), ACT.Copy,
                                         scale=scale).then_inc(s["xh_ready"], 1)

            def exp_half(n, c, scale):
                sc.wait_ge(s["a_sub"], n + c + 1)
                nc.scalar.activation(prob[:, c, :], prob[:, c, :], ACT.Exp, scale=scale).then_inc(s["a_exp"], 1)

            def exps(n, scale):
                for c in range(2):
                    exp_half(n, c, scale)

            def attT_copies(n):
                for c in range(2):
                    sc.wait_ge(s["a_attT"], 2 * n + c + 1)
                    nc.scalar.activation(attT[:, 4 * c:4 * c + 4, :], bank(4 + c).rearrange("p (t q) -> p t q", q=P),
                                         ACT.Copy).then_inc(s["a_attT_act"], 1)

            def attT_copy(n):
                sc.wait_ge(s["a_attT"], 2 * n + 1)
                nc.scalar.activation(attT[:, 0:4, :], bank(4).rearrange("p (t q) -> p t q", q=P),
                                     ACT.Copy).then_inc(s["a_attT_act"], 1)

            def queries_in(n, c, slot):
                sc.wait_ge(s["a_proj"], n)
                for h in range(2):
                    r = slice(64 * h, 64 * h + 64)
                    ins = nc.scalar.activation(qbd[r, 8 * c:8 * c + 8, h, :],
                                               ps[r, 2 + c, :].rearrange("p (b q) -> p b q", q=S),
                                               ACT.Identity, bias=wst[r, slot, 4 * P:4 * P + 1])
                ins.then_inc(s["a_act"], 1)

            def keys_in(n, slot, b=6):
                sc.wait_ge(s["a_proj"], n)
                nc.scalar.activation(kT[:, 0, 0:512], bank(b), ACT.Identity,
                                     bias=wst[:, slot, 4 * P + 1:4 * P + 2]).then_inc(s["a_act"], 1)

            turn_hi(0)
            sc.wait_ge(s["pool_set"], 1)
            queries_in(1, 0, 0)
            queries_in(2, 1, 0)
            keys_in(3, 0, 2)

            def m_round(n, slot):
                sc.wait_ge(s["m_scaled"], n + 1)
                nc.scalar.activation(stg[:, slot], stg[:, slot], ACT.Identity, bias=magic[:]).then_inc(s["m_round"], 1)

            def m_floor(n, slot):
                sc.wait_ge(s["m_based"], n + 1)
                nc.scalar.activation(stg[:, slot], stg[:, slot], ACT.Relu).then_inc(s["m_floor"], 1)

            def values_in(n, b, dst):
                sc.wait_ge(s["a_proj"], n)
                nc.scalar.activation(dst, bank(b), ACT.Copy).then_inc(s["a_act"], 1)

            def output_in(j):
                sc.wait_ge(s["a_out"], 2 * j - 1)
                nc.scalar.activation(of_batches(big[:, bass.ds(j - 1, 1), :], 0), ps[:, 6:7, :].rearrange(
                    "p a (t q) -> p a t q", q=S), ACT.Copy).then_inc(s["a_out_act"], 1)

            def pair_step(j, kind, slot):
                n = proj_base(j, slot == 0)
                if kind != LAST:
                    sc.wait_ge(s[f"w0_in{slot}"], 8 * (j + 1 - slot) + 16)
                    sc.wait_ge(s["a_proj"], n)
                    nc.scalar.activation(w_h[:, SPLIT[kind]], wst[:, slot, SPLIT[kind]],
                                         ACT.Copy).then_inc(s["a_w_h"], 1)
                if kind != FIRST:
                    attT_copies(j - 1)
                    m_round(j - 1, slot)
                exp_half(2 * j, 0, 0.125)
                if kind == ODD or kind == LAST:
                    output_in(j)
                exp_half(2 * j, 1, 0.125)
                if slot == 1:
                    values_in(n + 1, 2, v_sb[:, 0:2, :, :].rearrange("p t s d -> p (t s d)"))
                    values_in(n + 3, 4, v_sb[:, 4:6, :, :].rearrange("p t s d -> p (t s d)"))
                if kind == EVEN:
                    output_in(j)
                if kind != LAST:
                    q = n + (4 if slot == 1 else 0)
                    queries_in(q + 1, 0, slot)
                    queries_in(q + 2, 1, slot)
                    keys_in(q + 3, slot)
                if kind != FIRST:
                    m_floor(j - 1, slot)

            pair_step(0, FIRST, 1)
            with sc.Fori(0, HP0 // 2 - 1) as i:
                j = 2 * i + 1
                pair_step(j, ODD, 0)
                pair_step(j + 1, EVEN, 1)
            pair_step(HP0 - 1, LAST, 0)
            attT_copies(HP0 - 1)
            sc.wait_ge(s["a_out"], 2 * HP0 - 1)
            nc.scalar.activation(of_batches(big[:, HP0 - 1:HP0, :], 0), ps[:, 6:7, :].rearrange(
                "p a (t q) -> p a t q", q=S), ACT.Copy).then_inc(s["a_out_act"], 1)

            def rounds(w, q, a, b, done):
                for g in range(a, b):
                    nc.scalar.activation(w[:, g, :], w[:, g, :], ACT.Identity, scale=q["recip"][:, g:g + 1],
                                         bias=magic[:]).then_inc(done, 1)

            m_round(HP0 - 1, 1)
            m_floor(HP0 - 1, 1)
            sc.wait_ge(s["q_stats"], 1)
            rounds(st, qs, 0, 20, s["q_round"])
            for n in range(2):
                sc.wait_ge(s["w_turn"], n + 1)
                nc.scalar.activation(wqT[:, 4 * n:4 * n + 4, :], bank(6 + n).rearrange("p (t d) -> p t d", d=P),
                                     ACT.Copy, bias=-MAGIC).then_inc(s["w_act"], 1)
            sc.wait_ge(s["w_turn"], 3)
            nc.scalar.activation(wkv_h[:], bank(0), ACT.Copy).then_inc(s["w_act"], 1)
            for n in range(2):
                sc.wait_ge(s["w_turn"], 4 + n)
                nc.scalar.activation(woT[:, 4 * n:4 * n + 4, :],
                                     bank(1 + 5 * n).rearrange("p (t d) -> p t d", d=P),
                                     ACT.Copy).then_inc(s["w_act"], 1)

            sc.wait_ge(s["gu_first"], 16)
            nc.scalar.activation(gu_h[:, 0, :], gu_all[:, 0, :], ACT.Copy).then_inc(s["f_w_h"], 1)
            turn_hi(1)
            sc.wait_ge(s["g_sub"], 1)
            nc.scalar.activation(gp[:], gp[:], ACT.Exp).then_inc(s["g_exp"], 1)

            def expert_step(m, par, first, last, chunk=None):
                if not last:
                    if not first:
                        sc.wait_ge(s["f_gu"], 2 * m)
                    nc.scalar.activation(gu_h[:, 1 - par, :], gu_all[:, bass.ds(m + 1, 1), :].rearrange(
                        "p a c -> p (a c)"), ACT.Copy).then_inc(s["f_w_h"], 1)
                for c in range(2):
                    sc.wait_ge(s["f_gu"], 2 * m + c + 1)
                    if not first:
                        sc.wait_ge(s["f_h1"], 2 * m + c - 1)
                    nc.scalar.activation(act[:, c, :], bank(c), ACT.Silu).then_inc(s["f_act"], 1)
                    if chunk is not None:
                        (m_floor if c else m_round)(*chunk)

            expert_step(0, 0, True, False)
            for c in range(2):
                sc.wait_ge(s["gT"], c + 1)
                nc.scalar.activation(gT[:, 512 * c:512 * c + 512], ps[0:E, 4 + c, :],
                                     ACT.Copy).then_inc(s["gT_copied"], 1)
            for c in range(2):
                sc.wait_ge(s["row0_ps"], c + 1)
                nc.scalar.activation(rows[:, 0, 512 * c:512 * c + 512], bank(4 + c), ACT.Copy).then_inc(s["row0"], 1)
            sc.wait_ge(s["gu_in"], 16)
            with sc.Fori(0, 2) as i:
                for k in range(4):
                    expert_step(4 * i + 1 + k, 1 - k % 2, False, False,
                                (2 * i + HP0 + k // 2, k // 2) if k % 2 else None)
            expert_step(M0 - 2, 1, False, False)
            expert_step(M0 - 1, 0, False, True)

            sc.wait_ge(s["wx_in"], 16)
            nc.scalar.activation(wx_h, wx_st[:], ACT.Copy).then_inc(s["hi_set"], 1)
            turn_hi(2)
            sc.wait_ge(s["x_proj"], 1)
            nc.scalar.activation(kT[:, 1, 0:512], bank(0), ACT.Identity,
                                 bias=vec[:, V_BQ:V_BQ + 1]).then_inc(s["x_act"], 1)
            sc.wait_ge(s["x_proj"], 3)
            nc.scalar.activation(kT[:, 0, 0:512], bank(2), ACT.Identity,
                                 bias=vec[:, V_BK:V_BK + 1]).then_inc(s["x_act"], 1)
            sc.wait_ge(s["x_proj"], 5)
            nc.scalar.activation(v_sb[:, 0:4, 0, :], bank(6).rearrange("p (t d) -> p t d", d=P),
                                 ACT.Copy).then_inc(s["x_act"], 1)
            exps(2 * HP0, 1.0)
            attT_copy(HP0)

            turn_hi(3, vec[:, V_G1:V_G1 + 1])
            for n in range(32):
                g = ROUND_ORDER[n]
                if n in (0, 12):
                    sc.wait_ge(s["q_stats"], 2 + n // 12)
                nc.scalar.activation(st[:, g, :], ps[:, g // 4, P * (g % 4):P * (g % 4) + P], ACT.Identity,
                                     scale=qs["recip"][:, g:g + 1], bias=magic[:]).then_inc(s["q_round"], 1)

            def keys_turned(h):
                sc.wait_ge(s["k_turn"], 2 * h + 1)
                nc.scalar.activation(kT[:, h, 0:512], bank(4 + 2 * h), ACT.Copy).then_inc(s["k_act"], 1)

            keys_turned(0)

            def attT_both(h):
                for c in range(2):
                    sc.wait_ge(s["a_attT"], 2 * (HP0 + 1 + h) + c + 1)
                    nc.scalar.activation(attT[:, 4 * c:4 * c + 4, :], bank(4 + c).rearrange("p (t q) -> p t q", q=P),
                                         ACT.Copy).then_inc(s["a_attT_act"], 1)

            def outputs(h):
                for q in range(2):
                    for b in range(2):
                        sc.wait_ge(s["a_out"], O_L1 + 4 * h + 2 * q + b + 1)
                        nc.scalar.activation(
                            of_batches(big[:, 2 * h:2 * h + 2, 512 * q:512 * q + 512], b).rearrange(
                                "p a t q -> p t a q"),
                            bank(output_bank(h, q) + b).rearrange("p (t a q) -> p t a q", a=2, q=S),
                            ACT.Copy).then_inc(s["a_out_act"], 1)

            for hp in range(HP1):
                if hp > 0:
                    attT_both(hp - 1)
                exps(2 * HP0 + 2 + 2 * hp, float(P) ** -0.5)
                if hp == 0:
                    keys_turned(1)
                    for t in range(NT):
                        v = st[:, 4 * t + 2:4 * t + 4, :]
                        sc.wait_ge(s["q_clip"], 20 + 16 + 2 * t + 2)
                        nc.scalar.activation(v, v, ACT.Copy, bias=-MAGIC).then_inc(s["v_whole"], 1)
                    for t in range(NT):
                        for g in (4 * t + 2, 4 * t + 3):
                            sc.wait_ge(s["v_whole"], t + 1)
                            nc.scalar.activation(st[:, g, :], st[:, g, :], ACT.Copy,
                                                 scale=qs["scale"][:, g:g + 1]).then_inc(s["v_deq"], 1)
                if hp > 0:
                    outputs(hp - 1)
            attT_copy(HP0 + HP1)
            for q in range(2):
                sc.wait_ge(s["a_out"], O_L1 + 4 * (HP1 - 1) + 2 * q + 1)
                nc.scalar.activation(of_batches(big[:, 2 * HP1 - 2:2 * HP1, 512 * q:512 * q + 512], 0).rearrange(
                    "p a t q -> p t a q"), bank(output_bank(HP1 - 1, q)).rearrange("p (t a q) -> p t a q", a=2, q=S),
                                     ACT.Copy).then_inc(s["a_out_act"], 1)

            def aux_out(*key):
                n = AUX[key]
                src = bank(AUX_BANK[n])
                sc.wait_ge(s["aux_ps"], n + 1)
                if key[0] == "w13":
                    t0, k = 4 * key[2], min(4, 2 * MT - 4 * key[2])
                    nc.scalar.activation(w13T[:, t0:t0 + k, :], src[:, 0:k * P].rearrange("p (t d) -> p t d", d=P),
                                         ACT.Copy).then_inc(s["aux_act"], 1)
                else:
                    t0, k = 4 * key[2], min(4, MT - 4 * key[2])
                    nc.scalar.activation(w2T[:, t0:t0 + k, :].rearrange("p t (r c) -> p t c r", c=2),
                                         src[:, 0:k * P].rearrange("p (t c r) -> p t c r", c=2, r=64),
                                         ACT.Copy).then_inc(s["aux_act"], 1)

            for key in AUX_FIRST:
                aux_out(*key)
            turn_hi(4, vec[:, V_G2:V_G2 + 1])
            keys = ()
            for p in range(PAIRS):
                for m in range(MT):
                    for c in range(2):
                        n = 2 * (MT * p + m) + c
                        sc.wait_ge(s["m_gu"], n + 1)
                        if n >= 2:
                            sc.wait_ge(s["m_up"], n - 1)
                        g = PG * p + MT + 2 * m
                        nc.scalar.activation(act[:, c, :], bank(c), ACT.Silu,
                                             scale=msc[:, g:g + 1]).then_inc(s["m_act"], 1)
                    if (p, m) == (0, 0):
                        sc.wait_ge(s["g_sub"], 2)
                        nc.scalar.activation(gp[:], gp[:], ACT.Exp).then_inc(s["g_exp"], 1)
                    for key in keys:
                        aux_out(*key)
                    keys = AUX_AT.get((p, m), ())

        @block.tensor
        def _(pe):
            T = nc.tensor

            def turn_norm(k):
                for c in range(2):
                    pe.wait_ge(s["nrm_ready"], 2 * (k if k < 3 else k + 1) + c + 1)
                    for t in range(4):
                        ins = T.transpose(ps[:, 4 + c, P * t:P * t + P], nrm[:, 4 * c + t, :], ident)
                    ins.then_inc(s["turned"], 1)

            def project(out_bank, w0, src_h, src_l, c):
                return mm3(bank(out_bank), w_h[:, w0:w0 + P], w_l[:, w0:w0 + P],
                           src_h[:, 512 * c:512 * c + 512], src_l[:, 512 * c:512 * c + 512])

            def q_and_k_first():
                for n, (w0, a_h, a_l) in enumerate(((0, xh, xl), (P, ch, cl))):
                    for c in range(2):
                        if n == 1:
                            pe.wait_ge(s["a_act"], c + 1)
                        project(2 + c, w0, a_h, a_l, c).then_inc(s["a_proj"], 1)

            pe.wait_ge(s["cst_in"], 16)
            turn_norm(0)
            pe.wait_ge(s["lo_set"], 2)
            pe.wait_ge(s["a_w_l"], 1)
            pe.wait_ge(s["xl_ready"], 2)
            q_and_k_first()

            def scores(n, lhs, rhs, mask, nb, w, in_place=None):
                for c in range(2):
                    if in_place is not None:
                        in_place(c)
                    pe.wait_ge(s["a_sub"], n + c - 1) if not (isinstance(n, int) and n == 0) else None
                    T.matmul(bank(c), idb[:], mask.unsqueeze(1).to_broadcast([P, nb, w]), start=True, stop=False,
                             skip_group_check=True)
                    for b in range(nb):
                        ins = T.matmul(ps[:, c, w * b:w * b + w], lhs(nb * c + b), rhs(nb * c + b), start=False,
                                       stop=True, skip_group_check=True)
                    ins.then_inc(s["a_scores"], 1)

            def turn_probs(n, halves=(0, 1)):
                for c in halves:
                    pe.wait_ge(s["a_norm"], 2 * n + c + 1)
                    for t in range(4):
                        ins = T.transpose(ps[:, 4 + c, P * t:P * t + P], prob[:, c, P * t:P * t + P], ident)
                    ins.then_inc(s["a_attT"], 1)

            def values0(j, slot):
                for c in range(2):
                    pe.wait_ge(s["a_attT_act"], 2 * j + c + 1)
                    for t in range(4 * c, 4 * c + 4):
                        for b in range(2):
                            r = slice(64 * b, 64 * b + 64)
                            o = slice(S * t, S * t + S)
                            if t == 4 * c and b == 0:
                                T.matmul(ps[:, 6, o], v_sb[r, t, slot, :], attT[r, t, 0:64], start=True, stop=True,
                                         skip_group_check=True)
                            else:
                                T.matmul(ps[0:64, 6 + b, o], v_sb[r, t, slot, 0:64], attT[r, t, 0:64], start=True,
                                         stop=True, skip_group_check=True)
                            ins = T.matmul(ps[64:128, 6 + b, o], v_sb[r, t, slot, 64:128], attT[r, t, 64:128],
                                           start=True, stop=True, skip_group_check=True)
                            if t == NT - 1:
                                ins.then_inc(s["a_out"], 1)

            def pair_step(j, kind):
                odd = kind in (ODD, LAST)
                act0, dve0 = act_base(j, odd), dve_base(j, odd)
                pe.wait_ge(s["a_act"], act0)
                pe.wait_ge(s["a_dve"], dve0)
                scores(2 * j, lambda b: qbd[:, b, :, :], lambda b: kT[:, 0, S * b:S * b + S], caub[:], 8, S)
                if kind != FIRST:
                    values0(j - 1, 0 if odd else 1)
                if kind == LAST:
                    return
                pe.wait_ge(s["a_w_l"], j + 2)
                if not odd:
                    for u in range(4):
                        for t in range(2):
                            o = P * (2 * u + t)
                            ins = mm3(ps[:, 2 + u, 256 * t:256 * t + 256], ch[:, o:o + P], cl[:, o:o + P],
                                      w_h[:, 2 * P:4 * P], w_l[:, 2 * P:4 * P])
                        ins.then_inc(s["a_proj"], 1)
                if not odd:
                    pe.wait_ge(s["a_act"], act0 + 1)
                project(2, 0, xh, xl, 0).then_inc(s["a_proj"], 1)
                if not odd:
                    pe.wait_ge(s["a_dve"], dve0 + 1)
                project(3, 0, xh, xl, 1).then_inc(s["a_proj"], 1)
                if kind != FIRST:
                    pe.wait_ge(s["a_out_act"], j)
                project(6, P, ch, cl, 0).then_inc(s["a_proj"], 1)
                if kind != FIRST:
                    pe.wait_ge(s["a_out_dve"], j)
                project(7, P, ch, cl, 1).then_inc(s["a_proj"], 1)
                for c in range(2):
                    if not odd:
                        pe.wait_ge(s["a_dve" if c else "a_act"], (dve0 if c else act0) + 2)
                    turn_probs(j, (c,))

            pe.wait_ge(s["dve_set"], 1)
            pair_step(0, FIRST)
            pe.wait_ge(s["wo0_in"], 16)
            pe.wait_ge(s["a_act"], act_base(0, False) + 3)
            for j in range(HP0):
                ins = T.matmul(ps[:, 2, 0:D], vec[:, V_BV0 + j:V_BV0 + j + 1].to_broadcast([P, P]), wo0[:, j, :],
                               start=(j == 0), stop=(j == HP0 - 1))
            ins.then_inc(s["y_bias_ps"], 1)
            pe.wait_ge(s["y_bias_ready"], 1)
            with pe.Fori(0, HP0 // 2 - 1) as i:
                j = 2 * i + 1
                pair_step(j, ODD)
                pair_step(j + 1, EVEN)
            pair_step(HP0 - 1, LAST)
            turn_probs(HP0 - 1)
            values0(HP0 - 1, 1)

            def output_projection(w, c, bias=None):
                for t in range(4):
                    o = 512 * c + P * t
                    for j in range(8):
                        ins = T.matmul(ps[:, c, P * t:P * t + P], big[:, j, o:o + P], w[:, j, :], start=(j == 0),
                                       stop=(j == 7), skip_group_check=True)
                    if bias is not None:
                        ins = T.matmul(ps[:, c, P * t:P * t + P], ident, bias, start=False, stop=True,
                                       skip_group_check=True)
                ins.then_inc(s["y_ready"], 1)

            pe.wait_ge(s["a_out_act"], HP0)
            pe.wait_ge(s["a_out_dve"], HP0)
            for c in range(2):
                output_projection(wo0, c, y_bias[:])

            def turn_own(n, b):
                for t in range(4):
                    g = 4 * n + t
                    pe.wait_ge(s["q_clip" if g < 8 else "q_deq"], g + 1 if g < 8 else g - 7)
                    ins = T.transpose(ps[:, b, P * t:P * t + P], st[:, g, :], ident)
                ins.then_inc(s["w_turn"], 1)

            turn_own(0, 6)
            turn_own(1, 7)
            pe.wait_ge(s["ve_ready"], 3)
            turn_own(2, 0)
            pe.wait_ge(s["ve_ready"], 4)
            turn_own(3, 1)
            pe.wait_ge(s["w_act"], 1)
            turn_own(4, 6)

            def gate_logits(k):
                for t in range(NT):
                    ins = mm3(ps[:, LOGITS_BANK[k], E * t:E * t + E], xh[:, P * t:P * t + P], xl[:, P * t:P * t + P],
                              wg_h[:, E * k:E * k + E], wg_l[:, E * k:E * k + E])
                ins.then_inc(s["logits"], 1)

            def gates_turned():
                pe.wait_ge(s["gates"], 1)
                for c in range(2):
                    for t in range(4):
                        ins = T.transpose(ps[0:E, 4 + c, P * t:P * t + P], lg[:, 4 * c + t, :], ident)
                    ins.then_inc(s["gT"], 1)

            def gate_up(m, par, c, first):
                pe.wait_ge(s["f_w_l"], m + 1)
                if not first:
                    pe.wait_ge(s["f_act"], 2 * m + c - 1)
                    pe.wait_ge(s["f_h1"], 2 * m + c - 1)
                x0, x1 = xh[:, 512 * c:512 * c + 512], xl[:, 512 * c:512 * c + 512]
                mm3(bank(c), gu_h[:, par, 0:P], gu_l[:, par, 0:P], x0, x1)
                mm3(bank(2 + c), gu_h[:, par, P:2 * P], gu_l[:, par, P:2 * P], x0, x1).then_inc(s["f_gu"], 1)

            def expert_step(m, par, first, last):
                for c in range(2):
                    if not last:
                        gate_up(m + 1, 1 - par, c, False)
                    pe.wait_ge(s["f_hid"], 2 * m + c + 1)
                    d = d_all[:, bass.ds(m, 1), :].rearrange("p a d -> p (a d)")
                    for t in range(4):
                        ins = T.matmul(ps[:, 6 + c, P * t:P * t + P], hid[:, c, P * t:P * t + P], d,
                                       start=(first and t == 0), stop=last, skip_group_check=True)
                    ins.then_inc(s["f_down"], 1)

            turn_norm(1)
            pe.wait_ge(s["w_act"], 5)
            pe.wait_ge(s["w_dve"], 1)
            pe.wait_ge(s["xl_ready"], 4)
            gate_logits(0)
            gate_up(0, 0, 0, True)
            gate_up(0, 0, 1, True)
            gates_turned()
            for c in range(2):
                pe.wait_ge(s["gT_copied"], c + 1)
                T.matmul(bank(4 + c), ident[0:E, 0:1].to_broadcast([E, P]), gT[:, 512 * c:512 * c + 512],
                         start=True, stop=True).then_inc(s["row0_ps"], 1)
            pe.wait_ge(s["d_in"], 16)
            expert_step(0, 0, True, False)
            with pe.Fori(0, 2) as i:
                for k in range(4):
                    expert_step(4 * i + 1 + k, 1 - k % 2, False, False)
            expert_step(M0 - 2, 1, False, False)
            expert_step(M0 - 1, 0, False, True)
            turn_norm(2)
            pe.wait_ge(s["xl_ready"], 6)
            pe.wait_ge(s["lo_set"], 3)
            for n, (w0, a_h, a_l) in enumerate(((0, xh, xl), (P, ch, cl))):
                for c in range(2):
                    mm3(bank(2 * n + c), wx_h[:, w0:w0 + P], wx_l[:, w0:w0 + P], a_h[:, 512 * c:512 * c + 512],
                        a_l[:, 512 * c:512 * c + 512]).then_inc(s["x_proj"], 1)
            for c in range(2):
                for t in range(4):
                    o = 512 * c + P * t
                    ins = mm3(ps[:, 6 + c, P * t:P * t + P], ch[:, o:o + P], cl[:, o:o + P], wx_h[:, 2 * P:3 * P],
                              wx_l[:, 2 * P:3 * P])
                ins.then_inc(s["x_proj"], 1)
            pe.wait_ge(s["x_act"], 2)
            pe.wait_ge(s["x_dve"], 2)
            scores(2 * HP0, lambda b: kT[:, 1, P * b:P * b + P], lambda b: kT[:, 0, P * b:P * b + P], blkb[:], 4, P)
            turn_probs(HP0)
            for c in range(2):
                pe.wait_ge(s["a_attT_act" if c == 0 else "a_attT_dve"], 2 * HP0 + 1 if c == 0 else 1)
                pe.wait_ge(s["x_act" if c == 0 else "x_dve"], 3)
                for t in range(4):
                    T.matmul(ps[:, 6 + c, P * t:P * t + P], attT[:, 4 * c + t, :], v_sb[:, 4 * c + t, 0, :],
                             start=True, stop=False, skip_group_check=True)
                    ins = T.matmul(ps[:, 6 + c, P * t:P * t + P], ident, biases[:, 1, :], start=False, stop=True,
                                   skip_group_check=True)
                ins.then_inc(s["a_out"], 1)

            turn_norm(3)
            pe.wait_ge(s["xl_ready"], 8)
            for t in range(NT):
                mm3(bank(t), xh[:, P * t:P * t + P], xl[:, P * t:P * t + P], wkv_h[:],
                    wkv_l[:]).then_inc(s["kv_ps"], 1)

            def rotate(hp, i):
                n = 4 * hp + i
                c, hh = i // 2, i % 2
                b0 = rotation_bank(n)
                x0, x1 = xh[:, 512 * c:512 * c + 512], xl[:, 512 * c:512 * c + 512]
                last_use = n - (2 if n in (2, 4) else 1)
                if n == 2 or n >= 4:
                    pe.wait_ge(s["r_q1"], last_use + 1)
                mm2(bank(b0), wqT[:, 2 * hp + hh, :], x0, x1).then_inc(s["r_ps"], 1)
                if n == 2 or n >= 4:
                    pe.wait_ge(s["r_q2"], last_use + 1)
                mm2(bank(b0 + 1), wqR[:, 2 * hp + hh, :], x0, x1).then_inc(s["r_ps"], 1)

            pe.wait_ge(s["w_rot"], 1)
            pe.wait_ge(s["q_round"], 20 + 12)
            rotate(0, 0)
            pe.wait_ge(s["q_round"], 20 + 24)
            rotate(0, 1)
            rotate(0, 2)
            pe.wait_ge(s["q_round"], 20 + 32)
            rotate(0, 3)

            def turn_keys(h):
                pe.wait_ge(s["k_sin"], 2)
                pe.wait_ge(s["k_cos"], 2)
                for c in range(2):
                    b = 4 + 2 * h + c
                    for t in range(4):
                        o, k = P * t, 512 * c + P * t
                        T.matmul(ps[:, b, o:o + P], k_cos[:, h, k:k + P], ident, start=True, stop=False,
                                 skip_group_check=True)
                        ins = T.matmul(ps[:, b, o:o + P], k_sin[:, h, k:k + P], ident, start=False, stop=True,
                                       skip_group_check=True)
                    ins.then_inc(s["k_turn"], 1)

            turn_keys(0)

            def values1(hp, i):
                q, last = i // 2, hp == HP1 - 1
                b0 = output_bank(hp, q)
                if i == 0:
                    pe.wait_ge(s["a_attT_act"], 2 * HP0 + 1 + 2 * hp + (1 if last else 2))
                    pe.wait_ge(s["v_deq"], 16)
                if i == 2 and last:
                    pe.wait_ge(s["a_attT_dve"], 2)
                elif i % 2 == 0 and (hp > 0 or q > 0) and (i == 0 or b0 == 6):
                    pe.wait_ge(s["a_out_act"], HP0 + 2 * (2 * hp + q))
                for t in range(2 * (i % 2), 2 * (i % 2) + 2):
                    for b in range(2):
                        r = slice(64 * b, 64 * b + 64)
                        ins = T.matmul(ps[:, b0 + b, P * t:P * t + P], st[r, 4 * (4 * q + t) + 2 + hp // 2, :],
                                       attT[r, 4 * q + t, :], start=True, stop=True, skip_group_check=True)
                        if t == 3:
                            ins.then_inc(s["a_out"], 1)

            for hp in range(HP1):
                if hp > 0:
                    turn_probs(HP0 + hp)

                def in_place(c, hp=hp):
                    pe.wait_ge(s["r_q"], 4 * hp + 2 * c + 2)
                    pe.wait_ge(s["k_dve" if c else "k_act"], 1 if hp < 2 else 2)

                scores(2 * HP0 + 2 + 2 * hp, lambda b: qbd[:, b, :, :],
                       lambda b, hp=hp: kT[:, hp // 2, S * b:S * b + S], caub[:], 8, S, in_place)
                if hp == 0:
                    turn_keys(1)
                if hp == 1:
                    pe.wait_ge(s["k_act"], 2)
                    pe.wait_ge(s["k_dve"], 2)
                for i in range(4):
                    if hp + 1 < HP1:
                        rotate(hp + 1, i)
                    if hp > 0:
                        values1(hp - 1, i)
            turn_probs(HP0 + HP1)
            for i in range(4):
                values1(HP1 - 1, i)
            for c in range(2):
                pe.wait_ge(s["a_out_act"], HP0 + 4 * (HP1 - 1) + c + 1)
                pe.wait_ge(s["a_out_dve"], HP0 + c + 1)
                output_projection(woT, c)

            def aux(*key):
                n = AUX[key]
                b, before = AUX_BANK[n], [k for k in range(n) if AUX_BANK[k] == AUX_BANK[n]]
                if before:
                    pe.wait_ge(s["aux_act"], before[-1] + 1)
                p = key[1]
                if key[0] == "w13":
                    for g in range(MT + 4 * key[2], min(MT + 4 * key[2] + 4, PG)):
                        o = P * (g - MT - 4 * key[2])
                        ins = T.matmul(ps[:, b, o:o + P], qB[:, PG * p + g, :], idb[:], start=True, stop=True,
                                       skip_group_check=True)
                else:
                    pe.wait_ge(s["m_deq"], MT * (p + 1))
                    w2 = stg[:, p % 2].rearrange("p g d -> p (g d)")
                    for m in range(4 * key[2], min(4 * key[2] + 4, MT)):
                        for r in range(2):
                            o = P * (m - 4 * key[2]) + 64 * r
                            if m == 3:
                                T.matmul(ps[0:64, b, o:o + 64], w2[0:64, 448 * r + 384:448 * r + 448],
                                         ident[0:64, 0:64], start=True, stop=True, skip_group_check=True)
                                ins = T.matmul(ps[64:128, b, o:o + 64], w2[64:128, 448 * r:448 * r + 64],
                                               ident[64:128, 64:128], start=True, stop=True, skip_group_check=True)
                            else:
                                e, f = (0, P * m) if m < 3 else (64, P * (m - 4) + 64)
                                ins = T.transpose(ps[:, b, o:o + 64], w2[e:e + 64, 448 * r + f:448 * r + f + P],
                                                  ident[e:e + 64, e:e + 64])
                ins.then_inc(s["aux_ps"], 1)

            for key in AUX_FIRST:
                aux(*key)
            turn_norm(4)
            pe.wait_ge(s["aux_act"], len(AUX_FIRST))

            def m_gate_up(p, m, c):
                n = 2 * (MT * p + m) + c
                if n >= 2:
                    pe.wait_ge(s["m_act"], n - 1)
                    pe.wait_ge(s["m_up"], n - 1)
                if c == 0 and m % 2 == 0:
                    pe.wait_ge(s["aux_act"], AUX[("w13", p, m // 2)] + 1)
                x0, x1 = xh[:, 512 * c:512 * c + 512], xl[:, 512 * c:512 * c + 512]
                mm2(bank(c), w13T[:, 2 * m, :], x0, x1)
                mm2(bank(2 + c), w13T[:, 2 * m + 1, :], x0, x1).then_inc(s["m_gu"], 1)

            def m_down(p, m, e, c):
                r = slice(0, P) if m != 3 else (slice(0, 64) if e == 0 else slice(64, 128))
                lo, hi = (0, 3) if e == 0 else (3, 6)
                n = 2 * (MT * p + m) + c
                pe.wait_ge(s["m_up"], n + 1)
                if m % 4 == 0:
                    pe.wait_ge(s["aux_act"], AUX[("w2", p, m // 4)] + 1)
                if m == lo and (p, e) != (0, 0):
                    pe.wait_ge(s["m_gy"], 4 * p + 2 * e + c - 1)
                for t in range(4):
                    ins = T.matmul(ps[:, 6 + c, P * t:P * t + P], hid[r, c, P * t:P * t + P], w2T[r, m, :],
                                   start=(m == lo and t == 0), stop=(m == hi), skip_group_check=True)
                ins.then_inc(s["m_down"], 1)

            for c in range(2):
                pe.wait_ge(s["xl_ready"], 8 + c + 1)
                m_gate_up(0, 0, c)
            gate_logits(1)
            for p in range(PAIRS):
                for m in range(MT):
                    for c in range(2):
                        if m + 1 < MT:
                            m_gate_up(p, m + 1, c)
                        elif p + 1 < PAIRS:
                            m_gate_up(p + 1, 0, c)
                        if m <= 3:
                            m_down(p, m, 0, c)
                        if m > 3:
                            m_down(p, m, 1, c)
                    if m == 3:
                        m_down(p, m, 1, 0)
                        m_down(p, m, 1, 1)
                    if (p, m) == (0, 3):
                        pe.wait_ge(s["g_sub"], 2)
                    for key in AUX_AT.get((p, m), ()):
                        aux(*key)

        @block.vector
        def _(dve):
            V = nc.vector
            steps = [0]

            def step(ins):
                steps[0] += 1
                ins.then_inc(s["dve_step"], 1)
                dve.wait_ge(s["dve_step"], steps[0])

            dve.wait_ge(s["x_in"], 16)

            def norm(k, src, dst, rms, pre=None):
                for c in range(2):
                    if pre is not None:
                        step(pre(c))
                    h = slice(4 * c, 4 * c + 4)
                    for t in range(4 * c, 4 * c + 4):
                        ins = V.bn_stats(bst[:, t, :], src[:, t, :])
                    step(ins)
                    for t in range(4 * c, 4 * c + 4):
                        ins = V.bn_aggr(bmv[:, t, :], bst[:, t, :])
                    step(ins)
                    if rms:
                        step(V.tensor_tensor(ve[:, h], bmv[:, h, 0], bmv[:, h, 0], ALU.mult))
                        V.scalar_tensor_tensor(ve[:, h], ve[:, h], LN_EPS, bmv[:, h, 1], ALU.add,
                                               ALU.add).then_inc(s["ve_ready"], 1)
                    else:
                        V.tensor_scalar(ve[:, h], bmv[:, h, 1], LN_EPS, None, ALU.add).then_inc(s["ve_ready"], 1)
                for c in range(2):
                    dve.wait_ge(s["rstd_ready"], 2 * k + c + 1)
                    for t in range(4 * c, 4 * c + 4):
                        if rms:
                            ins = V.tensor_scalar(dst[:, t, :], src[:, t, :], rs[:, t:t + 1], None, ALU.mult)
                        else:
                            ins = V.tensor_scalar(dst[:, t, :], src[:, t, :], bmv[:, t, 0:1], rs[:, t:t + 1],
                                                  ALU.subtract, ALU.mult)
                    ins.then_inc(s["nrm_ready"], 1)

            def turn_lo(k, gain=None):
                for c in range(2):
                    dve.wait_ge(s["xh_ready"], 2 * k + c + 1)
                    o = slice(512 * c, 512 * c + 512)
                    V.scalar_tensor_tensor(xl[:, o], bank(4 + c), 1.0 if gain is None else gain,
                                           xh[:, o].bitcast(F32), ALU.mult, ALU.subtract).then_inc(s["xl_ready"], 1)

            norm(0, x_tok, nrm, False)
            dve.wait_ge(s["cst_in"], 16)
            V.tensor_copy(idb[:], ident)
            V.tensor_copy(caub[:], cst[:, C_CAU:C_CAU + S])
            V.tensor_copy(blkb[:], cst[:, C_BLK:C_BLK + P]).then_inc(s["dve_set"], 1)
            dve.wait_ge(s["hi_set"], 1)
            V.tensor_tensor(cl[:], cT[:], ch[:].bitcast(F32), ALU.subtract).then_inc(s["lo_set"], 1)
            dve.wait_ge(s["hi_set"], 2)
            V.tensor_tensor(wg_l[:], vec[:, V_WG0:V_WG0 + 2 * E], wg_h[:].bitcast(F32),
                            ALU.subtract).then_inc(s["lo_set"], 1)

            def w_lo(n, slot, cols):
                dve.wait_ge(s["a_w_h"], n)
                V.tensor_tensor(w_l[:, cols], wst[:, slot, cols], w_h[:, cols].bitcast(F32),
                                ALU.subtract).then_inc(s["a_w_l"], 1)

            def keys_in(n, slot, b=7):
                dve.wait_ge(s["a_proj"], n)
                V.tensor_scalar(kT[:, 0, 512:1024], bank(b), wst[:, slot, 4 * P + 1:4 * P + 2], None,
                                ALU.add).then_inc(s["a_dve"], 1)

            w_lo(1, 0, slice(0, 2 * P))
            turn_lo(0)
            keys_in(4, 0, 3)

            def softmax_in(n, nb, w):
                for c in range(2):
                    dve.wait_ge(s["a_scores"], n + c + 1)
                    sc3 = bank(c).rearrange("p (b k) -> p b k", k=w)
                    m = mx[:, nb * c:nb * c + nb]
                    V.tensor_reduce(m, sc3, AX, ALU.max).then_inc(s["a_max"], 1)
                    dve.wait_ge(s["a_max"], n + c + 1)
                    V.tensor_tensor(prob[:, c, :].rearrange("p (b k) -> p b k", k=w), sc3, per_group(m, nb, w),
                                    ALU.subtract).then_inc(s["a_sub"], 1)

            def softmax_sum(n, c, nb, w):
                dve.wait_ge(s["a_exp"], n + c + 1)
                d = den[:, nb * c:nb * c + nb]
                V.tensor_reduce(d, prob[:, c, :].rearrange("p (b k) -> p b k", k=w), AX, ALU.add).then_inc(s["a_sum"], 1)
                dve.wait_ge(s["a_sum"], n + c + 1)
                V.reciprocal(rden[:, nb * c:nb * c + nb], d).then_inc(s["a_den"], 1)

            def group_range(w, q, a, b):
                V.tensor_reduce(q["max"][:, a:b], w[:, a:b, :], AX, ALU.max).then_inc(s["q_red"], 1)
                V.tensor_reduce(q["min"][:, a:b], w[:, a:b, :], AX, ALU.min).then_inc(s["q_red"], 1)

            def quant_scales(q, lo, hi, done, reduced, extra=None, beside=None):
                v = {n: t[:, lo:hi] for n, t in q.items()}
                dve.wait_ge(s["q_red"], reduced)
                count = iter(range(8))

                def step(ins):
                    steps[0] += 1
                    ins.then_inc(s["dve_step"], 1)
                    if beside is not None:
                        beside(next(count))
                    dve.wait_ge(s["dve_step"], steps[0])

                step(V.tensor_tensor(v["scale"], v["max"], v["min"], ALU.subtract))
                step(V.tensor_scalar(v["scale"], v["scale"], 1e-5, 1.0 / QMAX, ALU.max, ALU.mult))
                step(V.reciprocal(v["recip"], v["scale"]))
                step(V.scalar_tensor_tensor(v["base"], v["min"], -1.0, v["recip"], ALU.mult, ALU.mult))
                step(V.tensor_scalar(v["base"], v["base"], MAGIC, None, ALU.add))
                step(V.tensor_scalar(v["base"], v["base"], MAGIC, 0.0, ALU.subtract, ALU.max))
                step(V.tensor_scalar(v["base"], v["base"], QMAX, -1.0, ALU.min, ALU.mult))
                step(V.tensor_scalar(v["lo"], v["base"], MAGIC, None, ALU.add))
                if extra is not None:
                    extra()
                V.tensor_scalar(v["hi"], v["lo"], QMAX, None, ALU.add).then_inc(done, 1)

            def clip(g, sem_out):
                V.tensor_scalar(st[:, g, :], st[:, g, :], qs["lo"][:, g:g + 1], qs["hi"][:, g:g + 1], ALU.max,
                                ALU.min).then_inc(sem_out, 1)

            def attT_copy(n):
                dve.wait_ge(s["a_attT"], 2 * n + 2)
                V.tensor_copy(attT[:, 4:8, :], bank(5).rearrange("p (t q) -> p t q", q=P)).then_inc(s["a_attT_dve"], 1)

            def m_ranges(n, slot, what):
                if what == "max":
                    dve.wait_ge(s[f"m_in{slot}"], 8 * n + 16 - 8 * slot)
                V.tensor_reduce(qm[what][:, slot, :], stg[:, slot], AX,
                                ALU.max if what == "max" else ALU.min).then_inc(s["m_red"], 1)

            def m_scales(n, slot, a, b):
                v = {k: t[:, slot, :] for k, t in qm.items()}
                sc_, mn, rc, bs = v["scale"], v["min"], v["recip"], v["base"]
                for k in range(a, b):
                    if k == 0:
                        dve.wait_ge(s["m_red"], 2 * n + 2)
                        ins = V.tensor_tensor(sc_, v["max"], mn, ALU.subtract)
                    else:
                        dve.wait_ge(s["m_step"], 7 * n + k)
                    if k == 1:
                        ins = V.tensor_scalar(sc_, sc_, 1e-5, 1.0 / QMAX, ALU.max, ALU.mult)
                    elif k == 2:
                        ins = V.reciprocal(rc, sc_)
                    elif k == 3:
                        ins = V.scalar_tensor_tensor(bs, mn, -1.0, rc, ALU.mult, ALU.mult)
                    elif k == 4:
                        ins = V.tensor_scalar(bs, bs, MAGIC, None, ALU.add)
                    elif k == 5:
                        ins = V.tensor_scalar(bs, bs, MAGIC, 0.0, ALU.subtract, ALU.max)
                    elif k == 6:
                        ins = V.tensor_scalar(bs, bs, QMAX, -1.0, ALU.min, ALU.mult)
                    elif k == 7:
                        V.tensor_copy(msc[:, bass.ds(MT * n, MT)], sc_)
                        ins = V.tensor_scalar(v["lo"], bs, MAGIC, None, ALU.add)
                    ins.then_inc(s["m_stats" if k == 7 else "m_step"], 1)

            def m_whole(n, slot):
                dve.wait_ge(s["m_floor"], n + 1)
                V.scalar_tensor_tensor(qB[:, bass.ds(MT * n, MT), :], stg[:, slot], QMAX,
                                       per_group(qm["base"][:, slot, :], MT, P), ALU.min,
                                       ALU.add).then_inc(s["m_clip"], 1)

            def values_in(n, b, dst):
                dve.wait_ge(s["a_proj"], n)
                V.tensor_copy(dst, bank(b)).then_inc(s["a_dve"], 1)

            def pair_step(j, kind, slot):
                first, last = kind == FIRST, kind == LAST
                n = proj_base(j, slot == 1)
                if not last:
                    w_lo(j + 2, 1 - slot, SPLIT[kind])
                softmax_in(2 * j, 8, S)
                if not first:
                    dve.wait_ge(s["a_out"], 2 * j)
                    V.tensor_copy(of_batches(big[:, bass.ds(j - 1, 1), :], 1), ps[:, 7:8, :].rearrange(
                        "p a (t q) -> p a t q", q=S)).then_inc(s["a_out_dve"], 1)
                softmax_sum(2 * j, 0, 8, S)
                softmax_sum(2 * j, 1, 8, S)
                if slot == 0:
                    values_in(n + 2, 3, v_sb[:, 2:4, :, :].rearrange("p t s d -> p (t s d)"))
                    values_in(n + 4, 5, v_sb[:, 6:8, :, :].rearrange("p t s d -> p (t s d)"))
                    m_ranges(j, slot, "max")
                if not last:
                    keys_in(n + (8 if slot == 0 else 4), 1 - slot)
                if slot == 1:
                    m_ranges(j, slot, "max")
                m_ranges(j, slot, "min")
                m_scales(j, slot, 0, 1)
                if first:
                    dve.wait_ge(s["wl_in"], 16)
                    dve.wait_ge(s["y_bias_ps"], 1)
                    dve.wait_ge(s["biases_in"], 16)
                    V.tensor_tensor(y_bias[:], ps[:, 2, 0:D], biases[:, 0, :], ALU.add).then_inc(s["y_bias_ready"], 1)
                elif slot == 0:
                    g = bass.ds(j - 2, 2)
                    V.tensor_reduce(qs["max"][:, g], st[:, g, :], AX, ALU.max).then_inc(s["q_red"], 1)
                m_scales(j, slot, 1, 2)
                if slot == 0 and not first:
                    V.tensor_reduce(qs["min"][:, g], st[:, g, :], AX, ALU.min).then_inc(s["q_red"], 1)
                m_scales(j, slot, 2, 8)
                if not first:
                    m_whole(j - 1, 1 - slot)
                if last:
                    group_range(st, qs, HP0 - 2, 20)

            pair_step(0, FIRST, 0)
            with dve.Fori(0, HP0 // 2 - 1) as i:
                j = 2 * i + 1
                pair_step(j, ODD, 1)
                pair_step(j + 1, EVEN, 0)
            pair_step(HP0 - 1, LAST, 1)
            dve.wait_ge(s["a_out"], 2 * HP0)
            V.tensor_copy(of_batches(big[:, HP0 - 1:HP0, :], 1), ps[:, 7:8, :].rearrange(
                "p a (t q) -> p a t q", q=S)).then_inc(s["a_out_dve"], 1)
            m_whole(HP0 - 1, 1)
            quant_scales(qs, 0, 20, s["q_stats"], 8, lambda: V.tensor_copy(wsc[:], qs["scale"][:, 0:8]))
            for g in range(20):
                dve.wait_ge(s["q_round"], g + 1)
                clip(g, s["q_clip"])

            def residual(done, count, b, gate):
                def half_of(c):
                    dve.wait_ge(s[done], count + c)
                    xx = x_tok[:, 4 * c:4 * c + 4, :]
                    return V.scalar_tensor_tensor(xx, bank(b + c).rearrange("p (t d) -> p t d", d=D),
                                                  tg[:, gate:gate + 1], xx, ALU.mult, ALU.add)
                return half_of

            dve.wait_ge(s["tanh_done"], 1)

            norm(1, x_tok, nrm, False, residual("y_ready", 1, 0, 0))
            dve.wait_ge(s["w_act"], 3)
            V.tensor_tensor(wkv_l[:], bank(0), wkv_h[:].bitcast(F32), ALU.subtract).then_inc(s["w_dve"], 1)
            dve.wait_ge(s["f_w_h"], 1)
            V.tensor_tensor(gu_l[:, 0, :], gu_all[:, 0, :], gu_h[:, 0, :].bitcast(F32), ALU.subtract).then_inc(s["f_w_l"], 1)
            turn_lo(1)
            rev = cst[:, C_REV:C_REV + E].unsqueeze(1).to_broadcast([P, NT, E])

            def first_of(step, dst, key, top):
                step(V.tensor_tensor(gk[:], key, per_group(top, NT, E), ALU.is_equal))
                step(V.tensor_tensor(gk[:], gk[:], rev, ALU.mult))
                step(V.tensor_reduce(gm[:], gk[:], AX, ALU.max))
                step(V.tensor_tensor(dst, gk[:], per_group(gm[:], NT, E), ALU.is_equal))

            def gating(k, beside=None):
                count = iter(range(100))

                def step_beside(ins):
                    steps[0] += 1
                    ins.then_inc(s["dve_step"], 1)
                    if beside is not None:
                        beside(next(count))
                    dve.wait_ge(s["dve_step"], steps[0])

                dve.wait_ge(s["logits"], k + 1)
                step(V.tensor_copy(lg[:], ps[:, LOGITS_BANK[k], 0:NT * E].rearrange("p (t e) -> p t e", e=E)))
                step(V.tensor_reduce(gm[:], lg[:], AX, ALU.max))
                V.tensor_tensor(gp[:], lg[:], per_group(gm[:], NT, E), ALU.subtract).then_inc(s["g_sub"], 1)
                dve.wait_ge(s["g_exp"], k + 1)
                if k == 1:
                    step_beside(V.tensor_reduce(gm[:], gp[:], AX, ALU.add))
                    step_beside(V.reciprocal(gm[:], gm[:]))
                    step_beside(V.tensor_tensor(gp[:], gp[:], per_group(gm[:], NT, E), ALU.mult))
                    step_beside(V.tensor_copy(lg[:], gp[:]))
                    step_beside(V.tensor_reduce(gm[:], lg[:], AX, ALU.max))
                first_of(step_beside, f1[:], lg[:], gm[:])
                step_beside(V.scalar_tensor_tensor(lg[:], f1[:], -3e38, lg[:], ALU.mult, ALU.add))
                step_beside(V.tensor_reduce(gm[:], lg[:], AX, ALU.max))
                first_of(step_beside, f2[:], lg[:], gm[:])
                step_beside(V.tensor_tensor(f1[:], f1[:], f2[:], ALU.add))
                step_beside(V.tensor_tensor(gp[:], gp[:], f1[:], ALU.mult))
                step_beside(V.tensor_reduce(gm[:], gp[:], AX, ALU.add))
                step_beside(V.reciprocal(gm[:], gm[:]))
                V.tensor_tensor(lg[:], gp[:], per_group(gm[:], NT, E), ALU.mult).then_inc(s["gates"], 1)

            gating(0)

            def expert_step(m, par, first, last, chunk=None, part=None):
                for c in range(2):
                    if c == 1 and not last:
                        dve.wait_ge(s["f_w_h"], m + 2)
                        V.tensor_tensor(gu_l[:, 1 - par, :], gu_all[:, bass.ds(m + 1, 1), :].rearrange(
                            "p a c -> p (a c)"), gu_h[:, 1 - par, :].bitcast(F32),
                                        ALU.subtract).then_inc(s["f_w_l"], 1)
                    dve.wait_ge(s["f_act"], 2 * m + c + 1)
                    if not first:
                        dve.wait_ge(s["f_hid"], 2 * m + c - 1)
                    V.tensor_tensor(hid1[:, c, :], act[:, c, :], bank(2 + c), ALU.mult).then_inc(s["f_h1"], 1)
                    if part == 0:
                        m_ranges(*chunk, "min" if c else "max")
                if part == 0:
                    m_scales(*chunk, 0, 8)
                if part == 1:
                    m_whole(*chunk)

            expert_step(0, 0, True, False)
            with dve.Fori(0, 2) as i:
                for k in range(4):
                    expert_step(4 * i + 1 + k, 1 - k % 2, False, False, (2 * i + HP0 + k // 2, k // 2), k % 2)
            expert_step(M0 - 2, 1, False, False)
            expert_step(M0 - 1, 0, False, True)

            norm(2, x_tok, nrm, False, residual("f_down", 2 * M0 - 1, 6, 2))
            dve.wait_ge(s["hi_set"], 3)
            V.tensor_tensor(wx_l, wx_st[:], wx_h.bitcast(F32), ALU.subtract).then_inc(s["lo_set"], 1)
            turn_lo(2)
            dve.wait_ge(s["x_proj"], 2)
            V.tensor_scalar(kT[:, 1, 512:1024], bank(1), vec[:, V_BQ:V_BQ + 1], None, ALU.add).then_inc(s["x_dve"], 1)
            dve.wait_ge(s["x_proj"], 4)
            V.tensor_scalar(kT[:, 0, 512:1024], bank(3), vec[:, V_BK:V_BK + 1], None, ALU.add).then_inc(s["x_dve"], 1)
            dve.wait_ge(s["x_proj"], 6)
            V.tensor_copy(v_sb[:, 4:8, 0, :], bank(7).rearrange("p (t d) -> p t d", d=P)).then_inc(s["x_dve"], 1)
            softmax_in(2 * HP0, 4, P)
            for c in range(2):
                softmax_sum(2 * HP0, c, 4, P)
            attT_copy(HP0)

            pre = residual("a_out", 2 * HP0 + 1, 6, 1)
            for c in range(2):
                step(pre(c))
                h = slice(4 * c, 4 * c + 4)
                for t in range(4 * c, 4 * c + 4):
                    ins = V.bn_stats(bst[:, t, :], x_tok[:, t, :])
                step(ins)
                for t in range(4 * c, 4 * c + 4):
                    ins = V.bn_aggr(bmv[:, t, :], bst[:, t, :])
                step(ins)
                V.tensor_scalar(ve[:, h], bmv[:, h, 1], LN_EPS, None, ALU.add).then_inc(s["ve_ready"], 1)
            for c in range(2):
                h = slice(4 * c, 4 * c + 4)
                dve.wait_ge(s["rstd_ready"], 6 + c + 1)
                step(V.tensor_tensor(gm[:, h], rs[:, h], rs[:, h], ALU.mult))
                step(V.tensor_tensor(gm[:, h], gm[:, h], bmv[:, h, 1], ALU.mult))
                V.tensor_scalar(ve[:, h], gm[:, h], LN_EPS, None, ALU.add).then_inc(s["ve_ready"], 1)
                for t in range(4 * c, 4 * c + 4):
                    ins = V.tensor_scalar(hs[:, t, :], x_tok[:, t, :], bmv[:, t, 0:1], rs[:, t:t + 1],
                                          ALU.subtract, ALU.mult)
                ins.then_inc(s["nrm_ready"], 1)
            for c in range(2):
                dve.wait_ge(s["rstd_ready"], 8 + c + 1)
                dve.wait_ge(s["nrm_ready"], 6 + c + 1)
                for t in range(4 * c, 4 * c + 4):
                    ins = V.tensor_scalar(nrm[:, t, :], hs[:, t, :], rs2[:, t:t + 1], None, ALU.mult)
                ins.then_inc(s["nrm_ready"], 1)
            turn_lo(3, vec[:, V_G1:V_G1 + 1])
            def kv_range(k):
                t, what = k // 2, ("max", "min")[k % 2]
                dve.wait_ge(s["kv_ps"], t + 1)
                V.tensor_reduce(qs[what][:, 4 * t:4 * t + 4], bank(t).rearrange("p (g d) -> p g d", d=P), AX,
                                (ALU.max, ALU.min)[k % 2]).then_inc(s["q_red"], 1)

            for k in range(8):
                kv_range(k)
            quant_scales(qs, 0, 16, s["q_stats"], 8 + 8, beside=lambda k: kv_range(8 + k))
            quant_scales(qs, 16, 32, s["q_stats"], 8 + 16)
            for n in range(16):
                dve.wait_ge(s["q_round"], 20 + ROUND_ORDER.index(CLIP_ORDER[n]) + 1)
                clip(CLIP_ORDER[n], s["q_clip"])

            cosT = cst[:, C_COS:C_COS + S].unsqueeze(1).to_broadcast([P, 8, S])
            sinT = cst[:, C_SIN:C_SIN + S].unsqueeze(1).to_broadcast([P, 8, S])

            def rotate(hp, i):
                n = 4 * hp + i
                h = 2 * hp + i % 2
                b0 = rotation_bank(n)
                for k, (dst, scale, table, done) in enumerate(((q1s, wsc, cosT, "r_q1"),
                                                               (q2s, wscR, sinT, "r_q2"))):
                    dve.wait_ge(s["r_ps"], 2 * n + k + 1)
                    if n >= 2:
                        dve.wait_ge(s["r_q"], n - 1)
                    V.scalar_tensor_tensor(dst[:, n % 2, :].rearrange("p (b q) -> p b q", q=S),
                                           bank(b0 + k).rearrange("p (b q) -> p b q", q=S),
                                           scale[:, h:h + 1], table, ALU.mult, ALU.mult).then_inc(s[done], 1)

            for b in range(2):
                dve.wait_ge(s["q_deq"], 12 + 8 * b + 8)
                kk = st[:, 16 * b:16 * b + 16, :].rearrange("p (t g) d -> p t g d", g=4)[:, :, 0:2, :]
                kr = k_sin[:, :, 512 * b:512 * b + 512].rearrange("p a (t d) -> p t a d", d=D)
                for a in range(2):
                    sinK = cst[:, C_SINK + 64 * a:C_SINK + 64 * a + 64].unsqueeze(1).unsqueeze(1).to_broadcast(
                        [P, 4, 2, 64])
                    ins = V.tensor_tensor(kr[:, :, :, 64 * a:64 * a + 64], kk[:, :, :, 64 - 64 * a:128 - 64 * a],
                                          sinK, ALU.mult)
                ins.then_inc(s["k_sin"], 1)
            dve.wait_ge(s["scr_in"], 32)
            for i in range(4):
                rotate(0, i)

            def clip_v(i):
                for n in range(16 + 4 * i, 16 + 4 * i + 4):
                    dve.wait_ge(s["q_round"], 20 + ROUND_ORDER.index(CLIP_ORDER[n]) + 1)
                    clip(CLIP_ORDER[n], s["q_clip"])

            def keys_turned(h):
                dve.wait_ge(s["k_turn"], 2 * h + 2)
                V.tensor_copy(kT[:, h, 512:1024], bank(5 + 2 * h)).then_inc(s["k_dve"], 1)

            keys_turned(0)
            clip_v(0)

            for hp in range(HP1):
                n = 2 * HP0 + 2 + 2 * hp
                softmax_in(n, 8, S)
                if hp == 0:
                    for i in range(1, 4):
                        clip_v(i)
                    keys_turned(1)
                for i in range(4):
                    if hp + 1 < HP1:
                        rotate(hp + 1, i)
                    if i < 2:
                        softmax_sum(n, i, 8, S)
            attT_copy(HP0 + HP1)
            for q in range(2):
                dve.wait_ge(s["a_out"], O_L1 + 4 * (HP1 - 1) + 2 * q + 2)
                V.tensor_copy(of_batches(big[:, 2 * HP1 - 2:2 * HP1, 512 * q:512 * q + 512], 1).rearrange(
                    "p a t q -> p t a q"),
                              bank(output_bank(HP1 - 1, q) + 1).rearrange("p (t a q) -> p t a q", a=2, q=S)
                              ).then_inc(s["a_out_dve"], 1)

            def attended(c):
                dve.wait_ge(s["y_ready"], 2 + c + 1)
                hh = hs[:, 4 * c:4 * c + 4, :]
                return V.tensor_tensor(hh, bank(c).rearrange("p (t d) -> p t d", d=D), hh, ALU.add)

            norm(5, hs, nrm, True, attended)

            turn_lo(4, vec[:, V_G2:V_G2 + 1])

            def gated(p, e, c):
                n = 4 * p + 2 * e + c
                dve.wait_ge(s["m_down"], DOWN[(p, 3 if e == 0 else 6, e, c)] + 1)
                if n >= 2:
                    dve.wait_ge(s["m_acc"], n)
                V.tensor_tensor(hid1[:, c, :].rearrange("p (t d) -> p t d", d=D),
                                bank(6 + c).rearrange("p (t d) -> p t d", d=D),
                                per_group(lg[:, 4 * c:4 * c + 4, 2 * p + e], 4, D), ALU.mult).then_inc(s["m_gy"], 1)

            def up(p, m, c):
                n = 2 * (MT * p + m) + c
                dve.wait_ge(s["m_act"], n + 1)
                if n >= 2:
                    pp, mm = divmod(MT * p + m - 1, MT)
                    dve.wait_ge(s["m_down"], DOWN[(pp, mm, 1 if mm >= 3 else 0, c)] + 1)
                g = PG * p + MT + 2 * m + 1
                V.scalar_tensor_tensor(hid[:, c, :], bank(2 + c), msc[:, g:g + 1], act[:, c, :],
                                       ALU.mult, ALU.mult).then_inc(s["m_up"], 1)

            def beside_gating(i):
                if i % 3 == 1:
                    up(0, 1 + i // 6, i // 3 % 2)

            up(0, 0, 0)
            up(0, 0, 1)
            gating(1, beside_gating)
            dve.wait_ge(s["gates"], 2)
            for p in range(PAIRS):
                for m in range(MT):
                    for c in range(2):
                        if p > 0 or m > 3:
                            up(p, m, c)
                        if m == 0 and p > 0:
                            gated(p - 1, 1, c)
                    if m == 3:
                        gated(p, 0, 0)
                        gated(p, 0, 1)
            for c in range(2):
                gated(PAIRS - 1, 1, c)
            for c in range(2):
                dve.wait_ge(s["m_acc"], 4 * PAIRS + c)
                hh = hs[:, 4 * c:4 * c + 4, :]
                step(V.tensor_tensor(hh, macc[:, 4 * c:4 * c + 4, :], hh, ALU.add))
                xx = x_tok[:, 4 * c:4 * c + 4, :]
                ins = V.scalar_tensor_tensor(xx, hh, tg[:, 3:4], xx, ALU.mult, ALU.add)
            ins.then_inc(s["x_new"], 1)


O_L1 = 2 * HP0 + 2
LOGITS_BANK = (6, 4)

K_GROUPS = [4 * t + i for t in range(NT) for i in (0, 1)]
V_GROUPS = [g + 2 for g in K_GROUPS]
ROUND_ORDER = K_GROUPS[:8] + V_GROUPS[4:8] + K_GROUPS[8:] + V_GROUPS[:4] + V_GROUPS[8:]
CLIP_ORDER = K_GROUPS + V_GROUPS


def aux_plan():
    first = [("w13", 0, u) for u in range(4)] + [("w2", 0, 0), ("w2", 0, 1)]
    banks = [6, 7, 2, 3, 6, 7]
    order, after = list(first), {}
    for p in range(PAIRS):
        if p > 0:
            after[(p, 0)] = [("w13", p, 2)]
            after[(p, 1)] = [("w13", p, 3)]
            after[(p, 2)] = [("w2", p, 1)]
        if p + 1 < PAIRS:
            after[(p, 4)] = [("w13", p + 1, 0)]
            after[(p, 5)] = [("w2", p + 1, 0)]
            after[(p, 6)] = [("w13", p + 1, 1)]
        for m in range(MT):
            order += after.get((p, m), [])
    banks += [4 + n % 2 for n in range(len(order) - len(banks))]
    return first, after, {key: n for n, key in enumerate(order)}, banks


AUX_FIRST, AUX_AT, AUX, AUX_BANK = aux_plan()


def output_bank(hp, q):
    return 2 if hp >= HP1 - 2 and q == 1 else 6


def rotation_bank(n):
    return {1: 0, 3: 6}.get(n, 2)


DOWN = {key: n for n, key in enumerate(
    (p, m, e, c) for p in range(PAIRS) for m in range(MT)
    for e in ((0,) if m < 3 else (0, 1) if m == 3 else (1,)) for c in range(2))}


def constants():
    c = np.zeros((P, C_END), np.float32)
    i = np.arange(P)
    c[:, C_ID:C_ID + P] = np.eye(P)
    c[:, C_CAU:C_CAU + S] = np.where(np.arange(S)[None] <= (i % S)[:, None], 0.0, -1e30)
    c[:, C_BLK:C_BLK + P] = np.where((i // S)[None] == (i // S)[:, None], 0.0, -1e30)
    inv = (np.float32(1.0) / np.float32(1e6) ** (np.arange(0, D, 2, dtype=np.float32) / np.float32(D))).astype(np.float32)
    freqs = np.arange(S, dtype=np.float32)[:, None] * inv[None]
    emb = np.concatenate([freqs, freqs], -1)
    cos, sin = np.cos(emb), np.sin(emb)
    sin = sin * np.where(i < 64, -1.0, 1.0)[None]
    c[:, C_COS:C_COS + S], c[:, C_SIN:C_SIN + S] = cos.T, sin.T
    c[:, C_COSK:C_COSK + D], c[:, C_SINK:C_SINK + D] = np.tile(cos, (2, 1)), np.tile(sin, (2, 1))
    c[:, C_REV:C_REV + E] = np.arange(E, 0, -1)
    return c


def kernel(**inputs):
    import concourse.bacc as _bacc
    from concourse.bass_utils import run_bass_kernel_spmd as _run

    a = {k: np.asarray(v) for k, v in inputs.items()}
    cst = constants()
    col = lambda v: v.reshape(-1, P).T
    row = lambda v: np.tile(v[None], (P, 1))
    vec = np.concatenate([col(a["L1_xattn_bq"]), col(a["L1_xattn_bk"]),
                          col(a["L1_ffn_g1"]), col(a["L1_ffn_g2"]), col(a["L0_xattn_bv"]), a["L0_ffn_w_gate"],
                          a["L1_ffn_w_gate"].T, row(a["g_xattn"]), row(a["g_ffn"])], 1)
    tiles = lambda w: w.reshape(-1, P, D)
    w0 = np.zeros((HP0, P, WST), np.float32)
    w0[:, :, 0:P] = tiles(a["L0_xattn_Wq"]).transpose(0, 2, 1)
    w0[:, :, P:2 * P] = tiles(a["L0_xattn_Wk"]).transpose(0, 2, 1)
    wv = tiles(a["L0_xattn_Wv"]).transpose(0, 2, 1)
    w0[1::2, :, 2 * P:3 * P] = wv[0::2]
    w0[1::2, :, 3 * P:4 * P] = wv[1::2]
    w0[:, :, 4 * P] = a["L0_xattn_bq"].reshape(HP0, P)
    w0[:, :, 4 * P + 1] = a["L0_xattn_bk"].reshape(HP0, P)
    hidden = np.array([M_HID * e + r for e in range(E) for r in range(P)] + [
        M_HID * e + P + r for e in range(E) for r in range(32)] + [M_HID * e + 160 + r for e in range(E) for r in range(16)])
    up_cols = lambda w: w.transpose(1, 0, 2).reshape(D, M0 * P)[:, hidden].reshape(D, M0, P)
    gu0 = np.concatenate([up_cols(a["L0_ffn_w_g"]), up_cols(a["L0_ffn_w_u"])], 2)
    wx = np.concatenate([a["L1_xattn_Wq"].T, a["L1_xattn_Wk"].T, a["L1_xattn_Wv"].T], 1)
    wl = np.concatenate([tiles(a["L1_ffn_w_q"]).transpose(1, 0, 2), tiles(a["L1_ffn_w_k"]).transpose(1, 0, 2),
                         tiles(a["L1_ffn_w_v"]).transpose(1, 0, 2), a["L1_ffn_w_o"].reshape(D, 8, P)], 1)
    pair = lambda w: w.reshape(PAIRS, MT, P, D).transpose(0, 2, 1, 3)
    w13 = np.stack([pair(a["L1_ffn_w1"]), pair(a["L1_ffn_w3"])], 3).reshape(PAIRS, P, 2 * MT, D)
    wm = np.concatenate([a["L1_ffn_w2"].reshape(PAIRS, P, MT, P), w13], 2)
    wm = wm.reshape(PAIRS, P, 3, MT, P).transpose(0, 2, 1, 3, 4).reshape(3 * PAIRS, P, MT, P)
    tok = lambda v: v.reshape(NT, P, D).transpose(1, 0, 2)
    arrays = {
        "cst": cst, "vec": vec, "x": tok(a["x"]), "ctx": a["ctx_1024"].reshape(TOK, D).T, "w0": w0,
        "wo0": a["L0_xattn_Wo"].T.reshape(HP0, P, D).transpose(1, 0, 2),
        "biases": np.stack([row(a["L0_xattn_bo"]), row(a["L1_xattn_bv"])], 1), "gu0": gu0,
        "d0": a["L0_ffn_w_d"].reshape(M0 * P, D)[hidden].reshape(M0, P, D).transpose(1, 0, 2), "wx": wx, "wl": wl, "wm": wm,
    }
    nc = _bacc.Bacc("TRN2", target_bir_lowering=False, num_devices=1)
    args = []
    for k in arrays:
        arrays[k] = np.ascontiguousarray(arrays[k])
        args.append(nc.dram_tensor(k + "_dram", arrays[k].shape, F32, kind="ExternalInput").ap())
    args.append(nc.dram_tensor("out_dram", (P, NT, D), F32, kind="ExternalOutput").ap())
    build(nc, *args)
    r = _run(nc, [{k + "_dram": v for k, v in arrays.items()}], core_ids=[0])
    got = r.results[0]["out_dram"]
    return got.transpose(1, 0, 2).reshape(B, S, D)
```
